# Optimizing a Trainium2 kernel written in Bass

```python
import numpy as np
import jax
import jax.numpy as jnp

def _softmax(x, axis=-1):
    return jax.nn.softmax(x, axis=axis)

def _gelu(x):
    return jax.nn.gelu(x, approximate=True)

def _silu(x):
    return jax.nn.silu(x)

def _sigmoid(x):
    return jax.nn.sigmoid(x)

def _layernorm(x, axis=-1, eps=1e-05):
    m = jnp.mean(x, axis=axis, keepdims=True)
    v = jnp.var(x, axis=axis, keepdims=True)
    return (x - m) / jnp.sqrt(v + eps)

def _scatter_add(tgt, idx, src, axis=0):
    return tgt.at[idx].add(src)

def _segment_sum(src, seg, n):
    return jax.ops.segment_sum(src, seg, n)
kernel_name = 'mk_adaln_attn_ffn_d2_seqx_r4_1048fc'

def setup_inputs(seed: int=0):
    np.random.seed(seed)
    _w = jnp.asarray

    def _rec_inputs():
        import jax
        import jax.numpy as jnp
        _rk = jax.random.key(seed)
        x = 7.22e-05 + 1 * jax.random.normal(jax.random.fold_in(_rk, 1), (8, 256, 256), jnp.float32)
        _lenS = 256 - jax.random.randint(jax.random.fold_in(_rk, 7), (8,), 0, max(1, 256 // 4) + 1, jnp.int32)
        _lenS2 = 256 - jax.random.randint(jax.random.fold_in(_rk, 8), (8,), 0, max(1, 256 // 4) + 1, jnp.int32)
        condB_tauraws = -5.74692 + 0.777674 * jax.random.normal(jax.random.fold_in(_rk, 11), (8,), jnp.float32)
        cond_256 = -0.000235209 + 0.019331 * jax.random.normal(jax.random.fold_in(_rk, 12), (8, 64), jnp.float32)
        condB_bn2 = jnp.zeros((8,), jnp.float32)
        cond_1024 = -4.10585e-05 + 0.0199478 * jax.random.normal(jax.random.fold_in(_rk, 14), (8, 256), jnp.float32)
        itok_B_0_2 = jax.random.randint(jax.random.fold_in(_rk, 15), (8,), 0, 3, jnp.int32)
        itok_B_0_6 = jax.random.randint(jax.random.fold_in(_rk, 16), (8,), 0, 7, jnp.int32)
        itok_B_0_63 = jax.random.randint(jax.random.fold_in(_rk, 17), (8,), 0, 64, jnp.int32)
        return (x, condB_tauraws, cond_256, condB_bn2, cond_1024, itok_B_0_2, itok_B_0_6, itok_B_0_63)
    x, condB_tauraws, cond_256, condB_bn2, cond_1024, itok_B_0_2, itok_B_0_6, itok_B_0_63 = _rec_inputs()

    def _L0_cond_setup():
        import jax, jax.numpy as jnp
        import numpy as np
        import math
        B, T, E, D = (4, 512, 256, 4)

        def _tau_init(t):
            a = 0.1 ** (1.0 / max(t - 1, 1))
            tt = -math.log(max(a, 1e-10))
            return math.log(math.exp(tt) - 1 + 1e-10)

        def causal_ema(b, tau_raw):
            alpha = jnp.exp(-jax.nn.softplus(tau_raw)).astype(b.dtype)

            def step(h, bt):
                h = alpha * h + bt
                return (h, h)
            h0 = jnp.zeros((b.shape[0], b.shape[2]), b.dtype)
            _, hs = jax.lax.scan(step, h0, jnp.swapaxes(b, 0, 1))
            return jnp.swapaxes(hs, 0, 1)
        key = jax.random.key(seed)
        ks = jax.random.split(key, 10)
        s = 0.02
        return {'x': jax.random.normal(ks[0], (B, T, E), jnp.float32), 'tau_ctx': jnp.float32(_tau_init(max(T // 2, 4))), 'tau_raws': jnp.array([_tau_init(max(T // 2 ** i, 2)) for i in range(D)], jnp.float32), 'Wg': jax.random.normal(ks[1], (E, 2 * E), jnp.float32) * s, 'bg': jnp.full((E,), -0.5, jnp.float32), 'Wn1': jax.random.normal(ks[2], (E // 4, E), jnp.float32) * s, 'bn1': jnp.zeros((E // 4,), jnp.float32), 'Wn2': jax.random.normal(ks[3], (D, E // 4), jnp.float32) * s, 'bn2': jnp.zeros((D,), jnp.float32), 'blend': jax.random.normal(ks[4], (D, E), jnp.float32) * s, 'Wsoma': jax.random.normal(ks[5], (E, E), jnp.float32) * s, 'bsoma': jnp.zeros((E,), jnp.float32), 'Wtemp': jax.random.normal(ks[6], (E, E), jnp.float32) * s, 'btemp': jnp.zeros((E,), jnp.float32), 'Wout': jax.random.normal(ks[7], (E, E), jnp.float32) * s, 'gamma': jnp.ones((E,), jnp.float32), 'beta': jnp.zeros((E,), jnp.float32)}
    _L0_cond_all = _L0_cond_setup()
    _L0_cond_in = {k: v for k, v in _L0_cond_all.items() if k in ('tau_ctx', 'Wg', 'bg', 'Wn1', 'bn1', 'Wsoma', 'bsoma', 'Wtemp', 'btemp', 'Wout', 'gamma', 'beta')}
    del _L0_cond_all

    def _L0_attn_setup():
        import jax, jax.numpy as jnp
        import numpy as np
        B, L, D = (2, 1024, 256)
        EXPAND = 2
        D_INNER = D * EXPAND
        K, M = (32, 1)
        H = D_INNER // K
        KS = 4
        NA = 4
        ND = K - NA
        C = 2 * D_INNER + K
        SD = H * M
        key = jax.random.key(seed)
        ks = jax.random.split(key, 8)
        x = jax.random.normal(ks[0], (B, L, D), jnp.float32)
        in_proj_w = jax.random.normal(ks[1], (D, C), jnp.float32) * (1.0 / np.sqrt(D))
        conv_k = jax.random.normal(ks[2], (KS, 1, C), jnp.float32) * 0.3
        conv_b = jnp.zeros((C,), jnp.float32)
        grid = np.linspace(0.1, 1.5, K * H).reshape(1, 1, K, H, 1)
        signs = np.resize([1.0, -1.0], grid.shape)
        theta = jnp.asarray(grid * signs, jnp.float32)
        decay_slopes = jnp.asarray(np.log(np.exp(np.geomspace(0.001, 0.1, ND)) - 1.0), jnp.float32)
        anchor_slopes = jnp.asarray(np.log(np.exp(np.geomspace(0.01, 0.1, NA)) - 1.0), jnp.float32)
        score_scale = jnp.ones((K,), jnp.float32)
        deriv_logits = jnp.asarray([5.0, 0.0, 0.0], jnp.float32)
        glorot = np.sqrt(2.0 / (SD + H))
        W_re = jax.random.normal(ks[3], (SD, H), jnp.float32) * glorot
        W_im = jax.random.normal(ks[4], (SD, H), jnp.float32) * glorot
        norm_scale = jnp.ones((2 * SD,), jnp.float32)
        out_proj_w = jax.random.normal(ks[5], (D_INNER, D), jnp.float32) * (1.0 / np.sqrt(D_INNER))
        return dict(x=x, in_proj_w=in_proj_w, conv_k=conv_k, conv_b=conv_b, theta=theta, decay_slopes=decay_slopes, anchor_slopes=anchor_slopes, score_scale=score_scale, deriv_logits=deriv_logits, W_re=W_re, W_im=W_im, norm_scale=norm_scale, out_proj_w=out_proj_w)
    _L0_attn_all = _L0_attn_setup()
    _L0_attn_in = {k: v for k, v in _L0_attn_all.items() if k in ('in_proj_w', 'conv_k', 'conv_b', 'theta', 'decay_slopes', 'anchor_slopes', 'score_scale', 'deriv_logits', 'W_re', 'W_im', 'norm_scale', 'out_proj_w')}
    del _L0_attn_all

    def _L0_cond2_setup():
        import jax, jax.numpy as jnp
        import numpy as np
        NEG_INF = -1e+30
        key = jax.random.key(seed)
        k1, k2, k3, k4, k5 = jax.random.split(key, 5)
        B, S, D, A = (16, 256, 256, 64)
        hidden = jax.random.normal(k1, (B, S, D), dtype=jnp.float32)
        W1 = jax.random.normal(k2, (D, A), dtype=jnp.float32) / np.sqrt(D)
        b1 = jax.random.normal(k3, (A,), dtype=jnp.float32) * 0.01
        v = jax.random.normal(k4, (A,), dtype=jnp.float32) / np.sqrt(A)
        prompt_type_ids = jax.random.randint(k5, (B,), 0, 3, dtype=jnp.int32)
        return {'hidden': hidden, 'W1': W1, 'b1': b1, 'v': v, 'prompt_type_ids': prompt_type_ids}
    _L0_cond2_all = _L0_cond2_setup()
    _L0_cond2_in = {k: v for k, v in _L0_cond2_all.items() if k in ('W1', 'b1', 'v')}
    del _L0_cond2_all

    def _L0_ffn_setup():
        import jax, jax.numpy as jnp
        import numpy as np
        EXPERTS = 8
        TOP_K = 2

        def swiglu(x, w1, w2, w3):
            h = x @ w1
            return h * jax.nn.sigmoid(h) * (x @ w2) @ w3
        key = jax.random.key(seed)
        ks = jax.random.split(key, 9)
        B, S, D = (4, 512, 256)
        H = 2 * D
        s = 0.02
        x = jax.random.normal(ks[0], (B, S, D), dtype=jnp.float32)
        gate_w = jax.random.normal(ks[1], (D, EXPERTS), dtype=jnp.float32) * s
        ew1 = jax.random.normal(ks[2], (EXPERTS, D, H), dtype=jnp.float32) * s
        ew2 = jax.random.normal(ks[3], (EXPERTS, D, H), dtype=jnp.float32) * s
        ew3 = jax.random.normal(ks[4], (EXPERTS, H, D), dtype=jnp.float32) * s
        sw1 = jax.random.normal(ks[5], (D, H), dtype=jnp.float32) * s
        sw2 = jax.random.normal(ks[6], (D, H), dtype=jnp.float32) * s
        sw3 = jax.random.normal(ks[7], (H, D), dtype=jnp.float32) * s
        return {'x': x, 'gate_w': gate_w, 'ew1': ew1, 'ew2': ew2, 'ew3': ew3, 'sw1': sw1, 'sw2': sw2, 'sw3': sw3}
    _L0_ffn_all = _L0_ffn_setup()
    _L0_ffn_in = {k: v for k, v in _L0_ffn_all.items() if k in ('gate_w', 'ew1', 'ew2', 'ew3', 'sw1', 'sw2', 'sw3')}
    del _L0_ffn_all

    def _L1_cond_setup():
        import jax, jax.numpy as jnp
        import numpy as np
        N_PROFILES = 8
        HIDDEN = 256
        BOTTLENECK = 128
        EPS = 1e-05
        key = jax.random.key(seed)
        ks = jax.random.split(key, 8)
        B, S, H, K, P = (16, 512, HIDDEN, BOTTLENECK, N_PROFILES)
        down_w = jax.random.normal(ks[0], (P, H, K), dtype=jnp.float32) * (1.0 / np.sqrt(H))
        down_b = jax.random.normal(ks[1], (P, K), dtype=jnp.float32) * 0.01
        up_w = jax.random.normal(ks[2], (P, K, H), dtype=jnp.float32) * (1.0 / np.sqrt(K))
        up_b = jax.random.normal(ks[3], (P, H), dtype=jnp.float32) * 0.01
        ln_g = jnp.ones((P, H), dtype=jnp.float32)
        ln_b = jnp.zeros((P, H), dtype=jnp.float32)
        hidden = jax.random.normal(ks[4], (B, S, H), dtype=jnp.float32)
        profile_ids = jax.random.randint(ks[5], (B,), 0, P)
        return {'hidden': hidden, 'profile_ids': profile_ids, 'down_w': down_w, 'down_b': down_b, 'up_w': up_w, 'up_b': up_b, 'ln_g': ln_g, 'ln_b': ln_b}
    _L1_cond_all = _L1_cond_setup()
    _L1_cond_in = {k: v for k, v in _L1_cond_all.items() if k in ('down_w', 'down_b', 'up_w', 'up_b', 'ln_g', 'ln_b')}
    del _L1_cond_all

    def _L1_attn_setup():
        import jax, jax.numpy as jnp
        import numpy as np
        EPS_RMS = 1e-06
        EPS_Q = 1e-05

        def rmsnorm(x, g):
            var = jnp.mean(x * x, axis=-1, keepdims=True)
            return g * (x * jax.lax.rsqrt(var + EPS_RMS))

        def activation_quant(x):
            scale = 127.0 / jnp.clip(jnp.max(jnp.abs(x), axis=-1, keepdims=True), EPS_Q)
            y = jnp.clip(jnp.round(x * scale), -128, 127) / scale
            return x + jax.lax.stop_gradient(y - x)

        def weight_quant(w):
            s = jnp.clip(jnp.mean(jnp.abs(w)), EPS_Q)
            y = jnp.clip(jnp.round(w / s), -1, 1) * s
            return w + jax.lax.stop_gradient(y - w)

        def bitlinear(x, w, g):
            xq = activation_quant(rmsnorm(x, g))
            wq = weight_quant(w)
            return jnp.einsum('btc,oc->bto', xq, wq)
        key = jax.random.key(seed)
        ks = jax.random.split(key, 5)
        B, T, C = (2, 512, 256)
        std = 1.0 / np.sqrt(C)
        inp = {'x': jax.random.normal(ks[0], (B, T, C), jnp.float32), 'wq': jax.random.normal(ks[1], (C, C), jnp.float32) * std, 'wk': jax.random.normal(ks[2], (C, C), jnp.float32) * std, 'wv': jax.random.normal(ks[3], (C, C), jnp.float32) * std, 'wo': jax.random.normal(ks[4], (C, C), jnp.float32) * std, 'gq': jnp.ones((C,), jnp.float32), 'gk': jnp.ones((C,), jnp.float32), 'gv': jnp.ones((C,), jnp.float32), 'go': jnp.ones((C,), jnp.float32)}
        return inp
    _L1_attn_all = _L1_attn_setup()
    _L1_attn_in = {k: v for k, v in _L1_attn_all.items() if k in ('wq', 'wk', 'wv', 'wo', 'gq', 'gk', 'gv', 'go')}
    del _L1_attn_all

    def _L1_cond2_setup():
        import jax, jax.numpy as jnp
        import numpy as np
        NUM_CATEGORIES = 64
        INPUT_DIM = 256
        HIDDEN_DIM = 256
        B = 64
        S = 64
        key = jax.random.key(seed)
        kx, kc, kw = jax.random.split(key, 3)
        x = jax.random.normal(kx, (B, S, INPUT_DIM), dtype=jnp.float32)
        cat_ids = jax.random.randint(kc, (B,), 0, NUM_CATEGORIES, dtype=jnp.int32)
        W = 0.02 * jax.random.normal(kw, (NUM_CATEGORIES, INPUT_DIM, HIDDEN_DIM), dtype=jnp.float32)
        b = jnp.zeros((NUM_CATEGORIES, HIDDEN_DIM), dtype=jnp.float32)
        return {'x': x, 'cat_ids': cat_ids, 'W': W, 'b': b}
    _L1_cond2_all = _L1_cond2_setup()
    _L1_cond2_in = {k: v for k, v in _L1_cond2_all.items() if k in ('W', 'b')}
    del _L1_cond2_all

    def _L1_ffn_setup():
        import jax, jax.numpy as jnp
        import numpy as np
        FP8_MAX = 448.0
        SCALE = 1.0
        _FP8_DTYPE = getattr(jnp, 'float8_e4m3fn', jnp.float16)

        def quantize_e4m3(t, scale):
            return jnp.clip(t / scale, -FP8_MAX, FP8_MAX).astype(_FP8_DTYPE)
        key = jax.random.key(seed)
        kx, kw = jax.random.split(key)
        B, N, C, F = (8, 1024, 256, 256)
        x = jax.random.normal(kx, (B, N, C), dtype=jnp.float32)
        weight = jax.random.normal(kw, (F, C), dtype=jnp.float32) * 0.02
        bias = jnp.zeros((F,), dtype=jnp.float32)
        return {'x': x, 'weight': weight, 'bias': bias}
    _L1_ffn_all = _L1_ffn_setup()
    _L1_ffn_in = {k: v for k, v in _L1_ffn_all.items() if k in ('weight', 'bias')}
    del _L1_ffn_all
    return {'x': x, 'condB_tauraws': condB_tauraws, 'cond_256': cond_256, 'condB_bn2': condB_bn2, 'cond_1024': cond_1024, 'itok_B_0_2': itok_B_0_2, 'itok_B_0_6': itok_B_0_6, 'itok_B_0_63': itok_B_0_63, 'L0_cond_tau_ctx': _L0_cond_in['tau_ctx'], 'L0_cond_Wg': _L0_cond_in['Wg'], 'L0_cond_bg': _L0_cond_in['bg'], 'L0_cond_Wn1': _L0_cond_in['Wn1'], 'L0_cond_bn1': _L0_cond_in['bn1'], 'L0_cond_Wsoma': _L0_cond_in['Wsoma'], 'L0_cond_bsoma': _L0_cond_in['bsoma'], 'L0_cond_Wtemp': _L0_cond_in['Wtemp'], 'L0_cond_btemp': _L0_cond_in['btemp'], 'L0_cond_Wout': _L0_cond_in['Wout'], 'L0_cond_gamma': _L0_cond_in['gamma'], 'L0_cond_beta': _L0_cond_in['beta'], 'L0_attn_in_proj_w': _L0_attn_in['in_proj_w'], 'L0_attn_conv_k': _L0_attn_in['conv_k'], 'L0_attn_conv_b': _L0_attn_in['conv_b'], 'L0_attn_theta': _L0_attn_in['theta'], 'L0_attn_decay_slopes': _L0_attn_in['decay_slopes'], 'L0_attn_anchor_slopes': _L0_attn_in['anchor_slopes'], 'L0_attn_score_scale': _L0_attn_in['score_scale'], 'L0_attn_deriv_logits': _L0_attn_in['deriv_logits'], 'L0_attn_W_re': _L0_attn_in['W_re'], 'L0_attn_W_im': _L0_attn_in['W_im'], 'L0_attn_norm_scale': _L0_attn_in['norm_scale'], 'L0_attn_out_proj_w': _L0_attn_in['out_proj_w'], 'L0_cond2_W1': _L0_cond2_in['W1'], 'L0_cond2_b1': _L0_cond2_in['b1'], 'L0_cond2_v': _L0_cond2_in['v'], 'L0_ffn_gate_w': _L0_ffn_in['gate_w'], 'L0_ffn_ew1': _L0_ffn_in['ew1'], 'L0_ffn_ew2': _L0_ffn_in['ew2'], 'L0_ffn_ew3': _L0_ffn_in['ew3'], 'L0_ffn_sw1': _L0_ffn_in['sw1'], 'L0_ffn_sw2': _L0_ffn_in['sw2'], 'L0_ffn_sw3': _L0_ffn_in['sw3'], 'L1_cond_down_w': _L1_cond_in['down_w'], 'L1_cond_down_b': _L1_cond_in['down_b'], 'L1_cond_up_w': _L1_cond_in['up_w'], 'L1_cond_up_b': _L1_cond_in['up_b'], 'L1_cond_ln_g': _L1_cond_in['ln_g'], 'L1_cond_ln_b': _L1_cond_in['ln_b'], 'L1_attn_wq': _L1_attn_in['wq'], 'L1_attn_wk': _L1_attn_in['wk'], 'L1_attn_wv': _L1_attn_in['wv'], 'L1_attn_wo': _L1_attn_in['wo'], 'L1_attn_gq': _L1_attn_in['gq'], 'L1_attn_gk': _L1_attn_in['gk'], 'L1_attn_gv': _L1_attn_in['gv'], 'L1_attn_go': _L1_attn_in['go'], 'L1_cond2_W': _L1_cond2_in['W'], 'L1_cond2_b': _L1_cond2_in['b'], 'L1_ffn_weight': _L1_ffn_in['weight'], 'L1_ffn_bias': _L1_ffn_in['bias']}

def reference(x, condB_tauraws, cond_256, condB_bn2, cond_1024, itok_B_0_2, itok_B_0_6, itok_B_0_63, L0_cond_tau_ctx, L0_cond_Wg, L0_cond_bg, L0_cond_Wn1, L0_cond_bn1, L0_cond_Wsoma, L0_cond_bsoma, L0_cond_Wtemp, L0_cond_btemp, L0_cond_Wout, L0_cond_gamma, L0_cond_beta, L0_attn_in_proj_w, L0_attn_conv_k, L0_attn_conv_b, L0_attn_theta, L0_attn_decay_slopes, L0_attn_anchor_slopes, L0_attn_score_scale, L0_attn_deriv_logits, L0_attn_W_re, L0_attn_W_im, L0_attn_norm_scale, L0_attn_out_proj_w, L0_cond2_W1, L0_cond2_b1, L0_cond2_v, L0_ffn_gate_w, L0_ffn_ew1, L0_ffn_ew2, L0_ffn_ew3, L0_ffn_sw1, L0_ffn_sw2, L0_ffn_sw3, L1_cond_down_w, L1_cond_down_b, L1_cond_up_w, L1_cond_up_b, L1_cond_ln_g, L1_cond_ln_b, L1_attn_wq, L1_attn_wk, L1_attn_wv, L1_attn_wo, L1_attn_gq, L1_attn_gk, L1_attn_gv, L1_attn_go, L1_cond2_W, L1_cond2_b, L1_ffn_weight, L1_ffn_bias):
    import jax
    import jax.numpy as jnp

    def _L0_cond_ref(x, tau_ctx, tau_raws, Wg, bg, Wn1, bn1, Wn2, bn2, blend, Wsoma, bsoma, Wtemp, btemp, Wout, gamma, beta):
        import jax, jax.numpy as jnp
        import numpy as np
        import math
        B, T, E, D = (4, 512, 256, 4)

        def _tau_init(t):
            a = 0.1 ** (1.0 / max(t - 1, 1))
            tt = -math.log(max(a, 1e-10))
            return math.log(math.exp(tt) - 1 + 1e-10)

        def causal_ema(b, tau_raw):
            alpha = jnp.exp(-jax.nn.softplus(tau_raw)).astype(b.dtype)

            def step(h, bt):
                h = alpha * h + bt
                return (h, h)
            h0 = jnp.zeros((b.shape[0], b.shape[2]), b.dtype)
            _, hs = jax.lax.scan(step, h0, jnp.swapaxes(b, 0, 1))
            return jnp.swapaxes(hs, 0, 1)
        ctx = causal_ema(x, tau_ctx)
        gate_in = jnp.concatenate([x, ctx], axis=-1)
        wg = jax.nn.sigmoid(jnp.einsum('btc,ec->bte', gate_in, Wg) + bg)
        gated = x * wg
        h1 = jax.nn.gelu(jnp.einsum('btc,hc->bth', x, Wn1) + bn1, approximate=False)
        mod = 0.5 + jax.nn.sigmoid(jnp.einsum('bth,dh->btd', h1, Wn2) + bn2)
        traces = jax.vmap(lambda tau, m: causal_ema(gated * m[..., None], tau))(tau_raws, jnp.moveaxis(mod, -1, 0))
        blend_w = jax.nn.softmax(blend, axis=0)
        temporal = jnp.einsum('dbtc,dc->btc', traces, blend_w)
        gate = jax.nn.sigmoid(jnp.einsum('btc,ec->bte', temporal, Wtemp) + btemp)
        soma = jax.nn.gelu(jnp.einsum('btc,ec->bte', x, Wsoma) + bsoma, approximate=False)
        out = jnp.einsum('btc,ec->bte', soma * gate, Wout)
        mu = out.mean(-1, keepdims=True)
        var = out.var(-1, keepdims=True)
        return (out - mu) / jnp.sqrt(var + 1e-05) * gamma + beta

    def _L0_attn_ref(x, in_proj_w, conv_k, conv_b, theta, decay_slopes, anchor_slopes, score_scale, deriv_logits, W_re, W_im, norm_scale, out_proj_w):
        import jax, jax.numpy as jnp
        import numpy as np
        B, L, D = (2, 1024, 256)
        EXPAND = 2
        D_INNER = D * EXPAND
        K, M = (32, 1)
        H = D_INNER // K
        KS = 4
        NA = 4
        ND = K - NA
        C = 2 * D_INNER + K
        SD = H * M
        b, l, _ = x.shape
        z = x @ in_proj_w
        zp = jnp.pad(z, ((0, 0), (KS - 1, 0), (0, 0)))
        z = jax.lax.conv_general_dilated(zp, conv_k, (1,), 'VALID', dimension_numbers=('NWC', 'WIO', 'NWC'), feature_group_count=C) + conv_b
        x_val = z[..., :D_INNER].reshape(b, l, K, H)
        x_gate = jax.nn.silu(z[..., D_INNER:2 * D_INNER])
        s_raw = z[..., -K:].reshape(b, l, K, 1)
        pos = jnp.arange(l, dtype=jnp.float32)
        slopes_d = jax.nn.softplus(decay_slopes).reshape(1, 1, -1, 1)
        dist = jnp.maximum(jnp.float32(l - 1) - pos, 0.0)
        w_d = jnp.exp(-slopes_d * dist[None, :, None, None])
        slopes_a = jax.nn.softplus(anchor_slopes).reshape(1, 1, -1, 1)
        w_a = jnp.exp(-slopes_a * pos[None, :, None, None])
        time_weight = jnp.concatenate([w_d, w_a], axis=2)
        p = jnp.exp(jnp.clip(score_scale[None, None, :, None] * s_raw, -20.0, 20.0))
        p_w = (p * time_weight).reshape(b, l, K, 1, 1)
        xv = x_val[..., None]
        phi = xv * theta
        cos_b, sin_b = (jnp.cos(phi), jnp.sin(phi))
        w = jax.nn.softmax(deriv_logits)
        poly = w[0] + w[1] * xv - w[2] * jnp.square(xv)
        re_m, im_m = (poly * cos_b, poly * sin_b)
        den = jnp.cumsum(p_w, axis=1)
        num_re = jnp.cumsum(p_w * re_m, axis=1)
        num_im = jnp.cumsum(p_w * im_m, axis=1)
        inv_den = 1.0 / jnp.maximum(den, 0.0001)
        re_flat = (num_re * inv_den).reshape(b, l, K, SD)
        im_flat = (num_im * inv_den).reshape(b, l, K, SD)
        mean_sq = (jnp.sum(jnp.square(re_flat), -1) + jnp.sum(jnp.square(im_flat), -1)) / (2 * SD)
        rs = jax.lax.rsqrt(mean_sq[..., None] + 1e-05)
        y = (jnp.dot(re_flat * rs * norm_scale[:SD], W_re) + jnp.dot(im_flat * rs * norm_scale[SD:], W_im)).reshape(b, l, D_INNER)
        return y * x_gate @ out_proj_w

    def _L0_cond2_ref(hidden, W1, b1, v, prompt_type_ids):
        import jax, jax.numpy as jnp
        import numpy as np
        NEG_INF = -1e+30
        B, S, D = hidden.shape
        attn_in = jnp.tanh(jnp.einsum('bsd,da->bsa', hidden, W1) + b1)
        scores = jnp.einsum('bsa,a->bs', attn_in, v)
        idx = jnp.arange(S)
        j = idx[:, None]
        l = idx[None, :]
        prefix_m = l <= j
        postfix_m = l >= j
        cloze_m = l != j
        pt = prompt_type_ids[:, None, None]
        mask = jnp.where(pt == 0, prefix_m[None], jnp.where(pt == 1, postfix_m[None], cloze_m[None]))
        masked_scores = jnp.where(mask, scores[:, None, :], NEG_INF)
        p = jax.nn.softmax(masked_scores, axis=-1)
        cnt = jnp.sum(mask, axis=-1).astype(hidden.dtype)
        pooled = jnp.einsum('bjl,bld->bjd', p, hidden) / cnt[..., None]
        return pooled

    def _L0_ffn_ref(x, gate_w, ew1, ew2, ew3, sw1, sw2, sw3):
        import jax, jax.numpy as jnp
        import numpy as np
        EXPERTS = 8
        TOP_K = 2

        def swiglu(x, w1, w2, w3):
            h = x @ w1
            return h * jax.nn.sigmoid(h) * (x @ w2) @ w3
        B, S, D = x.shape
        gate_out = x @ gate_w
        top_v, top_i = jax.lax.top_k(gate_out, TOP_K)
        masked = jnp.full_like(gate_out, -1e+20)
        bi = jnp.arange(B)[:, None, None]
        si = jnp.arange(S)[None, :, None]
        masked = masked.at[bi, si, top_i].set(top_v)
        probs = jax.nn.softmax(masked, axis=-1)
        chosen = jnp.zeros_like(gate_out, dtype=bool).at[bi, si, top_i].set(True)
        w = jnp.where(chosen, probs, 0.0)

        def one_expert(w1, w2, w3, we):
            return swiglu(x, w1, w2, w3) * we[..., None]
        out = jax.vmap(one_expert, in_axes=(0, 0, 0, 2))(ew1, ew2, ew3, w).sum(0)
        out = out + swiglu(x, sw1, sw2, sw3)
        return out

    def _L1_cond_ref(hidden, profile_ids, down_w, down_b, up_w, up_b, ln_g, ln_b):
        import jax, jax.numpy as jnp
        import numpy as np
        N_PROFILES = 8
        HIDDEN = 256
        BOTTLENECK = 128
        EPS = 1e-05
        Wd = down_w[profile_ids]
        bd = down_b[profile_ids][:, None]
        Wu = up_w[profile_ids]
        bu = up_b[profile_ids][:, None]
        g = ln_g[profile_ids][:, None]
        b = ln_b[profile_ids][:, None]
        z = jax.nn.relu(jnp.einsum('bsh,bhk->bsk', hidden, Wd) + bd)
        y = hidden + jnp.einsum('bsk,bkh->bsh', z, Wu) + bu
        mu = jnp.mean(y, axis=-1, keepdims=True)
        var = jnp.mean(jnp.square(y - mu), axis=-1, keepdims=True)
        return (y - mu) * jax.lax.rsqrt(var + EPS) * g + b

    def _L1_attn_ref(x, wq, wk, wv, wo, gq, gk, gv, go):
        import jax, jax.numpy as jnp
        import numpy as np
        EPS_RMS = 1e-06
        EPS_Q = 1e-05

        def rmsnorm(x, g):
            var = jnp.mean(x * x, axis=-1, keepdims=True)
            return g * (x * jax.lax.rsqrt(var + EPS_RMS))

        def activation_quant(x):
            scale = 127.0 / jnp.clip(jnp.max(jnp.abs(x), axis=-1, keepdims=True), EPS_Q)
            y = jnp.clip(jnp.round(x * scale), -128, 127) / scale
            return x + jax.lax.stop_gradient(y - x)

        def weight_quant(w):
            s = jnp.clip(jnp.mean(jnp.abs(w)), EPS_Q)
            y = jnp.clip(jnp.round(w / s), -1, 1) * s
            return w + jax.lax.stop_gradient(y - w)

        def bitlinear(x, w, g):
            xq = activation_quant(rmsnorm(x, g))
            wq = weight_quant(w)
            return jnp.einsum('btc,oc->bto', xq, wq)
        B, T, C = x.shape
        n_head = 16
        head_dim = C // n_head
        q = bitlinear(x, wq, gq).reshape(B, T, n_head, head_dim).transpose(0, 2, 1, 3)
        k = bitlinear(x, wk, gk).reshape(B, T, n_head, head_dim).transpose(0, 2, 1, 3)
        v = bitlinear(x, wv, gv).reshape(B, T, n_head, head_dim).transpose(0, 2, 1, 3)
        att = jnp.einsum('bhqd,bhkd->bhqk', q, k) * (1.0 / np.sqrt(head_dim))
        causal = jnp.tril(jnp.ones((T, T), dtype=bool))
        att = jnp.where(causal[None, None], att, -jnp.inf)
        att = jax.nn.softmax(att, axis=-1)
        y = jnp.einsum('bhqk,bhkd->bhqd', att, v)
        y = y.transpose(0, 2, 1, 3).reshape(B, T, C)
        return bitlinear(y, wo, go)

    def _L1_cond2_ref(x, cat_ids, W, b):
        import jax, jax.numpy as jnp
        import numpy as np
        NUM_CATEGORIES = 64
        INPUT_DIM = 256
        HIDDEN_DIM = 256
        B = 64
        S = 64
        selected_W = W[cat_ids]
        selected_b = b[cat_ids]
        out = jnp.einsum('bsd,bdh->bsh', x, selected_W) + selected_b[:, None, :]
        return out

    def _L1_ffn_ref(x, weight, bias):
        import jax, jax.numpy as jnp
        import numpy as np
        FP8_MAX = 448.0
        SCALE = 1.0
        _FP8_DTYPE = getattr(jnp, 'float8_e4m3fn', jnp.float16)

        def quantize_e4m3(t, scale):
            return jnp.clip(t / scale, -FP8_MAX, FP8_MAX).astype(_FP8_DTYPE)
        B, N, C = x.shape
        x2d = x.reshape(B * N, C)
        x_mat = quantize_e4m3(x2d, SCALE).astype(jnp.float16)
        w_mat = quantize_e4m3(weight, SCALE).astype(jnp.float16)
        out2d = (x_mat @ w_mat.T).astype(jnp.float32) * (SCALE * SCALE)
        out2d = out2d + bias
        return out2d.reshape(B, N, -1)
    x = x + _L0_attn_ref(_L0_cond_ref(x, L0_cond_tau_ctx, condB_tauraws, L0_cond_Wg, L0_cond_bg, L0_cond_Wn1, L0_cond_bn1, cond_256, condB_bn2, cond_1024, L0_cond_Wsoma, L0_cond_bsoma, L0_cond_Wtemp, L0_cond_btemp, L0_cond_Wout, L0_cond_gamma, L0_cond_beta), L0_attn_in_proj_w, L0_attn_conv_k, L0_attn_conv_b, L0_attn_theta, L0_attn_decay_slopes, L0_attn_anchor_slopes, L0_attn_score_scale, L0_attn_deriv_logits, L0_attn_W_re, L0_attn_W_im, L0_attn_norm_scale, L0_attn_out_proj_w)
    x = x + _L0_ffn_ref(_L0_cond2_ref(x, L0_cond2_W1, L0_cond2_b1, L0_cond2_v, itok_B_0_2), L0_ffn_gate_w, L0_ffn_ew1, L0_ffn_ew2, L0_ffn_ew3, L0_ffn_sw1, L0_ffn_sw2, L0_ffn_sw3)
    x = x + _L1_attn_ref(_L1_cond_ref(x, itok_B_0_6, L1_cond_down_w, L1_cond_down_b, L1_cond_up_w, L1_cond_up_b, L1_cond_ln_g, L1_cond_ln_b), L1_attn_wq, L1_attn_wk, L1_attn_wv, L1_attn_wo, L1_attn_gq, L1_attn_gk, L1_attn_gv, L1_attn_go)
    x = x + _L1_ffn_ref(_L1_cond2_ref(x, itok_B_0_63, L1_cond2_W, L1_cond2_b), L1_ffn_weight, L1_ffn_bias)
    return x

_drawn_inputs = setup_inputs


def setup_inputs(seed=0):
    import zlib

    import numpy as np

    out = dict(_drawn_inputs(seed))
    spreads = {'condB_bn2': (0.0, 2.0),
     'L0_cond_bg': (-0.5, 0.6),
     'L0_cond_bn1': (0.0, 2.0),
     'L0_cond_bsoma': (0.0, 0.1),
     'L0_cond_btemp': (0.0, 0.47),
     'L0_cond_gamma': (1.0, 0.2),
     'L0_cond_beta': (0.0, 0.1),
     'L0_attn_conv_b': (0.0, 0.1),
     'L0_attn_score_scale': (1.0, 0.6),
     'L0_attn_norm_scale': (1.0, 0.2),
     'L1_cond_ln_g': (1.0, 0.2),
     'L1_cond_ln_b': (0.0, 0.1),
     'L1_attn_gq': (1.0, 0.6),
     'L1_attn_gk': (1.0, 0.6),
     'L1_attn_gv': (1.0, 0.2),
     'L1_attn_go': (1.0, 0.2),
     'L1_cond2_b': (0.0, 0.332),
     'L1_ffn_bias': (0.0, 0.1)}
    factors = {'condB_tauraws': 8.0,
     'cond_256': 8.0,
     'cond_1024': 57.247,
     'L0_cond_Wn1': 8.0,
     'L0_attn_anchor_slopes': 36.56,
     'L0_cond2_W1': 8.0,
     'L0_cond2_b1': 64.0,
     'L0_cond2_v': 8.0,
     'L0_ffn_gate_w': 8.0,
     'L0_ffn_ew1': 8.0,
     'L0_ffn_ew2': 8.0,
     'L0_ffn_ew3': 8.0,
     'L0_ffn_sw1': 8.0,
     'L0_ffn_sw2': 8.0,
     'L0_ffn_sw3': 8.0,
     'L1_cond_down_b': 8.0,
     'L1_cond_up_b': 5.108}
    for name, (base, spread) in spreads.items():
        noise = np.random.default_rng([zlib.crc32(name.encode()), seed]).standard_normal(out[name].shape)
        drawn = base * np.exp(spread * noise) if base else spread * noise
        out[name] = jnp.asarray(drawn.astype(out[name].dtype))
    for name, factor in factors.items():
        out[name] = (out[name] * factor).astype(out[name].dtype)
    return out
```

```python
from contextlib import ExitStack

import concourse.bass as bass
import numpy as np
from concourse import mybir

F32 = mybir.dt.float32
BF16 = mybir.dt.bfloat16
F16 = mybir.dt.float16
I32 = mybir.dt.int32
ACT = mybir.ActivationFunctionType
ALU = mybir.AluOpType
AX = mybir.AxisListType

P = 128
B, S, D = 8, 256, 256
BT = 2
T = BT * S
TILES = B // BT
NS = T // P
DC = D // P
ND = 8
HID = 64
HEADS_B, HD_B = 32, 16
INNER = HEADS_B * HD_B
IC = INNER // P
C_IN = 2 * INNER + HEADS_B
TAPS = 4
NE, FF = 8, 512
EXPERTS = NE + 1
FC = FF // P
NH, HD = 16, 16
MAGIC = 12582912.0
TWO_PI = 6.283185307179586
TWO_PI_HI = 6.28125
TWO_PI_LO = TWO_PI - TWO_PI_HI
PI_SAFE = 3.1415925
NEG = -1e30

VEC_COLS = [("tau", 1 + ND), ("deriv", 3), ("bg", DC), ("btemp", DC), ("bsoma", DC), ("gamma", DC), ("beta", DC),
            ("bn1", 1), ("bn2", 1), ("blend", DC * ND), ("conv_k", TAPS * 9), ("conv_b", 9), ("theta", IC),
            ("slope", 1), ("score_scale", 1), ("norm_re", 1), ("norm_im", 1), ("b1", 1), ("fbias", DC),
            ("eps5", 1), ("eps6", 1), ("half_pi", 1), ("zero", 1)]
VEC = {}
_at = 0
for _name, _n in VEC_COLS:
    VEC[_name] = (_at, _n)
    _at += _n
NVEC = _at

WEIGHTS = {
    "w_g": (P, (2 * DC, D)), "w_n1": (P, (DC, HID)), "w_n2": (HID, (ND,)), "w_soma": (P, (DC, D)),
    "w_temp": (P, (DC, D)), "w_out": (P, (DC, D)), "w_in": (P, (DC, C_IN)), "w_re": (P, (P,)), "w_im": (P, (P,)),
    "w_proj": (P, (IC, D)), "w_1": (P, (DC, HID)), "v_col": (HID, (1,)), "w_route": (P, (DC, NE)),
    "g_rows": (P, (4, D)),
}
CONSTS = {
    "ident": (P, (P,)), "ones": (P, (1,)), "head_sum": (P, (IC, HEADS_B)),
    "pool_count": (P, (3, 2)), "dist": (HEADS_B, (S,)), "head_sel": (HEADS_B, (IC, P)),
    "causal": (P, (P,)), "expert_no": (P, (NS, NE)),
}


EARLY = ["ident", "ones", "w_n1", "w_soma", "w_g", "w_n2", "dist", "w_temp", "w_out"]
MID = ["w_in", "head_sel", "head_sum", "w_re", "w_im", "w_proj", "w_1", "v_col", "pool_count", "w_route",
       "expert_no"]
N_EARLY, N_MID = len(EARLY) + 1, len(MID) + 1
DVE_MAXIMA, DVE_SLOPES, DVE_SUMS = 4, 22, 43
CHAIN = {"dve": 261, "act": 96}


class Signal:

    def __init__(self, sem, per_tile, before):
        self.sem, self.per_tile, self.before, self.given = sem, per_tile, before, 0

    def at(self, t, k):
        return t * self.per_tile + (self.before + k)


def adaln_attention_ffn(nc, dram, out):
    with ExitStack() as ctx:
        def sb(name, shape, dt=F32):
            return ctx.enter_context(nc.sbuf_tensor(name, shape, dt))

        signals = []

        def signal(name, per_tile=1, before=0):
            signals.append((name, Signal(ctx.enter_context(nc.semaphore(name)), per_tile, before)))
            return signals[-1][1]

        w = {n: sb(n, [p, *shape]) for n, (p, shape) in (WEIGHTS | CONSTS).items()}
        vecs = sb("vecs", [P, NVEC])

        def col(name, k=0, p=P):
            at = VEC[name][0] + k
            return vecs[0:p, at:at + 1]

        expert_w = sb("expert_w", [P, EXPERTS, 2 * DC * FF + FC * D])

        def up_weight(e, which, c, m):
            at = (which * DC + c) * FF + m * P
            return expert_w[:, e, at:at + P]

        def down_weight(e, m, c):
            at = 2 * DC * FF + m * D + c * P
            return expert_w[:, e, at:at + P]

        ids_row = sb("ids_row", [1, 2 * B], I32)
        kind_ids = sb("kind_ids", [P, B], I32)

        decay = sb("decay", [P, 1 + ND])
        blend = sb("blend", [P, DC, ND])
        deriv = sb("deriv_w", [P, 4])
        half_b = sb("half_b", [P, 2 * DC + 1])
        slope = sb("slope_sb", [HEADS_B, 1])
        time_w = w["dist"]
        pool_mask = sb("pool_mask", [P, 3, 2, S], BF16)
        tern_qk = sb("tern_qk", [P, 2, DC, 4 * P], BF16)
        tern_vo = sb("tern_vo", [P, 2, DC, D], BF16)
        w_scale = sb("w_scale", [P, 8])
        qk_scale = sb("qk_scale", [P, 1])
        f8_w = sb("f8_w", [P, DC, D], BF16)
        ident_b = sb("ident_b", [P, P], BF16)
        causal_a = sb("causal_a", [P, 4 * P], BF16)
        kind = sb("kind", [P, B, 3])
        small = sb("small", [P, 640])

        def sm(at, n, p=P):
            return small[0:p, at:at + n]

        UNITS = 22
        arena = sb("arena", [P, UNITS * T])

        def unit(a, n=1, p=P):
            return arena[0:p, a * T:(a + n) * T]

        def chunks(a, n):
            return unit(a, n).rearrange("p (c n) -> p c n", c=n)

        zpad = sb("zpad", [P, 2, BT, TAPS - 1 + S])
        adapt_down = sb("adapt_down", [P, BT, DC, P])
        adapt_up = sb("adapt_up", [P, BT, D])
        adapt_bd = sb("adapt_bd", [P, BT])
        cat_b = sb("cat_b", [P, BT, DC])
        psum = ctx.enter_context(nc.psum_tensor("psum", [P, 8, T], F32))
        psum_b = psum[:, :, :].rearrange("p a n -> p (a n)").bitcast(BF16).rearrange("p (a n) -> p a n", a=8)

        loads = {n: signal(n + "_in", 0) for n in ("early", "mid", "attn", "late")}
        ids_in = signal("ids_in", 0)
        expert_in = signal("expert_in", 0)
        setup_dve = signal("setup_dve", 0)
        setup_act = signal("setup_act", 0)
        setup_pe = signal("setup_pe", 0)
        setup_pool = signal("setup_pool", 0)

        x_in = signal("x_in", 16)
        adapt_in = signal("adapt_in", 2 * BT * 16)
        adapt_rows_in = signal("adapt_rows_in", 3 * BT * 16)
        adapt_cols_in = signal("adapt_cols_in", 2 * BT * 16)
        cat_in = signal("cat_in", BT * 16)
        out_stored = signal("out_stored", 16, before=1)
        dve_chain = signal("dve_chain", CHAIN["dve"])
        act_chain = signal("act_chain", CHAIN["act"])
        ctx_ready = signal("ctx_ready")
        pe_soma = signal("pe_soma")
        pe_gate = signal("pe_gate")
        h1_ready = signal("h1_ready")
        soma_ready = signal("soma_ready")
        gate_tanh = signal("gate_tanh")
        pe_mod = signal("pe_mod")
        mod_tanh = signal("mod_tanh")
        mod_ready = signal("mod_ready")
        pe_mod_rows = signal("pe_mod_rows", ND)
        trace_ready = signal("trace_ready", ND)
        pe_trace_used = signal("pe_trace_used", ND)
        temporal_ready = signal("temporal_ready")
        pe_temp = signal("pe_temp")
        temp_tanh = signal("temp_tanh")
        mixed_ready = signal("mixed_ready")
        pe_cond = signal("pe_cond")
        cond_stats = signal("cond_stats")
        cond_std = signal("cond_std")
        cond_norm = signal("cond_norm")
        pe_cond_t = signal("pe_cond_t")
        cond_ready = signal("cond_ready")
        pe_z = signal("pe_z", 1 + 2 * IC)
        z_copied = signal("z_copied", 1 + 2 * IC)
        s_clipped = signal("s_clipped")
        p_exp = signal("p_exp")
        p_ready = signal("p_ready")
        pe_p_rows = signal("pe_p_rows", IC)
        val_ready = signal("val_ready", IC)
        gconv_ready = signal("gconv_ready", IC)
        phi_ready = signal("phi_ready", IC)
        gtanh_ready = signal("gtanh_ready", IC)
        angle_ready = signal("angle_ready", IC)
        trig_ready = signal("trig_ready", IC)
        mean_ready = signal("mean_ready", IC)
        sq_ready = signal("sq_ready", IC)
        pe_sq = signal("pe_sq", IC)
        pe_y = signal("pe_y", IC)
        yg_ready = signal("yg_ready", IC)
        rms_sqrt = signal("rms_sqrt")
        rms_ready = signal("rms_ready")
        pe_rms_rows = signal("pe_rms_rows")
        ynorm_ready = signal("ynorm_ready")
        pe_proj = signal("pe_proj")
        x1_ready = signal("x1_ready")
        pe_x1_rows = signal("pe_x1_rows")
        pe_score_hid = signal("pe_score_hid")
        x1_rows_ready = signal("x1_rows_ready")
        score_hid = signal("score_hid")
        pe_score = signal("pe_score")
        score_max = signal("score_max")
        pool_exp = signal("pool_exp")
        pool_p = signal("pool_p")
        pe_pool_t = signal("pe_pool_t")
        pool_t = signal("pool_t")
        pe_pool = signal("pe_pool")
        pool_ready = signal("pool_ready")
        pe_route = signal("pe_route")
        top_ready = signal("top_ready")
        route_exp = signal("route_exp")
        share_ready = signal("share_ready")
        pe_share_t = signal("pe_share_t")
        share_t = signal("share_t")
        pe_share_rows = signal("pe_share_rows", NE)
        share_rows = signal("share_rows", NE)
        xw_ready = signal("xw_ready", NE)
        pe_up = signal("pe_up", EXPERTS * FC)
        h_tanh = signal("h_tanh", EXPERTS * FC)
        h_read = signal("h_read", EXPERTS * FC)
        g_ready = signal("g_ready", EXPERTS * FC)
        pe_down = signal("pe_down", EXPERTS)
        x2_ready = signal("x2_ready")
        pe_bottle = signal("pe_bottle")
        bottle_ready = signal("bottle_ready")
        pe_adapt = signal("pe_adapt")
        adapt_stats = signal("adapt_stats")
        adapt_std = signal("adapt_std")
        adapt_ready = signal("adapt_ready")
        rms_in = signal("rms_in")
        int_ready = signal("int_ready", 3)
        pe_int_t = signal("pe_int_t", 3)
        int_t = signal("int_t", 3)
        pe_kscale = signal("pe_kscale")
        kscale_ready = signal("kscale_ready")
        kscale_diag = signal("kscale_diag")
        pe_q = signal("pe_q")
        q_ready = signal("q_ready")
        pe_k = signal("pe_k")
        k_ready = signal("k_ready")
        pe_v = signal("pe_v")
        v_ready = signal("v_ready")
        NSTEP = 3 * BT
        pe_logits = signal("pe_logits", NSTEP)
        row_max = signal("row_max", NSTEP)
        probs_ready = signal("probs_ready", NSTEP)
        pe_probs_t = signal("pe_probs_t", 4 * NSTEP)
        probs_t = signal("probs_t", 4 * NSTEP)
        pe_heads = signal("pe_heads", NSTEP)
        heads_ready = signal("heads_ready", 2 * BT)
        y_rms = signal("y_rms")
        y_int = signal("y_int")
        y_diag = signal("y_diag")
        pe_yint_t = signal("pe_yint_t")
        yint_t = signal("yint_t")
        pe_yscale = signal("pe_yscale")
        yscale_ready = signal("yscale_ready")
        pe_o = signal("pe_o")
        x3_ready = signal("x3_ready")
        pe_cat = signal("pe_cat")
        f8_ready = signal("f8_ready", before=1)
        pe_f8 = signal("pe_f8")
        half_ready = signal("half_ready")
        out_ready = signal("out_ready", before=1)

        x = chunks(0, 2)
        ctx_t, gated = chunks(2, 2), chunks(4, 2)
        scaled = [chunks(6, 2), chunks(8, 2)]
        trace = [chunks(10, 2), chunks(12, 2)]
        gate_t, soma = chunks(14, 2), chunks(16, 2)
        mod, h1 = unit(18, 1, ND), unit(19, 1, HID)
        temporal = chunks(2, 2)
        cond_rows = unit(4, 2).rearrange("p (s d) -> p s d", s=NS)
        cond = chunks(20, 2)
        conv = [unit(2), unit(3)]
        p_t, inv_den = unit(4, 1, HEADS_B), unit(5, 1, HEADS_B)
        phi, turns, angle, sin_t, cos_t, mean_re, mean_im = (unit(6 + k) for k in range(7))
        gtanh, gate_s = unit(13), unit(14)
        yg = chunks(15, 4)
        rms_b = unit(19, 1, HEADS_B)
        score_h = unit(2, 1, HID)
        masked = unit(3, 2).rearrange("p (g l) -> p g l", g=4)
        pool_w = unit(5, 2).rearrange("p (g l) -> p g l", g=4)
        pool_wt = unit(7, 2).rearrange("p (b n) -> p b n", b=BT)
        x1_rows = unit(9, 2).rearrange("p (s d) -> p s d", s=NS)
        pooled = chunks(20, 2)
        g_buf = [chunks(2, 4), chunks(15, 4)]
        act_h = [unit(6), unit(7)]
        xw = [chunks(8, 2), chunks(10, 2)]
        share_b = unit(12)
        share_tt = unit(19, 1, NE)
        adapt_rows = unit(13, 2).rearrange("p (g b d) -> p g b d", g=2, b=BT)
        adapt_bu = arena[32:33, 19 * T:20 * T].rearrange("p (b d) -> p b d", b=BT)
        cat_w = unit(19, 2).rearrange("p (b c d) -> p b c d", b=BT, c=DC)
        bottle = unit(2)
        adapt_y = unit(3, 2).rearrange("p (s d) -> p s d", s=NS)
        attn_in = unit(5, 2).rearrange("p (s d) -> p s d", s=NS)
        scaled_in = unit(7, 2).rearrange("p (s d) -> p s d", s=NS)
        int_rows = unit(9).bitcast(BF16).rearrange("p (s d) -> p s d", s=NS)
        int_tt = unit(10).bitcast(BF16).rearrange("p (c n) -> p c n", c=DC)
        q_t, k_t = chunks(11, 4), chunks(15, 4)
        v_rows = unit(19, 2).rearrange("p (s d) -> p s d", s=NS)
        row_diag = unit(21).rearrange("p (s q) -> p s q", s=NS)
        kscale_b = unit(3)
        probs = unit(2, 4)
        probs_tt = [unit(7), unit(8)]
        head_out = unit(9, 2).rearrange("p (s d) -> p s d", s=NS)
        yscale_b = unit(3)
        f8_t = chunks(4, 2)
        f8_a, f8_b = chunks(6, 2), chunks(8, 2)
        y_rows = unit(11).bitcast(BF16).rearrange("p (s d) -> p s d", s=NS)
        y_tt = unit(12).bitcast(BF16).rearrange("p (c n) -> p c n", c=DC)
        f8_q = unit(15).bitcast(BF16).rearrange("p (c n) -> p c n", c=DC)
        half_t = unit(13).bitcast(F16).rearrange("p (c n) -> p c n", c=DC)
        out_t = chunks(16, 2)

        stat = small[:, 24:32].rearrange("p (s k) -> p s k", k=2)
        stat_mean, stat_var = stat[:, :, 0], stat[:, :, 1]
        raw_qkvo = unit(2, 4).rearrange("p (k c d) -> p k c d", k=4, c=DC)
        raw_f8, f8_tmp = unit(6), unit(7)
        raw_mask = unit(8, 3).rearrange("p (k j l) -> p k j l", k=3, j=2)

        block = ctx.enter_context(nc.Block())

        @block.sync
        def _(sp):
            def load(name, dst, sig):
                sp.dma_start(dst, dram[name]).then_inc(sig.sem, 16)

            load("vecs", vecs[:, :], loads["early"])
            for s in (out_stored, f8_ready, out_ready):
                sp.sem_inc(s.sem, s.before)
            for n in EARLY:
                load(n, w[n][...], loads["early"])
            load("ids_row", ids_row[:, :], ids_in)
            for n in MID:
                load(n, w[n][...], loads["mid"])
            load("kind_ids", kind_ids[:, :], loads["mid"])
            load("qkvo", raw_qkvo, loads["attn"])
            load("pool_mask", raw_mask, loads["attn"])
            load("w_f8", raw_f8, loads["attn"])
            load("g_rows", w["g_rows"][...], loads["attn"])
            load("causal", w["causal"][...], loads["attn"])
            sp.wait_ge(ids_in.sem, 16)
            with sp.Fori(0, TILES) as t:
                sp.wait_ge(out_ready.sem, out_ready.at(t, 0))
                sp.dma_start(x, dram["x_t"][bass.ds(t, 1)].rearrange("a p c n -> (a p) c n")).then_inc(x_in.sem, 16)
                for b in range(BT):
                    who = sp.value_load(ids_row[0:1, bass.ds(t * BT + b + B, 1)])
                    if b == 0:
                        sp.wait_ge(f8_ready.sem, f8_ready.at(t, 0))
                    sp.dma_start(cat_b[:, b, :], dram["cat_b"][bass.ds(who, 1)].rearrange("a p c -> (a p) c")) \
                        .then_inc(adapt_cols_in.sem, 16)
                    who = sp.value_load(ids_row[0:1, bass.ds(t * BT + b, 1)])
                    sp.dma_start(adapt_down[:, b, :, :],
                                 dram["down_w"][bass.ds(who, 1)].rearrange("a p c n -> (a p) c n")) \
                        .then_inc(adapt_in.sem, 16)
                    sp.dma_start(adapt_up[:, b, :], dram["up_w"][bass.ds(who, 1)].rearrange("a p n -> (a p) n")) \
                        .then_inc(adapt_in.sem, 16)
                    sp.dma_start(adapt_bd[:, b:b + 1], dram["down_b"][bass.ds(who, 1)].rearrange("a p n -> (a p) n")) \
                        .then_inc(adapt_cols_in.sem, 16)
                for b in range(BT):
                    who = sp.value_load(ids_row[0:1, bass.ds(t * BT + b, 1)])
                    if b == 0:
                        sp.wait_ge(share_t.sem, share_t.at(t, 1))
                    for k, name in enumerate(("ln_g", "ln_b")):
                        src = dram[name][bass.ds(who, 1)].rearrange("a b d -> (a b) d")
                        sp.dma_start(adapt_rows[:, k, b, :], src.broadcast_to([P, D])).then_inc(adapt_rows_in.sem, 16)
                    sp.dma_start(adapt_bu[:, b, :], dram["up_b"][bass.ds(who, 1)].rearrange("a b d -> (a b) d")) \
                        .then_inc(adapt_rows_in.sem, 16)
                for b in range(BT):
                    who = sp.value_load(ids_row[0:1, bass.ds(t * BT + b + B, 1)])
                    if b == 0:
                        sp.wait_ge(pe_heads.sem, pe_heads.at(t, NSTEP))
                    sp.dma_start(cat_w[:, b, :, :], dram["cat_w"][bass.ds(who, 1)].rearrange("a p c n -> (a p) c n")) \
                        .then_inc(cat_in.sem, 16)
                sp.wait_ge(out_ready.sem, out_ready.at(t, 1))
                sp.dma_start(out[bass.ds(t, 1)].rearrange("a p c n -> (a p) c n"), out_t).then_inc(out_stored.sem, 16)
            sp.wait_ge(out_stored.sem, out_stored.at(TILES, 0))

        @block.gpsimd
        def _(pool):
            for e in range(EXPERTS):
                pool.dma_start(expert_w[:, e, :], dram["expert_w"][e]).then_inc(expert_in.sem, 16)
            nc.gpsimd.memset(zpad[:, :, :, 0:TAPS - 1], 0.0).then_inc(setup_pool.sem, 1)
            nc.gpsimd.memset(tern_qk[:, :, :, :], 0.0).then_inc(setup_pool.sem, 1)
            with pool.Fori(0, TILES) as t:
                pool.wait_ge(pool_ready.sem, pool_ready.at(t, 1))
                for e in range(NE):
                    pool.wait_ge(share_rows.sem, share_rows.at(t, e + 1))
                    if e >= 2:
                        pool.wait_ge(pe_up.sem, pe_up.at(t, FC * (e - 1)))
                    nc.gpsimd.tensor_tensor(xw[e % 2][:, :, :], pooled[:, :, :],
                                            share_b[:, None, :].broadcast_to([P, DC, T]), ALU.mult) \
                        .then_inc(xw_ready.sem, 1)

        @block.scalar
        def _(act):
            a = nc.scalar.activation

            def setup(ins):
                setup_act.given += 1
                ins.then_inc(setup_act.sem, 1)
                act.wait_ge(setup_act.sem, setup_act.given)

            act.wait_ge(loads["early"].sem, 16 * N_EARLY)
            setup(a(decay[:, :], vecs[:, VEC["tau"][0]:VEC["tau"][0] + 1 + ND], ACT.Exp))
            setup(a(sm(0, 1, HEADS_B), col("slope", 0, HEADS_B), ACT.Abs))
            setup(a(sm(1, 1, HEADS_B), sm(0, 1, HEADS_B), ACT.Exp, scale=-1.0))
            act.wait_ge(setup_dve.sem, DVE_MAXIMA)
            setup(a(blend[:, :, :], blend[:, :, :], ACT.Exp))
            setup(a(deriv[:, 0:3], deriv[:, 0:3], ACT.Exp))
            act.wait_ge(setup_dve.sem, DVE_SLOPES)
            setup(a(time_w[:, :], time_w[:, :], ACT.Exp, scale=slope[:, 0:1]))

            def step(t, ins, sig=act_chain):
                sig.given += 1
                ins.then_inc(sig.sem, 1)
                act.wait_ge(sig.sem, sig.at(t, sig.given))

            def condition(t):
                act.wait_ge(pe_soma.sem, pe_soma.at(t, 1))
                step(t, a(h1, psum[0:HID, 0, :], ACT.Gelu, bias=col("bn1", 0, HID)), h1_ready)
                act.wait_ge(out_stored.sem, out_stored.at(t, 0))
                step(t, a(soma[:, 0, :], psum[:, 1, :], ACT.Gelu, bias=col("bsoma", 0)))
                step(t, a(soma[:, 1, :], psum[:, 2, :], ACT.Gelu, bias=col("bsoma", 1)), soma_ready)
                act.wait_ge(pe_gate.sem, pe_gate.at(t, 1))
                step(t, a(gate_t[:, 0, :], psum[:, 3, :], ACT.Tanh, bias=half_b[:, 0:1], scale=0.5))
                step(t, a(gate_t[:, 1, :], psum[:, 4, :], ACT.Tanh, bias=half_b[:, 1:2], scale=0.5), gate_tanh)
                act.wait_ge(pe_mod.sem, pe_mod.at(t, 1))
                step(t, a(mod, psum[0:ND, 5, :], ACT.Tanh, bias=half_b[0:ND, 4:5], scale=0.5), mod_tanh)
                act.wait_ge(pe_trace_used.sem, pe_trace_used.at(t, ND))
                step(t, a(temporal[:, :, :], psum[:, 0:2, :], ACT.Copy), temporal_ready)
                act.wait_ge(pe_temp.sem, pe_temp.at(t, 1))
                step(t, a(gate_t[:, 0, :], psum[:, 2, :], ACT.Tanh, bias=half_b[:, 2:3], scale=0.5))
                step(t, a(gate_t[:, 1, :], psum[:, 3, :], ACT.Tanh, bias=half_b[:, 3:4], scale=0.5), temp_tanh)
                act.wait_ge(cond_stats.sem, cond_stats.at(t, 1))
                step(t, a(sm(0, NS), stat_var, ACT.Sqrt, bias=col("eps5"), scale=0.25), cond_std)
                act.wait_ge(pe_cond_t.sem, pe_cond_t.at(t, 1))
                step(t, a(cond[:, 0, :], psum[:, 6, :], ACT.Identity, bias=col("beta", 0), scale=col("gamma", 0)))
                step(t, a(cond[:, 1, :], psum[:, 7, :], ACT.Identity, bias=col("beta", 1), scale=col("gamma", 1)),
                     cond_ready)

            def z_out(t, bank, which, chunk, n, p=P):
                act.wait_ge(pe_z.sem, pe_z.at(t, n + 1))
                step(t, a(conv[which][0:p, :], psum[0:p, bank, :], ACT.Identity,
                          bias=col("conv_b", chunk, p), scale=col("conv_k", TAPS * chunk + TAPS - 1, p)))
                step(t, a(zpad[0:p, which, :, TAPS - 1:], psum[0:p, bank, :].rearrange("p (b n) -> p b n", b=BT),
                          ACT.Copy), z_copied)

            def scan_attention(t):
                z_out(t, 0, 0, 8, 0, HEADS_B)
                act.wait_ge(s_clipped.sem, s_clipped.at(t, 1))
                step(t, a(p_t, conv[0][0:HEADS_B, :], ACT.Exp), p_exp)
                for c in range(IC):
                    if c == 0:
                        act.wait_ge(p_ready.sem, p_ready.at(t, 1))
                    else:
                        act.wait_ge(yg_ready.sem, yg_ready.at(t, c))
                    z_out(t, 1, 0, c, 1 + 2 * c)
                    z_out(t, 2, 1, IC + c, 2 + 2 * c)
                    act.wait_ge(val_ready.sem, val_ready.at(t, c + 1))
                    step(t, a(phi, conv[0], ACT.Identity, bias=col("zero"), scale=col("theta", c)), phi_ready)
                    act.wait_ge(gconv_ready.sem, gconv_ready.at(t, c + 1))
                    step(t, a(gtanh, conv[1], ACT.Tanh, scale=0.5), gtanh_ready)
                    act.wait_ge(angle_ready.sem, angle_ready.at(t, c + 1))
                    step(t, a(sin_t, angle, ACT.Sin))
                    step(t, a(angle, angle, ACT.Abs))
                    step(t, a(cos_t, angle, ACT.Sin, bias=col("half_pi"), scale=-1.0), trig_ready)
                    act.wait_ge(mean_ready.sem, mean_ready.at(t, c + 1))
                    step(t, a(sin_t, mean_im, ACT.Square))
                    step(t, a(cos_t, mean_re, ACT.Square), sq_ready)
                act.wait_ge(pe_sq.sem, pe_sq.at(t, IC))
                step(t, a(rms_b, psum[0:HEADS_B, 6, :], ACT.Sqrt, bias=col("eps5", 0, HEADS_B)), rms_sqrt)

            def pool_prompt(t):
                act.wait_ge(pe_x1_rows.sem, pe_x1_rows.at(t, 1))
                step(t, a(x1_rows.rearrange("p s d -> p (s d)"), psum[:, 1:3, :].rearrange("p a n -> p (a n)"),
                          ACT.Copy), x1_rows_ready)
                act.wait_ge(pe_score_hid.sem, pe_score_hid.at(t, 1))
                step(t, a(score_h, psum[0:HID, 3, :], ACT.Tanh, bias=col("b1", 0, HID)), score_hid)
                act.wait_ge(score_max.sem, score_max.at(t, 1))
                for g in range(4):
                    step(t, a(pool_w[:, g, :], masked[:, g, :], ACT.Exp, bias=sm(8 + g, 1), accum_out=sm(12 + g, 1)),
                         pool_exp if g == 3 else act_chain)
                act.wait_ge(pe_pool_t.sem, pe_pool_t.at(t, 1))
                step(t, a(pool_wt.rearrange("p b n -> p (b n)"), psum[:, 5:7, :].rearrange("p a n -> p (a n)"),
                          ACT.Copy), pool_t)
                act.wait_ge(pe_pool.sem, pe_pool.at(t, 1))
                step(t, a(pooled[:, 0, :], psum[:, 7, :], ACT.Copy))
                step(t, a(pooled[:, 1, :], psum[:, 1, :], ACT.Copy), pool_ready)

            def experts(t):
                act.wait_ge(top_ready.sem, top_ready.at(t, 1))
                step(t, a(sm(160, NS), sm(160, NS), ACT.Exp), route_exp)
                act.wait_ge(pe_share_t.sem, pe_share_t.at(t, 1))
                step(t, a(share_tt, psum[0:NE, 1, :], ACT.Copy), share_t)

                def share_out(e):
                    act.wait_ge(pe_share_rows.sem, pe_share_rows.at(t, e + 1))
                    if e:
                        act.wait_ge(xw_ready.sem, xw_ready.at(t, e))
                    step(t, a(share_b, psum[:, 2, :], ACT.Copy), share_rows)

                share_out(0)
                for e in range(EXPERTS):
                    for m in range(FC):
                        n = e * FC + m
                        act.wait_ge(pe_up.sem, pe_up.at(t, n + 1))
                        if n >= 2:
                            act.wait_ge(g_ready.sem, g_ready.at(t, n - 1))
                        step(t, a(act_h[n % 2], psum[:, 3 + n % 2, :], ACT.Tanh, scale=0.5), h_tanh)
                    if e + 1 < NE:
                        share_out(e + 1)

            def adapter(t):
                act.wait_ge(pe_bottle.sem, pe_bottle.at(t, 1))
                act.wait_ge(adapt_cols_in.sem, adapt_cols_in.at(t, 2 * BT * 16))
                for b in range(BT):
                    step(t, a(bottle[:, b * S:(b + 1) * S], psum[:, 1, b * S:(b + 1) * S], ACT.Relu,
                              bias=adapt_bd[:, b:b + 1]), bottle_ready if b else act_chain)
                act.wait_ge(adapt_stats.sem, adapt_stats.at(t, 1))
                step(t, a(sm(0, NS), stat_var, ACT.Sqrt, bias=col("eps5")), adapt_std)

            def mean_square(t, rows, scratch, sums, std, signal_sums):
                for s in range(NS):
                    step(t, a(scratch[:, s, :], rows[:, s, :], ACT.Square, accum_out=sm(sums + s, 1)))
                step(t, a(sm(std, NS), sm(sums, NS), ACT.Sqrt, bias=col("eps6"), scale=1.0 / D), signal_sums)

            def attention(t):
                act.wait_ge(adapt_ready.sem, adapt_ready.at(t, 1))
                mean_square(t, attn_in, adapt_y, 200, 204, rms_in)
                for g in range(3):
                    act.wait_ge(pe_int_t.sem, pe_int_t.at(t, g + 1))
                    if g == 1:
                        act.wait_ge(pe_q.sem, pe_q.at(t, 1))
                    if g == 2:
                        act.wait_ge(pe_k.sem, pe_k.at(t, 1))
                    step(t, a(int_tt[:, :, :], psum_b[:, 0:2, 0:T], ACT.Copy), int_t)
                    if g == 0:
                        act.wait_ge(pe_q.sem, pe_q.at(t, 1))
                        step(t, a(q_t[:, :, :], psum[:, 2:6, :], ACT.Copy), q_ready)
                    if g == 1:
                        act.wait_ge(pe_kscale.sem, pe_kscale.at(t, 1))
                        step(t, a(kscale_b, psum[:, 6, :], ACT.Copy), kscale_ready)

                def probs_out(n):
                    act.wait_ge(row_max.sem, row_max.at(t, n + 1))
                    if n:
                        act.wait_ge(pe_probs_t.sem, pe_probs_t.at(t, 4 * n))
                    b, part = divmod(n, 3)
                    qc, half = (0, 0) if part == 0 else (1, part - 1)
                    s = b * 2 + qc
                    per, width = (4, P) if qc == 0 else (2, S)
                    for r in range(4):
                        for j in range(per):
                            head = 4 * (half * 2 + j) + r
                            at = r * T + j * width
                            last = r == 3 and j == per - 1
                            step(t, a(probs[:, at:at + width], psum[:, r, j * width:(j + 1) * width], ACT.Exp,
                                      bias=sm(320 + s * NH + head, 1), scale=sm(216 + s, 1),
                                      accum_out=sm(384 + s * NH + head, 1)), probs_ready if last else act_chain)

                def probs_t_out(n):
                    for r in range(4):
                        k = 4 * n + r
                        act.wait_ge(pe_probs_t.sem, pe_probs_t.at(t, k + 1))
                        step(t, a(probs_tt[k % 2], psum[:, 4 + k % 2, :], ACT.Copy), probs_t)

                for n in range(NSTEP):
                    probs_out(n)
                    probs_t_out(n)
                act.wait_ge(heads_ready.sem, heads_ready.at(t, 2 * BT))
                mean_square(t, head_out, scaled_in, 200, 204, y_rms)
                act.wait_ge(pe_yint_t.sem, pe_yint_t.at(t, 1))
                step(t, a(y_tt[:, :, :], psum_b[:, 0:2, 0:T], ACT.Copy), yint_t)
                act.wait_ge(pe_yscale.sem, pe_yscale.at(t, 1))
                step(t, a(yscale_b, psum[:, 2, :], ACT.Copy), yscale_ready)

            def last_ffn(t):
                act.wait_ge(pe_f8.sem, pe_f8.at(t, 1))
                step(t, a(half_t[:, :, :], psum[:, 4:6, :], ACT.Copy), half_ready)

            with act.Fori(0, TILES) as t:
                condition(t)
                scan_attention(t)
                pool_prompt(t)
                experts(t)
                adapter(t)
                attention(t)
                last_ffn(t)

        @block.vector
        def _(dve):
            v = nc.vector

            def setup(ins):
                setup_dve.given += 1
                ins.then_inc(setup_dve.sem, 1)
                dve.wait_ge(setup_dve.sem, setup_dve.given)

            def round_to_even(dst, src):
                return v.tensor_scalar(dst, src, MAGIC, MAGIC, ALU.add, ALU.subtract)

            dve.wait_ge(loads["early"].sem, 16 * N_EARLY)
            at, n = VEC["blend"]
            raw_blend = vecs[:, at:at + n].rearrange("p (c d) -> p c d", c=DC)
            setup(v.tensor_reduce(out=sm(20, DC), in_=raw_blend, axis=AX.X, op=ALU.max))
            setup(v.tensor_tensor(blend[:, :, :], raw_blend, sm(20, DC)[:, :, None].broadcast_to([P, DC, ND]), ALU.subtract))
            at, n = VEC["deriv"]
            setup(v.tensor_reduce(out=sm(22, 1), in_=vecs[:, at:at + n], axis=AX.X, op=ALU.max))
            setup(v.tensor_scalar(deriv[:, 0:3], vecs[:, at:at + n], sm(22, 1), None, ALU.subtract))
            assert setup_dve.given == DVE_MAXIMA
            at = VEC["bg"][0]
            setup(v.tensor_scalar(half_b[:, 0:2 * DC], vecs[:, at:at + 2 * DC], 0.5, None, ALU.mult))
            setup(v.tensor_scalar(half_b[0:ND, 2 * DC:2 * DC + 1], col("bn2", 0, ND), 0.5, None, ALU.mult))
            act_u, s1, s2, acc, r = (sm(k, 1, HEADS_B) for k in (1, 2, 3, 4, 5))
            dve.wait_ge(setup_act.sem, 3)
            setup(v.tensor_scalar(s1, act_u, 2.0, None, ALU.add))
            setup(v.reciprocal(s1, s1))
            setup(v.tensor_tensor(s1, s1, act_u, ALU.mult))
            setup(v.tensor_tensor(s2, s1, s1, ALU.mult))
            setup(v.tensor_scalar(acc, s2, 1.0 / 19, 1.0 / 17, ALU.mult, ALU.add))
            for k in (15, 13, 11, 9, 7, 5, 3, 1):
                setup(v.tensor_scalar(acc, acc, s2, 1.0 / k, ALU.mult, ALU.add))
            setup(v.tensor_tensor(acc, acc, s1, ALU.mult))
            setup(v.tensor_scalar(r, col("slope", 0, HEADS_B), 0.0, None, ALU.max))
            setup(v.scalar_tensor_tensor(slope[:, :], acc, -2.0, r, ALU.mult, ALU.subtract))
            assert setup_dve.given == DVE_SLOPES
            setup(v.tensor_scalar(decay[:, :], decay[:, :], 1.0, None, ALU.add))
            setup(v.reciprocal(decay[:, :], decay[:, :]))
            dve.wait_ge(setup_act.sem, 5)
            setup(v.tensor_reduce(out=sm(20, DC), in_=blend[:, :, :], axis=AX.X, op=ALU.add))
            setup(v.reciprocal(sm(20, DC), sm(20, DC)))
            setup(v.tensor_tensor(blend[:, :, :], blend[:, :, :], sm(20, DC)[:, :, None].broadcast_to([P, DC, ND]),
                                  ALU.mult))
            setup(v.tensor_scalar(blend[:, :, :], blend[:, :, :], 0.5, None, ALU.mult))
            setup(v.tensor_reduce(out=sm(22, 1), in_=deriv[:, 0:3], axis=AX.X, op=ALU.add))
            setup(v.reciprocal(sm(22, 1), sm(22, 1)))
            setup(v.tensor_scalar(deriv[:, 0:3], deriv[:, 0:3], sm(22, 1), None, ALU.mult))
            setup(v.tensor_scalar(deriv[:, 3:4], deriv[:, 2:3], -1.0, None, ALU.mult))
            dve.wait_ge(loads["mid"].sem, 16 * N_MID)
            setup(v.tensor_scalar(w["w_re"][:, :], w["w_re"][:, :], col("norm_re"), 0.5, ALU.mult, ALU.mult))
            setup(v.tensor_scalar(w["w_im"][:, :], w["w_im"][:, :], col("norm_im"), 0.5, ALU.mult, ALU.mult))
            setup(v.tensor_copy(sm(40, B), kind_ids[:, :]))
            setup(v.tensor_scalar(kind[:, :, 0], sm(40, B), 0.0, None, ALU.is_equal))
            setup(v.tensor_scalar(kind[:, :, 1], sm(40, B), 1.0, None, ALU.is_equal))
            setup(v.tensor_tensor(kind[:, :, 2], kind[:, :, 0], kind[:, :, 1], ALU.add))
            setup(v.tensor_scalar(kind[:, :, 2], kind[:, :, 2], -1.0, 1.0, ALU.mult, ALU.add))
            setup(v.tensor_copy(ident_b[:, :], w["ident"][:, :]))
            dve.wait_ge(loads["attn"].sem, 16 * 5)
            setup(v.tensor_copy(pool_mask[:, :, :, :], raw_mask))
            dve.wait_ge(setup_pool.sem, 2)
            setup(v.tensor_copy(causal_a[:, :].rearrange("p (k n) -> p k n", k=4),
                                w["causal"][:, None, :].broadcast_to([P, 4, P])))
            setup(v.tensor_reduce(out=sm(44, 4), in_=raw_qkvo.rearrange("p k c d -> p k (c d)"), axis=AX.X, op=ALU.add,
                                  apply_absolute_value=True))
            assert setup_dve.given == DVE_SUMS
            dve.wait_ge(setup_pe.sem, 1)
            setup(v.tensor_scalar(w_scale[:, 0:4], psum[:, 0, 0:4], 1.0 / (D * D), 1e-5, ALU.mult, ALU.max))
            assert setup_dve.given == DVE_SUMS + 1
            setup(v.reciprocal(w_scale[:, 4:8], w_scale[:, 0:4]))
            setup(v.tensor_scalar(qk_scale[:, :], w_scale[:, 0:1], w_scale[:, 1:2], HD ** -0.5, ALU.mult, ALU.mult))
            for k in range(4):
                raw = raw_qkvo[:, k, :, :]
                setup(v.tensor_scalar(raw, raw, w_scale[:, 4 + k:5 + k], MAGIC, ALU.mult, ALU.add))
                setup(v.tensor_scalar(raw, raw, MAGIC, 1.0, ALU.subtract, ALU.min))
                if k < 2:
                    for c in range(DC):
                        setup(v.tensor_scalar(tern_qk[:, k, c, :].rearrange("p (h d) -> p h d", h=NH)[:, :, 0:HD],
                                              raw[:, c, :].rearrange("p (h d) -> p h d", h=NH), -1.0, None, ALU.max))
                else:
                    setup(v.tensor_scalar(tern_vo[:, k - 2, :, :], raw, -1.0, None, ALU.max))

            def float8_values(run, val, tmp, dst):
                run(v.tensor_scalar(val, val, 448.0, -448.0, ALU.min, ALU.max))
                run(v.tensor_scalar(tmp.bitcast(I32), val.bitcast(I32), 0x7F800000, None, ALU.bitwise_and))
                run(v.tensor_scalar(tmp, tmp, 2.0 ** -6, 1.5 * 2.0 ** 20, ALU.max, ALU.mult))
                run(v.tensor_tensor(val, val, tmp, ALU.add))
                run(v.tensor_tensor(dst, val, tmp, ALU.subtract))

            float8_values(setup, raw_f8, f8_tmp, f8_w[:, :, :].rearrange("p c d -> p (c d)"))

            def step(t, ins, sig=dve_chain, wait=True):
                sig.given += 1
                ins.then_inc(sig.sem, 1)
                if wait:
                    dve.wait_ge(sig.sem, sig.at(t, sig.given))

            def averages(t, dst, src, decay_col, last):
                for c in range(DC):
                    for b in range(BT):
                        tokens = slice(b * S, (b + 1) * S)
                        step(t, v.tensor_tensor_scan(dst[:, c, tokens], decay_col.broadcast_to([P, S]), src[:, c, tokens],
                                                     0.0, ALU.mult, ALU.add),
                             last if (c, b) == (DC - 1, BT - 1) else dve_chain)

            def row_stats(t, rows, last):
                for s in range(NS):
                    step(t, v.bn_stats(sm(32 + 6 * s, 6), rows[:, s, :]))
                step(t, v.memset(sm(620, 1), 0.0), wait=False)
                for s in range(NS):
                    step(t, v.bn_aggr(sm(24 + 2 * s, 2), sm(32 + 6 * s, 6)), last if s == NS - 1 else dve_chain,
                         wait=s == NS - 1)

            def condition(t):
                dve.wait_ge(x_in.sem, x_in.at(t, 16))
                averages(t, ctx_t, x, decay[:, 0:1], ctx_ready)
                dve.wait_ge(gate_tanh.sem, gate_tanh.at(t, 1))
                step(t, v.scalar_tensor_tensor(gated[:, :, :], gate_t[:, :, :], 1.0, x[:, :, :], ALU.add, ALU.mult))
                dve.wait_ge(mod_tanh.sem, mod_tanh.at(t, 1))
                step(t, v.tensor_scalar(mod, mod, 0.5, 1.0, ALU.mult, ALU.add), mod_ready)
                for d in range(ND):
                    dve.wait_ge(pe_mod_rows.sem, pe_mod_rows.at(t, d + 1))
                    for c in range(DC):
                        step(t, v.scalar_tensor_tensor(scaled[d % 2][:, c, :], gated[:, c, :], blend[:, c, d:d + 1],
                                                       psum[:, 6 + d % 2, :], ALU.mult, ALU.mult))
                    if d >= 2:
                        dve.wait_ge(pe_trace_used.sem, pe_trace_used.at(t, d - 1))
                    averages(t, trace[d % 2], scaled[d % 2], decay[:, 1 + d:2 + d], trace_ready)
                dve.wait_ge(temp_tanh.sem, temp_tanh.at(t, 1))
                step(t, v.scalar_tensor_tensor(gate_t[:, :, :], gate_t[:, :, :], 1.0, soma[:, :, :], ALU.add, ALU.mult),
                     mixed_ready)
                dve.wait_ge(pe_cond.sem, pe_cond.at(t, 1))
                rows = psum[:, 4:6, :].rearrange("p a (k d) -> p (a k) d", k=2)
                row_stats(t, rows, cond_stats)
                dve.wait_ge(cond_std.sem, cond_std.at(t, 1))
                step(t, v.reciprocal(sm(4, NS), sm(0, NS)))
                step(t, v.tensor_scalar(sm(4, NS), sm(4, NS), 0.5, None, ALU.mult))
                for s in range(NS):
                    step(t, v.tensor_scalar(cond_rows[:, s, :], rows[:, s, :], stat[:, s, 0:1], sm(4 + s, 1),
                                            ALU.subtract, ALU.mult), cond_norm if s == NS - 1 else dve_chain)

            def taps(t, which, chunk, n, p, last):
                dve.wait_ge(z_copied.sem, z_copied.at(t, n + 1))
                acc = conv[which][0:p, :].rearrange("p (b n) -> p b n", b=BT)
                for j in range(TAPS - 1):
                    step(t, v.scalar_tensor_tensor(acc, zpad[0:p, which, :, j:j + S], col("conv_k", TAPS * chunk + j, p),
                                                   acc, ALU.mult, ALU.add), last if j == TAPS - 2 else dve_chain)

            def scan_attention(t):
                taps(t, 0, 8, 0, HEADS_B, dve_chain)
                raw = conv[0][0:HEADS_B, :]
                step(t, v.tensor_scalar(raw, raw, col("score_scale", 0, HEADS_B), 20.0, ALU.mult, ALU.min))
                step(t, v.tensor_scalar(raw, raw, -20.0, None, ALU.max), s_clipped)
                dve.wait_ge(p_exp.sem, p_exp.at(t, 1))
                by_batch = p_t.rearrange("p (b n) -> p b n", b=BT)
                step(t, v.tensor_tensor(by_batch, by_batch, time_w[:, None, :].broadcast_to([HEADS_B, BT, S]), ALU.mult))
                one = w["ones"][:, 0:1]
                for b in range(BT):
                    tokens = slice(b * S, (b + 1) * S)
                    step(t, v.tensor_tensor_scan(inv_den[:, tokens], one[0:HEADS_B, :].broadcast_to([HEADS_B, S]),
                                                 p_t[:, tokens], 0.0, ALU.mult, ALU.add))
                step(t, v.tensor_scalar(inv_den, inv_den, 1e-4, None, ALU.max))
                step(t, v.reciprocal(inv_den, inv_den), p_ready)
                for c in range(IC):
                    val = conv[0]
                    taps(t, 0, c, 1 + 2 * c, P, val_ready)
                    taps(t, 1, IC + c, 2 + 2 * c, P, gconv_ready)
                    dve.wait_ge(phi_ready.sem, phi_ready.at(t, c + 1))
                    step(t, v.tensor_scalar(turns, phi, 1.0 / TWO_PI, MAGIC, ALU.mult, ALU.add))
                    step(t, v.tensor_scalar(turns, turns, MAGIC, None, ALU.subtract))
                    step(t, v.scalar_tensor_tensor(phi, turns, -TWO_PI_HI, phi, ALU.mult, ALU.add))
                    step(t, v.scalar_tensor_tensor(angle, turns, -TWO_PI_LO, phi, ALU.mult, ALU.add))
                    step(t, v.tensor_scalar(angle, angle, PI_SAFE, -PI_SAFE, ALU.min, ALU.max), angle_ready)
                    step(t, v.tensor_scalar(turns, val, deriv[:, 3:4], deriv[:, 1:2], ALU.mult, ALU.add))
                    step(t, v.tensor_tensor(turns, turns, val, ALU.mult))
                    dve.wait_ge(pe_p_rows.sem, pe_p_rows.at(t, c + 1))
                    step(t, v.scalar_tensor_tensor(phi, turns, deriv[:, 0:1], psum[:, 3, :], ALU.add, ALU.mult))
                    dve.wait_ge(gtanh_ready.sem, gtanh_ready.at(t, c + 1))
                    step(t, v.scalar_tensor_tensor(gate_s, gtanh, 1.0, conv[1], ALU.add, ALU.mult))
                    dve.wait_ge(trig_ready.sem, trig_ready.at(t, c + 1))
                    step(t, v.tensor_tensor(cos_t, phi, cos_t, ALU.mult))
                    step(t, v.tensor_tensor(sin_t, phi, sin_t, ALU.mult))
                    for mean, part in ((mean_re, cos_t), (mean_im, sin_t)):
                        for b in range(BT):
                            tokens = slice(b * S, (b + 1) * S)
                            step(t, v.tensor_tensor_scan(mean[:, tokens], one.broadcast_to([P, S]), part[:, tokens],
                                                         0.0, ALU.mult, ALU.add))
                    step(t, v.tensor_tensor(mean_re, mean_re, psum[:, 4, :], ALU.mult))
                    step(t, v.tensor_tensor(mean_im, mean_im, psum[:, 4, :], ALU.mult), mean_ready)
                    dve.wait_ge(pe_y.sem, pe_y.at(t, c + 1))
                    step(t, v.tensor_tensor(yg[:, c, :], psum[:, 5, :], gate_s, ALU.mult), yg_ready)
                    dve.wait_ge(pe_sq.sem, pe_sq.at(t, c + 1))
                dve.wait_ge(rms_sqrt.sem, rms_sqrt.at(t, 1))
                step(t, v.reciprocal(rms_b, rms_b), rms_ready)
                dve.wait_ge(pe_rms_rows.sem, pe_rms_rows.at(t, 1))
                step(t, v.tensor_tensor(yg[:, :, :], yg[:, :, :], psum[:, 1:5, :], ALU.mult), ynorm_ready)
                dve.wait_ge(pe_proj.sem, pe_proj.at(t, 1))
                step(t, v.tensor_tensor(x[:, 0, :], x[:, 0, :], psum[:, 0, :], ALU.add))
                step(t, v.tensor_tensor(x[:, 1, :], x[:, 1, :], psum[:, 5, :], ALU.add), x1_ready)

            def pool_prompt(t):
                now = sm(600, 3 * BT)
                step(t, v.tensor_copy(now.rearrange("p (b k) -> p b k", b=BT), kind[:, bass.ds(t * BT, BT), :]))
                dve.wait_ge(pe_score.sem, pe_score.at(t, 1))
                for b in range(BT):
                    dst = masked[:, 2 * b:2 * b + 2, :]
                    for k in range(3):
                        src = psum[:, 4, b * S:(b + 1) * S][:, None, :].broadcast_to([P, 2, S]) if k == 0 else dst
                        step(t, v.scalar_tensor_tensor(dst, pool_mask[:, k, :, :], sm(600 + 3 * b + k, 1), src,
                                                       ALU.mult, ALU.add))
                step(t, v.tensor_reduce(out=sm(8, 4), in_=masked, axis=AX.X, op=ALU.max, negate=True), score_max)
                for b in range(BT):
                    cnt = sm(56 + 2 * b, 2)
                    step(t, v.tensor_scalar(cnt, w["pool_count"][:, 0, :], sm(600 + 3 * b, 1), None, ALU.mult))
                    for k in (1, 2):
                        step(t, v.scalar_tensor_tensor(cnt, w["pool_count"][:, k, :], sm(600 + 3 * b + k, 1), cnt,
                                                       ALU.mult, ALU.add))
                dve.wait_ge(pool_exp.sem, pool_exp.at(t, 1))
                step(t, v.tensor_tensor(sm(12, 4), sm(12, 4), sm(56, 4), ALU.mult))
                step(t, v.reciprocal(sm(12, 4), sm(12, 4)))
                for g in range(4):
                    step(t, v.tensor_scalar(pool_w[:, g, :], pool_w[:, g, :], sm(12 + g, 1), None, ALU.mult),
                         pool_p if g == 3 else dve_chain)

            def route(t):
                def cols(at):
                    return sm(at, NS * NE).rearrange("p (s e) -> p s e", s=NS)

                def wide(at):
                    return sm(at, NS)[:, :, None].broadcast_to([P, NS, NE])

                score, first, tmp, second, share = cols(64), cols(96), cols(128), cols(288), cols(256)
                top1, top2, which, e2, w1, w2 = 164, 168, 172, 160, 176, 180
                number = w["expert_no"][:, :, :]
                dve.wait_ge(pe_route.sem, pe_route.at(t, 1))
                step(t, v.tensor_copy(score, psum[:, 0, 0:NS * NE].rearrange("p (s e) -> p s e", s=NS)))
                for top, onehot in ((top1, first), (top2, second)):
                    step(t, v.tensor_reduce(out=sm(top, NS), in_=score, axis=AX.X, op=ALU.max))
                    step(t, v.tensor_tensor(tmp, score, wide(top), ALU.is_lt))
                    step(t, v.scalar_tensor_tensor(tmp, tmp, float(NE), number, ALU.mult, ALU.add))
                    step(t, v.tensor_reduce(out=sm(which, NS), in_=tmp, axis=AX.X, op=ALU.min))
                    step(t, v.tensor_tensor(onehot, number, wide(which), ALU.is_equal))
                    if top == top1:
                        step(t, v.scalar_tensor_tensor(score, first, -3e38, score, ALU.mult, ALU.add))
                step(t, v.tensor_tensor(sm(e2, NS), sm(top2, NS), sm(top1, NS), ALU.subtract), top_ready)
                dve.wait_ge(route_exp.sem, route_exp.at(t, 1))
                step(t, v.tensor_scalar(sm(w1, NS), sm(e2, NS), 1.0, None, ALU.add))
                step(t, v.reciprocal(sm(w1, NS), sm(w1, NS)))
                step(t, v.tensor_tensor(sm(w2, NS), sm(e2, NS), sm(w1, NS), ALU.mult))
                step(t, v.tensor_tensor(share, first, wide(w1), ALU.mult))
                step(t, v.tensor_tensor(second, second, wide(w2), ALU.mult))
                step(t, v.tensor_tensor(share, share, second, ALU.add), share_ready)

            def experts(t):
                route(t)
                for e in range(EXPERTS):
                    for m in range(FC):
                        n = e * FC + m
                        dve.wait_ge(h_tanh.sem, h_tanh.at(t, n + 1))
                        step(t, v.scalar_tensor_tensor(act_h[n % 2], act_h[n % 2], 1.0, psum[:, 3 + n % 2, :],
                                                       ALU.add, ALU.mult), h_read)
                        if e >= 2:
                            dve.wait_ge(pe_down.sem, pe_down.at(t, e - 1))
                        step(t, v.scalar_tensor_tensor(g_buf[e % 2][:, m, :], act_h[n % 2], 0.5, psum[:, 5 + n % 2, :],
                                                       ALU.mult, ALU.mult), g_ready)
                dve.wait_ge(pe_down.sem, pe_down.at(t, EXPERTS))
                step(t, v.tensor_tensor(x[:, 0, :], x[:, 0, :], psum[:, 0, :], ALU.add))
                step(t, v.tensor_tensor(x[:, 1, :], x[:, 1, :], psum[:, 7, :], ALU.add), x2_ready)

            def adapter(t):
                dve.wait_ge(pe_adapt.sem, pe_adapt.at(t, 1))
                rows = psum[:, 2:4, :].rearrange("p a (k d) -> p (a k) d", k=2)
                row_stats(t, rows, adapt_stats)
                dve.wait_ge(adapt_std.sem, adapt_std.at(t, 1))
                step(t, v.reciprocal(sm(4, NS), sm(0, NS)))
                for s in range(NS):
                    step(t, v.tensor_scalar(attn_in[:, s, :], rows[:, s, :], stat[:, s, 0:1], sm(4 + s, 1),
                                            ALU.subtract, ALU.mult))
                dve.wait_ge(adapt_rows_in.sem, adapt_rows_in.at(t, 3 * BT * 16))
                for b in range(BT):
                    mine = attn_in[:, 2 * b:2 * b + 2, :]
                    for k, op in ((0, ALU.mult), (1, ALU.add)):
                        row = adapt_rows[:, k, b, :][:, None, :].broadcast_to([P, 2, D])
                        step(t, v.tensor_tensor(mine, mine, row, op), adapt_ready if (b, k) == (1, 1) else dve_chain)

            def to_integers(t, rows, g, dst, scale_at, last):
                row = w["g_rows"][:, g, :][:, None, :].broadcast_to([P, NS, D])
                step(t, v.tensor_tensor(scaled_in, rows, row, ALU.mult))
                step(t, v.tensor_reduce(out=sm(212, NS), in_=scaled_in, axis=AX.X, op=ALU.max,
                                        apply_absolute_value=True))
                step(t, v.tensor_tensor(sm(212, NS), sm(212, NS), sm(208, NS), ALU.mult))
                step(t, v.tensor_scalar(sm(212, NS), sm(212, NS), 1e-5, None, ALU.max))
                step(t, v.tensor_scalar(sm(scale_at, NS), sm(212, NS), 1.0 / 127, None, ALU.mult))
                step(t, v.reciprocal(sm(212, NS), sm(scale_at, NS)))
                step(t, v.tensor_tensor(sm(212, NS), sm(212, NS), sm(208, NS), ALU.mult))
                step(t, v.tensor_tensor(scaled_in, scaled_in, sm(212, NS)[:, :, None].broadcast_to([P, NS, D]), ALU.mult))
                step(t, round_to_even(dst, scaled_in), last)

            def attention(t):
                dve.wait_ge(rms_in.sem, rms_in.at(t, 1))
                step(t, v.reciprocal(sm(208, NS), sm(204, NS)))
                for g in range(3):
                    if g:
                        dve.wait_ge(pe_int_t.sem, pe_int_t.at(t, g))
                    to_integers(t, attn_in, g, int_rows, 224 + 4 * g, int_ready)
                    if g == 0:
                        step(t, v.tensor_scalar(sm(216, NS), sm(224, NS), qk_scale[:, 0:1], None, ALU.mult))
                        step(t, v.tensor_scalar(sm(220, NS), sm(216, NS), -1.0, None, ALU.mult))
                    if g == 1:
                        for s in range(NS):
                            step(t, v.tensor_scalar(row_diag[:, s, :], w["ident"][:, :], sm(228 + s, 1), None, ALU.mult),
                                 kscale_diag if s == NS - 1 else dve_chain)
                    if g == 2:
                        step(t, v.tensor_scalar(sm(232, NS), sm(232, NS), w_scale[:, 2:3], None, ALU.mult))
                dve.wait_ge(pe_k.sem, pe_k.at(t, 1))
                dve.wait_ge(kscale_ready.sem, kscale_ready.at(t, 1))
                step(t, v.tensor_tensor(k_t[:, :, :], psum[:, 2:6, :], kscale_b[:, None, :].broadcast_to([P, 4, T]), ALU.mult),
                     k_ready)
                dve.wait_ge(pe_v.sem, pe_v.at(t, 1))
                for s in range(NS):
                    at = (s % 2) * D
                    step(t, v.tensor_scalar(v_rows[:, s, :], psum[:, 2 + s // 2, at:at + D], sm(232 + s, 1), None, ALU.mult),
                         v_ready if s == NS - 1 else dve_chain)
                for n in range(NSTEP):
                    b, part = divmod(n, 3)
                    qc, half = (0, 0) if part == 0 else (1, part - 1)
                    s = b * 2 + qc
                    per, width = (4, P) if qc == 0 else (2, S)
                    dve.wait_ge(pe_logits.sem, pe_logits.at(t, n + 1))
                    at = s * NH + 8 * half
                    top = sm(448 + at, 4 * per).rearrange("p (j r) -> p r j", r=4)
                    step(t, v.tensor_reduce(out=top, in_=psum[:, 0:4, :].rearrange("p r (j k) -> p r j k", j=per),
                                            axis=AX.X, op=ALU.max))
                    step(t, v.tensor_scalar(sm(320 + at, 4 * per), sm(448 + at, 4 * per), sm(220 + s, 1), None, ALU.mult),
                         row_max)
                    if part in (0, 2):
                        dve.wait_ge(pe_heads.sem, pe_heads.at(t, n + 1))
                        step(t, v.reciprocal(sm(512 + s * NH, NH), sm(384 + s * NH, NH)))
                        step(t, v.tensor_tensor(head_out[:, s, :].rearrange("p (h d) -> p h d", h=NH),
                                                psum[:, 6 + qc, 0:D].rearrange("p (h d) -> p h d", h=NH),
                                                sm(512 + s * NH, NH)[:, :, None].broadcast_to([P, NH, HD]), ALU.mult),
                             heads_ready)
                dve.wait_ge(y_rms.sem, y_rms.at(t, 1))
                step(t, v.reciprocal(sm(208, NS), sm(204, NS)))
                to_integers(t, head_out, 3, y_rows, 236, y_int)
                step(t, v.tensor_scalar(sm(236, NS), sm(236, NS), w_scale[:, 3:4], None, ALU.mult))
                for s in range(NS):
                    step(t, v.tensor_scalar(row_diag[:, s, :], w["ident"][:, :], sm(236 + s, 1), None, ALU.mult),
                         y_diag if s == NS - 1 else dve_chain)
                dve.wait_ge(yscale_ready.sem, yscale_ready.at(t, 1))
                dve.wait_ge(pe_o.sem, pe_o.at(t, 1))
                step(t, v.tensor_tensor(f8_a[:, :, :], psum[:, 3:5, :], yscale_b[:, None, :].broadcast_to([P, DC, T]),
                                        ALU.mult))
                step(t, v.tensor_tensor(x[:, :, :], x[:, :, :], f8_a[:, :, :], ALU.add), x3_ready)

            def last_ffn(t):
                dve.wait_ge(pe_cat.sem, pe_cat.at(t, 1))
                dve.wait_ge(adapt_cols_in.sem, adapt_cols_in.at(t, 2 * BT * 16))
                for c in range(DC):
                    for b in range(BT):
                        tokens = slice(b * S, (b + 1) * S)
                        step(t, v.tensor_scalar(f8_a[:, c, tokens], psum[:, 5 + c, tokens], cat_b[:, b, c:c + 1], None,
                                                ALU.add))
                flat = [z.rearrange("p c n -> p (c n)") for z in (f8_a, f8_b, f8_q)]
                given = []

                def run(ins):
                    given.append(ins)
                    step(t, ins, f8_ready if len(given) == 5 else dve_chain)

                float8_values(run, *flat)
                dve.wait_ge(half_ready.sem, half_ready.at(t, 1))
                dve.wait_ge(out_stored.sem, out_stored.at(t, 0))
                for c in range(DC):
                    step(t, v.scalar_tensor_tensor(out_t[:, c, :], half_t[:, c, :], col("fbias", c), x[:, c, :],
                                                   ALU.add, ALU.add), out_ready if c == DC - 1 else dve_chain)

            with dve.Fori(0, TILES) as t:
                condition(t)
                scan_attention(t)
                pool_prompt(t)
                experts(t)
                adapter(t)
                attention(t)
                last_ffn(t)

        @block.tensor
        def _(pe):
            mm = nc.tensor.matmul

            def add_up(dst, pairs):
                for k, (lhs, rhs) in enumerate(pairs):
                    ins = mm(dst, lhs, rhs, start=k == 0, stop=k == len(pairs) - 1)
                return ins

            dve_sums = setup_dve
            pe.wait_ge(dve_sums.sem, DVE_SUMS)
            pe.wait_ge(loads["early"].sem, 16 * N_EARLY)
            mm(psum[:, 0, 0:4], w["ones"][:, 0:1].broadcast_to([P, P]), sm(44, 4), start=True, stop=True).then_inc(setup_pe.sem, 1)
            pe.wait_ge(setup_dve.sem, DVE_SUMS + 1)

            def condition(t):
                pe.wait_ge(x_in.sem, x_in.at(t, 16))
                pe.wait_ge(out_ready.sem, out_ready.at(t, 0))
                add_up(psum[0:HID, 0, :], [(w["w_n1"][:, c, :], x[:, c, :]) for c in range(DC)])
                for e in range(DC):
                    ins = add_up(psum[:, 1 + e, :], [(w["w_soma"][:, c, e * P:(e + 1) * P], x[:, c, :]) for c in range(DC)])
                ins.then_inc(pe_soma.sem, 1)
                pe.wait_ge(ctx_ready.sem, ctx_ready.at(t, 1))
                for e in range(DC):
                    cols = slice(e * P, (e + 1) * P)
                    if e == 1:
                        pe.wait_ge(h1_ready.sem, h1_ready.at(t, 1))
                    ins = add_up(psum[:, 3 + e, :], [(w["w_g"][:, c, cols], x[:, c, :]) for c in range(DC)]
                                 + [(w["w_g"][:, DC + c, cols], ctx_t[:, c, :]) for c in range(DC)])
                ins.then_inc(pe_gate.sem, 1)
                mm(psum[0:ND, 5, :], w["w_n2"][:, :], h1, start=True, stop=True).then_inc(pe_mod.sem, 1)
                pe.wait_ge(mod_ready.sem, mod_ready.at(t, 1))

                def mod_rows(d):
                    mm(psum[:, 6 + d % 2, :], w["ident"][0:ND, d:d + 1].broadcast_to([ND, P]), mod,
                       start=True, stop=True).then_inc(pe_mod_rows.sem, 1)

                mod_rows(0)
                mod_rows(1)
                pe.wait_ge(soma_ready.sem, soma_ready.at(t, 1))
                for d in range(ND):
                    pe.wait_ge(trace_ready.sem, trace_ready.at(t, d + 1))
                    for c in range(DC):
                        ins = mm(psum[:, c, :], w["ident"][:, :], trace[d % 2][:, c, :], start=d == 0, stop=d == ND - 1,
                                 skip_group_check=True)
                    ins.then_inc(pe_trace_used.sem, 1)
                    if d + 2 < ND:
                        mod_rows(d + 2)
                pe.wait_ge(temporal_ready.sem, temporal_ready.at(t, 1))
                for e in range(DC):
                    ins = add_up(psum[:, 2 + e, :],
                                 [(w["w_temp"][:, c, e * P:(e + 1) * P], temporal[:, c, :]) for c in range(DC)])
                ins.then_inc(pe_temp.sem, 1)
                pe.wait_ge(mixed_ready.sem, mixed_ready.at(t, 1))
                for s in range(NS):
                    ins = add_up(psum[:, 4 + s // 2, (s % 2) * D:(s % 2 + 1) * D],
                                 [(gate_t[:, c, s * P:(s + 1) * P], w["w_out"][:, c, :]) for c in range(DC)])
                ins.then_inc(pe_cond.sem, 1)
                pe.wait_ge(cond_norm.sem, cond_norm.at(t, 1))
                for c in range(DC):
                    for s in range(NS):
                        ins = nc.tensor.transpose(psum[:, 6 + c, s * P:(s + 1) * P], cond_rows[:, s, c * P:(c + 1) * P],
                                                  w["ident"][:, :])
                ins.then_inc(pe_cond_t.sem, 1)

            def scan_attention(t):
                def z_part(bank, at, width):
                    add_up(psum[0:width, bank, :], [(w["w_in"][:, c, at:at + width], cond[:, c, :]) for c in range(DC)]) \
                        .then_inc(pe_z.sem, 1)

                def head_rows(bank, c, src):
                    sel = w["head_sel"][:, c, :]
                    return mm(psum[:, bank, :], sel, src, start=True, stop=True)

                pe.wait_ge(cond_ready.sem, cond_ready.at(t, 1))
                z_part(0, 2 * INNER, HEADS_B)
                z_part(1, 0, P)
                z_part(2, INNER, P)
                for c in range(IC):
                    if c == 0:
                        pe.wait_ge(p_ready.sem, p_ready.at(t, 1))
                    head_rows(3, c, p_t)
                    head_rows(4, c, inv_den).then_inc(pe_p_rows.sem, 1)
                    if c + 1 < IC:
                        pe.wait_ge(z_copied.sem, z_copied.at(t, 3 + 2 * c))
                        z_part(1, (c + 1) * P, P)
                        z_part(2, INNER + (c + 1) * P, P)
                    pe.wait_ge(mean_ready.sem, mean_ready.at(t, c + 1))
                    add_up(psum[:, 5, :], [(w["w_re"][:, :], mean_re), (w["w_im"][:, :], mean_im)]) \
                        .then_inc(pe_y.sem, 1)
                    pe.wait_ge(sq_ready.sem, sq_ready.at(t, c + 1))
                    for k, part in enumerate((cos_t, sin_t)):
                        ins = mm(psum[0:HEADS_B, 6, :], w["head_sum"][:, c, :], part, start=c == 0 and k == 0,
                                 stop=c == IC - 1 and k == 1, skip_group_check=True)
                    ins.then_inc(pe_sq.sem, 1)
                    pe.wait_ge(yg_ready.sem, yg_ready.at(t, c + 1))
                pe.wait_ge(rms_ready.sem, rms_ready.at(t, 1))
                for c in range(IC):
                    ins = head_rows(1 + c, c, rms_b)
                ins.then_inc(pe_rms_rows.sem, 1)
                pe.wait_ge(ynorm_ready.sem, ynorm_ready.at(t, 1))
                for e, bank in ((0, 0), (1, 5)):
                    ins = add_up(psum[:, bank, :], [(w["w_proj"][:, c, e * P:(e + 1) * P], yg[:, c, :]) for c in range(IC)])
                ins.then_inc(pe_proj.sem, 1)

            def pool_prompt(t):
                pe.wait_ge(x1_ready.sem, x1_ready.at(t, 1))
                for s in range(NS):
                    for c in range(DC):
                        at = (s % 2) * D + c * P
                        ins = nc.tensor.transpose(psum[:, 1 + s // 2, at:at + P], x[:, c, s * P:(s + 1) * P],
                                                  w["ident"][:, :])
                ins.then_inc(pe_x1_rows.sem, 1)
                add_up(psum[0:HID, 3, :], [(w["w_1"][:, c, :], x[:, c, :]) for c in range(DC)]) \
                    .then_inc(pe_score_hid.sem, 1)
                pe.wait_ge(score_hid.sem, score_hid.at(t, 1))
                mm(psum[:, 4, :], w["v_col"][:, 0:1].broadcast_to([HID, P]), score_h, start=True, stop=True).then_inc(pe_score.sem, 1)
                pe.wait_ge(pool_p.sem, pool_p.at(t, 1))
                for b in range(BT):
                    for l in range(2):
                        for j in range(2):
                            at = l * S + j * P
                            ins = nc.tensor.transpose(psum[:, 5 + b, at:at + P],
                                                      pool_w[:, 2 * b + j, l * P:(l + 1) * P], w["ident"][:, :])
                ins.then_inc(pe_pool_t.sem, 1)
                pe.wait_ge(pool_t.sem, pool_t.at(t, 1))
                for c, bank in ((0, 7), (1, 1)):
                    for b in range(BT):
                        ins = add_up(psum[:, bank, b * S:(b + 1) * S],
                                     [(x1_rows[:, 2 * b + l, c * P:(c + 1) * P], pool_wt[:, b, l * S:(l + 1) * S])
                                      for l in range(2)])
                ins.then_inc(pe_pool.sem, 1)

            def experts(t):
                pe.wait_ge(pool_ready.sem, pool_ready.at(t, 1))
                for s in range(NS):
                    ins = add_up(psum[:, 0, s * NE:(s + 1) * NE],
                                 [(pooled[:, c, s * P:(s + 1) * P], w["w_route"][:, c, :]) for c in range(DC)])
                ins.then_inc(pe_route.sem, 1)
                pe.wait_ge(share_ready.sem, share_ready.at(t, 1))
                for s in range(NS):
                    ins = nc.tensor.transpose(psum[0:NE, 1, s * P:(s + 1) * P],
                                              small[:, 256 + s * NE:256 + (s + 1) * NE], w["ident"][:, :])
                ins.then_inc(pe_share_t.sem, 1)
                pe.wait_ge(share_t.sem, share_t.at(t, 1))

                def share_rows_of(e):
                    if e:
                        pe.wait_ge(share_rows.sem, share_rows.at(t, e))
                    mm(psum[:, 2, :], w["ident"][0:NE, e:e + 1].broadcast_to([NE, P]), share_tt, start=True, stop=True) \
                        .then_inc(pe_share_rows.sem, 1)

                def down(e):
                    pe.wait_ge(g_ready.sem, g_ready.at(t, (e + 1) * FC))
                    for c, bank in ((0, 0), (1, 7)):
                        for m in range(FC):
                            ins = mm(psum[:, bank, :], down_weight(e, m, c), g_buf[e % 2][:, m, :],
                                     start=e == 0 and m == 0, stop=e == EXPERTS - 1 and m == FC - 1, skip_group_check=True)
                    ins.then_inc(pe_down.sem, 1)

                pe.wait_ge(expert_in.sem, EXPERTS * 16)
                share_rows_of(0)
                for e in range(EXPERTS):
                    if e + 1 < NE:
                        share_rows_of(e + 1)
                    for m in range(FC):
                        n = e * FC + m
                        if n >= 2:
                            pe.wait_ge(h_read.sem, h_read.at(t, n - 1))
                        add_up(psum[:, 3 + n % 2, :], [(up_weight(e, 0, c, m), pooled[:, c, :]) for c in range(DC)])
                        if n >= 2:
                            pe.wait_ge(g_ready.sem, g_ready.at(t, n - 1))
                        if e < NE and m == 0:
                            pe.wait_ge(xw_ready.sem, xw_ready.at(t, e + 1))
                        src = xw[e % 2] if e < NE else pooled
                        add_up(psum[:, 5 + n % 2, :], [(up_weight(e, 1, c, m), src[:, c, :]) for c in range(DC)]) \
                            .then_inc(pe_up.sem, 1)
                    if e:
                        down(e - 1)
                down(EXPERTS - 1)

            def adapter(t):
                pe.wait_ge(x2_ready.sem, x2_ready.at(t, 1))
                pe.wait_ge(adapt_in.sem, adapt_in.at(t, 2 * BT * 16))
                pe.wait_ge(adapt_rows_in.sem, adapt_rows_in.at(t, 3 * BT * 16))
                for b in range(BT):
                    tokens = slice(b * S, (b + 1) * S)
                    ins = add_up(psum[:, 1, tokens], [(adapt_down[:, b, c, :], x[:, c, tokens]) for c in range(DC)])
                ins.then_inc(pe_bottle.sem, 1)
                pe.wait_ge(bottle_ready.sem, bottle_ready.at(t, 1))
                for s in range(NS):
                    b, at = s // 2, (s % 2) * D
                    tokens = slice(s * P, (s + 1) * P)
                    dst = psum[:, 2 + s // 2, at:at + D]
                    for c in range(DC):
                        mm(dst[:, c * P:(c + 1) * P], x[:, c, tokens], w["ident"][:, :], start=c == 0, stop=False,
                           skip_group_check=True)
                    mm(dst, w["ones"][32:33, 0:1].broadcast_to([1, P]), adapt_bu[:, b, :], start=False, stop=False,
                       skip_group_check=True)
                    ins = mm(dst, bottle[:, tokens], adapt_up[:, b, :], start=False, stop=True, skip_group_check=True)
                ins.then_inc(pe_adapt.sem, 1)

            def integers_t(rows, dst_bank=0):
                for c in range(DC):
                    for s in range(NS):
                        ins = nc.tensor.transpose(psum_b[:, dst_bank + c, s * P:(s + 1) * P],
                                                  rows[:, s, c * P:(c + 1) * P], ident_b[:, :])
                return ins

            def attention(t):
                for g in range(3):
                    pe.wait_ge(int_ready.sem, int_ready.at(t, g + 1))
                    if g:
                        pe.wait_ge(int_t.sem, int_t.at(t, g))
                    integers_t(int_rows).then_inc(pe_int_t.sem, 1)
                    if g == 0:
                        pe.wait_ge(int_t.sem, int_t.at(t, 1))
                    if g == 1:
                        pe.wait_ge(q_ready.sem, q_ready.at(t, 1))
                        pe.wait_ge(int_t.sem, int_t.at(t, 2))
                    if g < 2:
                        for k in range(4):
                            ins = add_up(psum[:, 2 + k, :], [(tern_qk[:, g, c, k * P:(k + 1) * P], int_tt[:, c, :])
                                                             for c in range(DC)])
                        ins.then_inc((pe_q, pe_k)[g].sem, 1)
                    else:
                        pe.wait_ge(int_t.sem, int_t.at(t, 3))
                        pe.wait_ge(k_ready.sem, k_ready.at(t, 1))
                        for s in range(NS):
                            ins = add_up(psum[:, 2 + s // 2, (s % 2) * D:(s % 2 + 1) * D],
                                         [(int_tt[:, c, s * P:(s + 1) * P], tern_vo[:, 0, c, :]) for c in range(DC)])
                        ins.then_inc(pe_v.sem, 1)
                    if g == 1:
                        pe.wait_ge(kscale_diag.sem, kscale_diag.at(t, 1))
                        mm(psum[:, 6, :], w["ones"][:, 0:1].broadcast_to([P, P]), row_diag.rearrange("p s q -> p (s q)"), start=True, stop=True) \
                            .then_inc(pe_kscale.sem, 1)
                pe.wait_ge(v_ready.sem, v_ready.at(t, 1))
                for n in range(NSTEP):
                    b, part = divmod(n, 3)
                    qc, half = (0, 0) if part == 0 else (1, part - 1)
                    s = b * 2 + qc
                    per, width = (4, P) if qc == 0 else (2, S)
                    if n:
                        pe.wait_ge(probs_ready.sem, probs_ready.at(t, n))
                    for r in range(4):
                        blocks = psum[:, r, :].rearrange("p (j k) -> p j k", j=per)[:, :, width - P:]
                        mm(blocks, ident_b[:, :], causal_a[:, 0:per * P].rearrange("p (j k) -> p j k", j=per),
                           start=True, stop=False, skip_group_check=True)
                    for j in range(per):
                        for r in range(4):
                            k = half * 2 + j
                            rows = slice(32 * r, 32 * r + 32)
                            ins = mm(psum[:, r, j * width:(j + 1) * width], q_t[rows, k, s * P:(s + 1) * P],
                                     k_t[rows, k, b * S:b * S + width], start=False, stop=j == per - 1,
                                     skip_group_check=True)
                    ins.then_inc(pe_logits.sem, 1)
                    pe.wait_ge(probs_ready.sem, probs_ready.at(t, n + 1))

                    def weighted(r):
                        i = 4 * n + r
                        pe.wait_ge(probs_t.sem, probs_t.at(t, i + 1))
                        for j in range(per):
                            head = 4 * (half * 2 + j) + r
                            if qc == 0 and b and j == 0 and r == 0 or qc and part == 1 and b and j == 0 and r == 0:
                                pe.wait_ge(heads_ready.sem, heads_ready.at(t, 1 if qc == 0 else 2))
                            for kc in range(width // P):
                                at = j * width + kc * P
                                ins = mm(psum[:, 6 + qc, head * HD:(head + 1) * HD], probs_tt[i % 2][:, at:at + P],
                                         v_rows[:, 2 * b + kc, head * HD:(head + 1) * HD], start=kc == 0,
                                         stop=kc == width // P - 1)
                        return ins

                    for r in range(4):
                        i = 4 * n + r
                        if i >= 2:
                            pe.wait_ge(probs_t.sem, probs_t.at(t, i - 1))
                        for k in range(4):
                            ins = nc.tensor.transpose(psum[:, 4 + i % 2, k * P:(k + 1) * P],
                                                      probs[:, r * T + k * P:r * T + (k + 1) * P], w["ident"][:, :])
                        ins.then_inc(pe_probs_t.sem, 1)
                        if r:
                            weighted(r - 1)
                    weighted(3).then_inc(pe_heads.sem, 1)
                pe.wait_ge(y_int.sem, y_int.at(t, 1))
                integers_t(y_rows).then_inc(pe_yint_t.sem, 1)
                pe.wait_ge(y_diag.sem, y_diag.at(t, 1))
                mm(psum[:, 2, :], w["ones"][:, 0:1].broadcast_to([P, P]), row_diag.rearrange("p s q -> p (s q)"), start=True, stop=True) \
                    .then_inc(pe_yscale.sem, 1)
                pe.wait_ge(yint_t.sem, yint_t.at(t, 1))
                for e in range(DC):
                    ins = add_up(psum[:, 3 + e, :], [(tern_vo[:, 1, c, e * P:(e + 1) * P], y_tt[:, c, :]) for c in range(DC)])
                ins.then_inc(pe_o.sem, 1)

            def last_ffn(t):
                pe.wait_ge(x3_ready.sem, x3_ready.at(t, 1))
                pe.wait_ge(cat_in.sem, cat_in.at(t, BT * 16))
                for e in range(DC):
                    for b in range(BT):
                        tokens = slice(b * S, (b + 1) * S)
                        ins = add_up(psum[:, 5 + e, tokens],
                                     [(cat_w[:, b, c, e * P:(e + 1) * P], x[:, c, tokens]) for c in range(DC)])
                ins.then_inc(pe_cat.sem, 1)
                pe.wait_ge(f8_ready.sem, f8_ready.at(t, 1))
                for e in range(DC):
                    ins = add_up(psum[:, 4 + e, :], [(f8_w[:, c, e * P:(e + 1) * P], f8_q[:, c, :]) for c in range(DC)])
                ins.then_inc(pe_f8.sem, 1)

            with pe.Fori(0, TILES) as t:
                condition(t)
                scan_attention(t)
                pool_prompt(t)
                experts(t)
                adapter(t)
                attention(t)
                last_ffn(t)

        for name, s in signals:
            if s in (dve_chain, act_chain) or s.given:
                assert s.per_tile in (0, s.given), (name, s.per_tile, s.given)


def setup_arrays(inputs):
    f = {n: np.asarray(a) for n, a in inputs.items()}

    def rows(a, k):
        return a.reshape(k, P, -1).transpose(1, 0, 2)

    def lhs(a, k):
        return rows(a.T, k)

    vecs = np.zeros((P, NVEC), np.float32)

    def put(name, a):
        at, n = VEC[name]
        a = np.asarray(a)
        vecs[:a.shape[0], at:at + n] = a.reshape(a.shape[0], n)

    def chunk_cols(a, k):
        return a.reshape(k, P).T

    put("tau", np.broadcast_to(np.concatenate([f["L0_cond_tau_ctx"].reshape(1), f["condB_tauraws"]]), (P, 1 + ND)))
    put("deriv", np.broadcast_to(f["L0_attn_deriv_logits"], (P, 3)))
    for name, key in (("bg", "bg"), ("btemp", "btemp"), ("bsoma", "bsoma"), ("gamma", "gamma"), ("beta", "beta")):
        put(name, chunk_cols(f["L0_cond_" + key], DC))
    put("bn1", f["L0_cond_bn1"].reshape(HID, 1))
    put("bn2", f["condB_bn2"].reshape(ND, 1))
    put("blend", f["cond_1024"].reshape(ND, DC, P).transpose(2, 1, 0))
    taps = np.zeros((TAPS, 9 * P), np.float32)
    taps[:, :C_IN] = f["L0_attn_conv_k"][:, 0, :]
    put("conv_k", taps.reshape(TAPS, 9, P).transpose(2, 1, 0))
    cb = np.zeros(9 * P, np.float32)
    cb[:C_IN] = f["L0_attn_conv_b"]
    put("conv_b", chunk_cols(cb, 9))
    put("theta", chunk_cols(f["L0_attn_theta"].reshape(-1), IC))
    put("slope", np.concatenate([f["L0_attn_decay_slopes"], f["L0_attn_anchor_slopes"]]).reshape(-1, 1))
    put("score_scale", f["L0_attn_score_scale"].reshape(-1, 1))
    put("norm_re", np.tile(f["L0_attn_norm_scale"][:HD_B], P // HD_B).reshape(-1, 1))
    put("norm_im", np.tile(f["L0_attn_norm_scale"][HD_B:], P // HD_B).reshape(-1, 1))
    put("b1", f["L0_cond2_b1"].reshape(-1, 1))
    put("fbias", chunk_cols(f["L1_ffn_bias"], DC))
    for name, value in (("eps5", 1e-5), ("eps6", 1e-6), ("half_pi", np.pi / 2), ("zero", 0.0)):
        put(name, np.full((P, 1), value, np.float32))

    def block_diagonal(a):
        out = np.zeros((P, P), np.float32)
        for k in range(P // HD_B):
            out[k * HD_B:(k + 1) * HD_B, k * HD_B:(k + 1) * HD_B] = a
        return out

    x = f["x"].reshape(TILES, T, DC, P).transpose(0, 3, 2, 1)
    a = {
        "x_t": x, "vecs": vecs,
        "w_g": lhs(f["L0_cond_Wg"], 2 * DC), "w_n1": lhs(f["L0_cond_Wn1"], DC), "w_n2": f["cond_256"].T,
        "w_soma": lhs(f["L0_cond_Wsoma"], DC), "w_temp": lhs(f["L0_cond_Wtemp"], DC),
        "w_out": lhs(f["L0_cond_Wout"], DC), "w_in": rows(f["L0_attn_in_proj_w"], DC),
        "w_re": block_diagonal(f["L0_attn_W_re"]), "w_im": block_diagonal(f["L0_attn_W_im"]),
        "w_proj": rows(f["L0_attn_out_proj_w"], IC), "w_1": rows(f["L0_cond2_W1"], DC),
        "v_col": f["L0_cond2_v"].reshape(HID, 1),
        "w_route": rows(f["L0_ffn_gate_w"], DC),
        "qkvo": np.stack([lhs(f["L1_attn_" + n], DC) for n in ("wq", "wk", "wv", "wo")], 1),
        "w_f8": lhs(f["L1_ffn_weight"], DC),
        "g_rows": np.broadcast_to(np.stack([f["L1_attn_" + n] for n in ("gq", "gk", "gv", "go")]), (P, 4, D)),
        "ids_row": np.concatenate([f["itok_B_0_6"], f["itok_B_0_63"]]).reshape(1, 2 * B),
        "kind_ids": np.broadcast_to(f["itok_B_0_2"], (P, B)),
        "down_w": f["L1_cond_down_w"].reshape(8, DC, P, P).transpose(0, 2, 1, 3),
        "down_b": f["L1_cond_down_b"].reshape(8, P, 1),
        "up_w": f["L1_cond_up_w"], "up_b": f["L1_cond_up_b"].reshape(8, 1, D),
        "ln_g": f["L1_cond_ln_g"].reshape(8, 1, D), "ln_b": f["L1_cond_ln_b"].reshape(8, 1, D),
        "cat_w": f["L1_cond2_W"].reshape(64, DC, P, D).transpose(0, 2, 1, 3),
        "cat_b": f["L1_cond2_b"].reshape(64, DC, P).transpose(0, 2, 1),
    }
    up = np.stack([np.concatenate([f["L0_ffn_ew1"], f["L0_ffn_sw1"][None]]),
                   np.concatenate([f["L0_ffn_ew2"], f["L0_ffn_sw2"][None]])], 1)
    up = up.reshape(EXPERTS, 2, DC, P, FF).transpose(0, 3, 1, 2, 4).reshape(EXPERTS, P, -1)
    down = np.concatenate([f["L0_ffn_ew3"], f["L0_ffn_sw3"][None]])
    down = down.reshape(EXPERTS, FC, P, D).transpose(0, 2, 1, 3).reshape(EXPERTS, P, -1)
    a["expert_w"] = np.concatenate([up, down], 2)

    a["ident"] = np.eye(P, dtype=np.float32)
    a["ones"] = np.ones((P, 1), np.float32)
    head = np.arange(INNER) // HD_B
    sel = (np.arange(HEADS_B)[:, None] == head[None, :]).astype(np.float32)
    a["head_sel"] = sel.reshape(HEADS_B, IC, P)
    a["head_sum"] = sel.T.reshape(IC, P, HEADS_B).transpose(1, 0, 2) / np.float32(2 * HD_B)
    j, l = np.arange(S)[:, None], np.arange(S)[None, :]
    mask = np.stack([np.where(m, 0.0, NEG) for m in (l <= j, l >= j, l != j)]).astype(np.float32)
    a["pool_mask"] = mask.reshape(3, 2, P, S).transpose(2, 0, 1, 3)
    count = np.stack([np.arange(S) + 1, S - np.arange(S), np.full(S, S - 1)]).astype(np.float32)
    a["pool_count"] = count.reshape(3, 2, P).transpose(2, 0, 1)
    pos = np.arange(S, dtype=np.float32)
    a["dist"] = np.where(np.arange(HEADS_B)[:, None] < HEADS_B - 4, S - 1 - pos, pos).astype(np.float32)
    q, k = np.arange(P)[:, None], np.arange(P)[None, :]
    a["causal"] = np.where(k <= q, 0.0, NEG).astype(np.float32)
    a["expert_no"] = np.broadcast_to(np.arange(NE, dtype=np.float32), (P, NS, NE))
    return {n: np.ascontiguousarray(v) for n, v in a.items()}


def kernel(**inputs):
    import concourse.bacc as bacc
    from concourse.bass_utils import run_bass_kernel_spmd

    nc = bacc.Bacc("TRN2", target_bir_lowering=False, num_devices=1)
    arrays = setup_arrays(inputs)
    dram = {n: nc.dram_tensor("in_" + n, a.shape, mybir.dt.from_np(a.dtype), kind="ExternalInput").ap()
            for n, a in arrays.items()}
    out = nc.dram_tensor("out_t", (TILES, P, DC, T), F32, kind="ExternalOutput").ap()
    adaln_attention_ffn(nc, dram, out)
    r = run_bass_kernel_spmd(nc, [{"in_" + n: a for n, a in arrays.items()}], core_ids=[0])
    y = np.asarray(r.results[0]["out_t"])
    return y.transpose(0, 3, 2, 1).reshape(B, S, D)
```

```python
from contextlib import ExitStack

import concourse.bass as bass
import numpy as np
from concourse import mybir

F32 = mybir.dt.float32
BF16 = mybir.dt.bfloat16
F16 = mybir.dt.float16
I32 = mybir.dt.int32
ACT = mybir.ActivationFunctionType
ALU = mybir.AluOpType
AX = mybir.AxisListType

P = 128
B, S, D = 8, 256, 256
BT = 2
T = BT * S
TILES = B // BT
NS = T // P
DC = D // P
ND = 8
HID = 64
HEADS_B, HD_B = 32, 16
INNER = HEADS_B * HD_B
IC = INNER // P
C_IN = 2 * INNER + HEADS_B
TAPS = 4
NE, FF = 8, 512
EXPERTS = NE + 1
FC = FF // P
BLOCKS = TILES * NS
SLOTS = 2 * BLOCKS + NE
SLOT_PAIRS = SLOTS // 2
NH, HD = 16, 16
MAGIC = 12582912.0
TWO_PI = 6.283185307179586
TWO_PI_HI = 6.28125
TWO_PI_LO = TWO_PI - TWO_PI_HI
PI_SAFE = 3.1415925
NEG = -1e30

VEC_COLS = [("tau", 1 + ND), ("deriv", 3), ("bg", DC), ("btemp", DC), ("bsoma", DC), ("gamma", DC), ("beta", DC),
            ("bn1", 1), ("bn2", 1), ("blend", DC * ND), ("conv_k", TAPS * 9), ("conv_b", 9), ("theta", IC),
            ("slope", 1), ("score_scale", 1), ("norm_re", 1), ("norm_im", 1), ("b1", 1), ("fbias", DC),
            ("eps5", 1), ("eps6", 1), ("half_pi", 1), ("zero", 1)]
VEC = {}
_at = 0
for _name, _n in VEC_COLS:
    VEC[_name] = (_at, _n)
    _at += _n
NVEC = _at

WEIGHTS = {
    "w_g": (P, (2 * DC, D)), "w_n1": (P, (DC, HID)), "w_n2": (HID, (ND,)), "w_soma": (P, (DC, D)),
    "w_temp": (P, (DC, D)), "w_out": (P, (DC, D)), "w_in": (P, (DC, C_IN)), "w_re": (P, (P,)), "w_im": (P, (P,)),
    "w_proj": (P, (IC, D)), "w_1": (P, (DC, HID)), "v_col": (HID, (1,)), "w_route": (P, (DC, NE)),
    
}
CONSTS = {
    "ident": (P, (P,)), "ones": (P, (1,)), "head_sum": (P, (IC, HEADS_B)),
    "pool_count": (P, (3, 2)), "dist": (HEADS_B, (S,)), "head_sel": (HEADS_B, (IC, P)),
    "causal": (P, (P,)), "expert_no": (P, (NS, NE)),
}


EARLY = ["ident", "ones", "w_n1", "w_soma", "w_g", "w_n2", "dist", "w_temp", "w_out"]
MID = ["w_in", "head_sel", "head_sum", "w_re", "w_im", "w_proj", "w_1", "v_col", "pool_count", "w_route",
       "expert_no"]
N_EARLY, N_MID = len(EARLY) + 1, len(MID) + 1
DVE_MAXIMA, DVE_SLOPES, DVE_SUMS = 4, 22, 43
ORDER_STEPS = 24
CHAIN = {"dve_1": 350, "act_1": 56, "dve_3": 212, "act_3": 98}
PAIRS = TILES // 2


class Signal:

    def __init__(self, sem, per_tile, before):
        self.sem, self.per_tile, self.before, self.given = sem, per_tile, before, 0

    def at(self, t, k, u=None):
        if u is None:
            return t * self.per_tile + (self.before + k)
        return t * (2 * self.per_tile) + (self.before + 2 * (k - 1) + u + 1)


def adaln_attention_ffn(nc, dram, out):
    with ExitStack() as ctx:
        def sb(name, shape, dt=F32):
            return ctx.enter_context(nc.sbuf_tensor(name, shape, dt))

        signals = []

        def signal(name, per_tile=1, before=0):
            signals.append((name, Signal(ctx.enter_context(nc.semaphore(name)), per_tile, before)))
            return signals[-1][1]

        def further(last, n, per_tile):
            signals.append((signals[0][0], Signal(last.sem, per_tile, last.before + n * last.per_tile)))
            return signals[-1][1]

        w = {n: sb(n, [p, *shape]) for n, (p, shape) in (WEIGHTS | CONSTS).items()}
        vecs = sb("vecs", [P, NVEC])

        def col(name, k=0, p=P):
            at = VEC[name][0] + k
            return vecs[0:p, at:at + 1]

        expert_w = sb("expert_w", [P, EXPERTS, 2 * DC * FF + FC * D])

        def up_weight(which, c, m):
            at = (which * DC + c) * FF + m * P
            return expert_w[:, 0, at:at + P]

        def down_weight(m, c):
            at = 2 * DC * FF + m * D + c * P
            return expert_w[:, 0, at:at + P]

        def routed_weight(e, at, n):
            return expert_w[:, bass.ds(e, 1), at:at + n].rearrange("p e n -> p (e n)")

        ids_row = sb("ids_row", [1, 2 * B], I32)
        kind_ids = sb("kind_ids", [P, B], I32)

        decay = sb("decay", [P, 1 + ND])
        blend = sb("blend", [P, DC, ND])
        deriv = sb("deriv_w", [P, 4])
        half_b = sb("half_b", [P, 2 * DC + 1])
        slope = sb("slope_sb", [HEADS_B, 1])
        time_w = w["dist"]
        pool_mask = sb("pool_mask", [P, 3, 2, S], BF16)
        tern_qk = sb("tern_qk", [P, 2, DC, 4 * P], BF16)
        tern_vo = sb("tern_vo", [P, 2, DC, D], BF16)
        w_scale = sb("w_scale", [P, 8])
        qk_scale = sb("qk_scale", [P, 1])
        f8_w = sb("f8_w", [P, DC, D], BF16)
        ident_b = sb("ident_b", [P, P], BF16)
        causal_a = sb("causal_a", [P, 4 * P], BF16)
        kind = sb("kind", [P, B, 3])
        picks = sb("picks", [P, 2, BLOCKS, NE])
        shares = sb("shares", [P, 2, BLOCKS])
        slots = sb("slots", [P, 2, BLOCKS], I32)
        slots_now = [sb("slots_now_a", [P, 2, NS], I32), sb("slots_now_b", [P, 2, NS], I32)]
        slot_expert = sb("slot_expert", [1, SLOTS], I32)
        smalls = [sb("small_a", [P, 640]), sb("small_b", [P, 640])]

        UNITS = 22
        arena_a = sb("arena", [P, UNITS * T])
        spare = expert_w[:, :, :].rearrange("p e n -> p (e n)")
        EXPERT = 2 * DC * FF + FC * D
        arena_b = spare[:, 5 * EXPERT:5 * EXPERT + UNITS * T]

        class Stream:

            def __init__(self, u, arena):
                def unit(a, n=1, p=P):
                    return arena[0:p, a * T:(a + n) * T]

                def chunks(a, n, units=None):
                    return unit(a, units or n).rearrange("p (c n) -> p c n", c=n)

                def rows(a, n=2):
                    return unit(a, n).rearrange("p (s d) -> p s d", s=NS)

                self.unit, self.chunk, self.rows = unit, chunks, rows
                self.small, self.bank0 = smalls[u], 4 * u
                self.stat = smalls[u][:, 24:32].rearrange("p (s k) -> p s k", k=2)
                self.stat_mean, self.stat_var = self.stat[:, :, 0], self.stat[:, :, 1]
                self.x = chunks(0, 2)
                self.ctx_t, self.gated = chunks(2, 2), chunks(4, 2)
                self.scaled = [chunks(6, 2), chunks(8, 2)]
                self.trace = [chunks(10, 2), chunks(12, 2)]
                self.gate_t, self.soma = chunks(14, 2), chunks(16, 2)
                self.mod, self.h1 = unit(18, 1, ND), unit(19, 1, HID)
                self.temporal, self.cond_rows = chunks(2, 2), rows(4)
                self.cond = chunks(20, 2)
                self.conv = [unit(2), unit(3)]
                self.p_t, self.inv_den = unit(4, 1, HEADS_B), unit(5, 1, HEADS_B)
                self.phi, self.turns, self.angle, self.sin_t, self.cos_t, self.mean_re, self.mean_im = \
                    (unit(6 + k) for k in range(7))
                self.gtanh, self.gate_s, self.yg = unit(13), unit(14), chunks(15, 4)
                self.rms_b = unit(19, 1, HEADS_B)
                self.zpad = zpads[u]
                self.score_h = unit(2, 1, HID)
                self.masked = unit(3, 2).rearrange("p (g l) -> p g l", g=4)
                self.pool_w = unit(5, 2).rearrange("p (g l) -> p g l", g=4)
                self.pool_wt = unit(7, 2).rearrange("p (b n) -> p b n", b=BT)
                self.x1_rows, self.pooled, self.pooled_rows = rows(9), chunks(20, 2), rows(11)
                self.picked = [rows(5), rows(7)]
                self.bottle, self.adapt_y = unit(2), rows(3)
                self.attn_in, self.scaled_in = rows(5), rows(7)
                self.int_rows = unit(9).bitcast(BF16).rearrange("p (s d) -> p s d", s=NS)
                self.int_tt = unit(10).bitcast(BF16).rearrange("p (c n) -> p c n", c=DC)
                self.q_t, self.k_t, self.v_rows = chunks(11, 4), chunks(15, 4), rows(19)
                self.row_diag = unit(21).rearrange("p (s q) -> p s q", s=NS)
                self.kscale_b = unit(3)
                self.probs, self.probs_tt = [unit(2), unit(4)], [unit(7), unit(8)]
                self.head_out, self.yscale_b = rows(9), unit(3)
                self.y_rows = unit(11).bitcast(BF16).rearrange("p (s d) -> p s d", s=NS)
                self.y_tt = unit(12).bitcast(BF16).rearrange("p (c n) -> p c n", c=DC)
                self.f8_t, self.f8_a, self.f8_b = chunks(4, 2), chunks(6, 2), chunks(8, 2)
                self.f8_q = unit(15).bitcast(BF16).rearrange("p (c n) -> p c n", c=DC)
                self.half_t = unit(13).bitcast(F16).rearrange("p (c n) -> p c n", c=DC)
                self.out_t = chunks(16, 2)
                own = spare[:, (1 + 6 * u) * 1024:(7 + 6 * u) * 1024]

                def part(at, n, pattern, **sizes):
                    return own[:, at:at + n].rearrange(pattern, **sizes)

                self.adapt_down = part(0, 512, "p (b c n) -> p b c n", b=BT, c=DC)
                self.adapt_up = part(512, 512, "p (b n) -> p b n", b=BT)
                self.adapt_rows = part(1024, 1024, "p (g b d) -> p g b d", g=2, b=BT)
                self.cat_w = part(2048, 1024, "p (b c n) -> p b c n", b=BT, c=DC)
                self.adapt_bu = own[0:1, 3072:3584].rearrange("p (b d) -> p b d", b=BT)
                self.adapt_bd = own[:, 3584:3584 + BT]
                self.cat_b = own[:, 3586:3586 + BT * DC].rearrange("p (b c) -> p b c", b=BT)

            def sm(self, at, n, p=P):
                return self.small[0:p, at:at + n]

            def bank(self, k, n=1, p=P):
                b = self.bank0 + k
                return psum[0:p, b, :] if n == 1 else psum[0:p, b:b + n, :]

            def bank_b(self, k, n):
                return psum_b[:, self.bank0 + k:self.bank0 + k + n, 0:T]

            def token_banks(self, k):
                return self.bank(k, 2).rearrange("p a (k d) -> p (a k) d", k=2)

        zpads = [sb("zpad_a", [P, 2, BT, TAPS - 1 + S]), sb("zpad_b", [P, 2, BT, TAPS - 1 + S])]
        psum = ctx.enter_context(nc.psum_tensor("psum", [P, 8, T], F32))
        psum_b = psum[:, :, :].rearrange("p a n -> p (a n)").bitcast(BF16).rearrange("p (a n) -> p a n", a=8)
        streams = [Stream(0, arena_a), Stream(1, arena_b)]
        A = streams[0]
        sm = A.sm
        g_rows = spare[:, 0:1024].rearrange("p (k d) -> p k d", k=4)
        raw_qkvo = A.unit(2, 4).rearrange("p (k c d) -> p k c d", k=4, c=DC)
        raw_f8, f8_tmp = A.unit(6), A.unit(7)
        raw_mask = A.unit(8, 3).rearrange("p (k j l) -> p k j l", k=3, j=2)
        earlier = A.unit(21)[:, 0:P]
        slot_block = A.unit(21, 1, 1)[:, P:P + SLOTS * (NE - 1)].rearrange("p (j e) -> p j e", j=SLOTS)
        zeros = spare[:, 5 * EXPERT + UNITS * T:5 * EXPERT + UNITS * T + D]
        pooled_in, x1_in = [A.chunk(0, 2), A.chunk(2, 2)], [A.chunk(4, 2), A.chunk(6, 2)]
        rows_in = [A.rows(8), A.rows(10)]
        g_buf, act_h = A.chunk(12, 4), [A.unit(16), A.unit(17)]
        slot_rows = A.unit(18).rearrange("p (q d) -> p q d", q=2)
        slot_t = A.unit(19).rearrange("p (q c n) -> p q c n", q=2, c=DC)
        slot_out = A.unit(20).rearrange("p (q d) -> p q d", q=2)
        slot_h, slot_g = [A.unit(16), A.unit(17)], [A.unit(12), A.unit(13)]
        slot_g_t = [A.chunk(14, 4, 1), A.chunk(15, 4, 1)]

        x1_dram = nc.dram_tensor("x1_scratch", (TILES, P, DC, T), F32).ap()
        pooled_dram = nc.dram_tensor("pooled_scratch", (TILES, P, DC, T), F32).ap()
        rows_dram = nc.dram_tensor("rows_scratch", (TILES, P, NS, D), F32).ap()
        slot_in_dram = nc.dram_tensor("slot_in_scratch", (SLOTS, P, D), F32).ap()
        slot_out_dram = nc.dram_tensor("slot_out_scratch", (SLOTS, P, D), F32).ap()
        x2_dram = nc.dram_tensor("x2_scratch", (TILES, P, DC, T), F32).ap()

        loads = {n: signal(n + "_in", 0) for n in ("early", "mid", "attn")}
        ids_in = signal("ids_in", 0)
        expert_in = signal("expert_in", 0)
        late_expert_in = signal("late_expert_in", 0)
        g_rows_in = signal("g_rows_in", 0)
        zeros_ready = signal("zeros_ready", 0)
        slots_zeroed = signal("slots_zeroed", 0)
        setup_dve = signal("setup_dve", 0)
        setup_act = signal("setup_act", 0)
        setup_pe = signal("setup_pe", 0)
        setup_pool = signal("setup_pool", 0)

        x_in = [signal(f"x_in_{u}", 16) for u in (0, 1)]
        dve_chain_1 = signal("dve_chain_1", CHAIN["dve_1"])
        act_chain_1 = signal("act_chain_1", CHAIN["act_1"])
        ctx_ready = signal("ctx_ready")
        pe_soma = signal("pe_soma")
        h1_ready = signal("h1_ready")
        soma_ready = signal("soma_ready")
        pe_gate = signal("pe_gate")
        gate_tanh = signal("gate_tanh")
        pe_mod = signal("pe_mod")
        mod_tanh = signal("mod_tanh")
        mod_ready = signal("mod_ready")
        pe_mod_rows = signal("pe_mod_rows", ND)
        trace_ready = signal("trace_ready", ND)
        pe_trace_used = signal("pe_trace_used", ND)
        temporal_ready = signal("temporal_ready")
        pe_temp = signal("pe_temp")
        temp_tanh = signal("temp_tanh")
        mixed_ready = signal("mixed_ready")
        pe_cond = signal("pe_cond")
        cond_stats = signal("cond_stats")
        cond_std = signal("cond_std")
        cond_norm = signal("cond_norm")
        pe_cond_t = signal("pe_cond_t")
        cond_ready = signal("cond_ready")
        pe_s = signal("pe_s")
        s_copied = signal("s_copied")
        s_clipped = signal("s_clipped")
        p_exp = signal("p_exp")
        p_ready = signal("p_ready")
        pe_val = signal("pe_val", IC)
        val_copied = signal("val_copied", IC)
        pe_zg = signal("pe_zg", IC)
        zg_copied = signal("zg_copied", IC)
        pe_p_rows = signal("pe_p_rows", IC)
        val_ready = signal("val_ready", IC)
        gconv_ready = signal("gconv_ready", IC)
        phi_ready = signal("phi_ready", IC)
        gtanh_ready = signal("gtanh_ready", IC)
        angle_ready = signal("angle_ready", IC)
        trig_ready = signal("trig_ready", IC)
        mean_ready = signal("mean_ready", IC)
        sq_ready = signal("sq_ready", IC)
        pe_sq = signal("pe_sq", IC)
        pe_y = signal("pe_y", IC)
        yg_ready = signal("yg_ready", IC)
        rms_sqrt = signal("rms_sqrt")
        rms_ready = signal("rms_ready")
        pe_rms_rows = signal("pe_rms_rows")
        ynorm_ready = signal("ynorm_ready")
        pe_proj = signal("pe_proj")
        x1_ready = signal("x1_ready")
        pe_x1_rows = signal("pe_x1_rows")
        pe_score_hid = signal("pe_score_hid")
        x1_rows_ready = signal("x1_rows_ready")
        score_hid = signal("score_hid")
        pe_score = signal("pe_score")
        score_max = signal("score_max")
        pool_exp = signal("pool_exp")
        pool_p = signal("pool_p")
        pe_pool_t = signal("pe_pool_t")
        pool_t = signal("pool_t")
        pe_pool = signal("pe_pool")
        pool_ready = signal("pool_ready")
        pe_pool_rows = signal("pe_pool_rows")
        pool_rows_ready = signal("pool_rows_ready")
        pe_route = signal("pe_route")
        top_ready = signal("top_ready")
        route_exp = signal("route_exp")
        picks_ready = signal("picks_ready", 1, before=2)
        x1_stored = [signal(f"x1_stored_{u}", 48, before=16) for u in (0, 1)]
        order_in = signal("order_in", 0)
        sort_dve = signal("sort_dve", 0)
        sort_pe = signal("sort_pe", 0)
        ffn_in = [further(x_in[u], PAIRS, 32) for u in (0, 1)]
        rows_got = [signal(f"rows_got_{u}", 16) for u in (0, 1)]
        x2_stored = [further(x1_stored[u], PAIRS, 16) for u in (0, 1)]
        scattered = [signal(f"scattered_{u}", 2 * NS * 16) for u in (0, 1)]
        slots_now_ready = signal("slots_now_ready", 2)
        pe_up = signal("pe_up", 2 * FC)
        h_tanh = signal("h_tanh", 2 * FC)
        h_read = signal("h_read", 2 * FC)
        g_ready = signal("g_ready", 2 * FC)
        pe_down = signal("pe_down", 2)
        x2_ready = signal("x2_ready", 2, before=1)
        slot_rows_in = [signal(f"slot_rows_in_{p}", 16) for p in (0, 1)]
        slot_stored = [signal(f"slot_stored_{p}", 16, before=16) for p in (0, 1)]
        pe_slot_t = signal("pe_slot_t", 2, before=2)
        slot_t_ready = signal("slot_t_ready", 2)
        pe_slot_h = further(pe_up, PAIRS, 2)
        pe_slot_u = signal("pe_slot_u", 2)
        slot_tanh = further(h_tanh, PAIRS, 2)
        slot_h_ready = further(h_read, PAIRS, 2)
        slot_g_ready = further(g_ready, PAIRS, 2)
        pe_slot_g_t = signal("pe_slot_g_t", 2)
        slot_g_t_ready = signal("slot_g_t_ready", 2)
        pe_slot_out = further(pe_down, PAIRS, 2)
        slot_out_ready = signal("slot_out_ready", 2, before=1)
        x2_in = [further(ffn_in[u], PAIRS, 16) for u in (0, 1)]
        own_in = [signal(f"own_in_{u}", 8 * BT * 16) for u in (0, 1)]
        out_stored = [further(x2_stored[u], PAIRS, 16) for u in (0, 1)]
        gathered = [further(scattered[u], PAIRS, 2 * NS * 16) for u in (0, 1)]
        picked_slots = signal("picked_slots")
        picked_sum = signal("picked_sum")
        pe_picked_t = signal("pe_picked_t")
        x2_whole = signal("x2_whole")
        dve_chain_3 = further(dve_chain_1, PAIRS, CHAIN["dve_3"])
        act_chain_3 = further(act_chain_1, PAIRS, CHAIN["act_3"])
        NG = 12 * BT
        pe_bottle = signal("pe_bottle")
        bottle_ready = signal("bottle_ready")
        pe_adapt = signal("pe_adapt")
        adapt_stats = further(cond_stats, TILES, 1)
        adapt_std = further(cond_std, TILES, 1)
        adapt_ready = signal("adapt_ready")
        rms_in = signal("rms_in", 2)
        int_ready = signal("int_ready", 4)
        pe_int_t = signal("pe_int_t", 4)
        int_t = signal("int_t", 4)
        pe_scale = signal("pe_scale", 2)
        diag_ready = signal("diag_ready", 2)
        scale_ready = signal("scale_ready", 2)
        pe_q = signal("pe_q")
        q_ready = signal("q_ready")
        pe_k = signal("pe_k")
        k_ready = signal("k_ready")
        pe_v = signal("pe_v")
        v_ready = signal("v_ready")
        pe_logits = signal("pe_logits", NG)
        row_max = signal("row_max", NG)
        probs_ready = signal("probs_ready", NG)
        pe_probs_t = signal("pe_probs_t", NG)
        probs_t = signal("probs_t", NG)
        pe_heads = signal("pe_heads", NG)
        heads_ready = signal("heads_ready", 2 * BT)
        pe_o = signal("pe_o")
        x3_ready = signal("x3_ready")
        pe_cat = signal("pe_cat")
        f8_ready = signal("f8_ready")
        pe_f8 = signal("pe_f8")
        half_ready = signal("half_ready")
        out_ready = signal("out_ready", 1, before=2)

        class Group:

            def __init__(self, n):
                self.b, k = divmod(n, 12)
                self.s = 2 * self.b + (k >= 4)
                r = k % 4
                self.heads = [r, r + 4, r + 8, r + 12] if k < 4 else [r, r + 4] if k < 8 else [r + 8, r + 12]
                self.width = P if k < 4 else S
                self.first, self.last = k in (0, 4), k in (3, 11)

        def group(n):
            return Group(n)

        def period(sig):
            return sig.per_tile if sig in once else 2 * sig.per_tile

        once = [dve_chain_1, act_chain_1, dve_chain_3, act_chain_3, slots_now_ready, h_tanh, h_read, g_ready, x2_ready,
                setup_dve, setup_act, setup_pe, setup_pool]

        block = ctx.enter_context(nc.Block())

        @block.sync
        def _(sp):
            def load(name, dst, sig):
                sp.dma_start(dst, dram[name]).then_inc(sig.sem, 16)

            def fetch(dst, src, t, sig):
                sp.dma_start(dst, src[bass.ds(t, 1)].rearrange("a p c n -> (a p) c n")).then_inc(sig.sem, 16)

            def keep(dst, t, src, sig):
                sp.dma_start(dst[bass.ds(t, 1)].rearrange("a p c n -> (a p) c n"), src).then_inc(sig.sem, 16)

            load("vecs", vecs[:, :], loads["early"])
            for s in (picks_ready, x2_ready, pe_slot_t, slot_out_ready, out_ready, *x1_stored, *slot_stored):
                sp.sem_inc(s.sem, s.before)
            for n in EARLY:
                load(n, w[n][...], loads["early"])
            load("ids_row", ids_row[:, :], ids_in)
            for n in MID:
                load(n, w[n][...], loads["mid"])
            load("kind_ids", kind_ids[:, :], loads["mid"])
            load("qkvo", raw_qkvo, loads["attn"])
            load("pool_mask", raw_mask, loads["attn"])
            load("w_f8", raw_f8, loads["attn"])
            load("causal", w["causal"][...], loads["attn"])
            sp.wait_ge(zeros_ready.sem, 1)
            sp.dma_start(slot_in_dram.rearrange("n p d -> p n d"),
                         zeros[:, None, :].broadcast_to([P, SLOTS, D])).then_inc(slots_zeroed.sem, 16)
            with sp.Fori(0, PAIRS) as t:
                for u in (0, 1):
                    sp.wait_ge(x1_stored[u].sem, x1_stored[u].at(t, 0))
                    fetch(streams[u].x, dram["x_t"], t * 2 + u, x_in[u])
                for u in (0, 1):
                    sp.wait_ge(pool_rows_ready.sem, pool_rows_ready.at(t, 1, u))
                    keep(x1_dram, t * 2 + u, streams[u].x, x1_stored[u])
                    keep(rows_dram, t * 2 + u, streams[u].pooled_rows, x1_stored[u])
                    keep(pooled_dram, t * 2 + u, streams[u].pooled, x1_stored[u])
            def shared_in(t):
                u = t % 2
                fetch(pooled_in[u], pooled_dram, t, ffn_in[u])
                fetch(x1_in[u], x1_dram, t, ffn_in[u])
                fetch(rows_in[u], rows_dram, t, rows_got[u])

            for u in (0, 1):
                sp.wait_ge(x1_stored[u].sem, x1_stored[u].at(PAIRS, 0))
            sp.wait_ge(picks_ready.sem, picks_ready.at(PAIRS - 1, 1, 1))
            load("earlier", earlier, order_in)
            load("slot_block", slot_block, order_in)
            shared_in(0)
            shared_in(1)
            sp.wait_ge(slots_zeroed.sem, 16)
            for e in range(5, EXPERTS):
                sp.dma_start(expert_w[:, e, :], dram["expert_w"][e]).then_inc(late_expert_in.sem, 16)
            for t in range(TILES):
                u = t % 2
                sp.wait_ge(x2_ready.sem, x2_ready.at(0, t + 1))
                keep(x2_dram, t, x1_in[u], x2_stored[u])
                if t + 2 < TILES:
                    sp.wait_ge(x2_stored[u].sem, x2_stored[u].at(t // 2 + 1, 0))
                    sp.wait_ge(scattered[u].sem, scattered[u].at(t // 2 + 1, 0))
                    shared_in(t + 2)
            for u in (0, 1):
                sp.wait_ge(scattered[u].sem, scattered[u].at(PAIRS, 0))
                sp.wait_ge(x2_stored[u].sem, x2_stored[u].at(PAIRS, 0))
            with sp.Fori(0, SLOT_PAIRS) as i:
                for p in (0, 1):
                    sp.wait_ge(pe_slot_t.sem, pe_slot_t.at(i, p - 1))
                    sp.dma_start(slot_rows[:, p, :], slot_in_dram[bass.ds(i * 2 + p, 1)].rearrange("a p d -> (a p) d")) \
                        .then_inc(slot_rows_in[p].sem, 16)
            for p in (0, 1):
                sp.wait_ge(slot_stored[p].sem, slot_stored[p].at(SLOT_PAIRS, 0))
            sp.wait_ge(ids_in.sem, 16)
            sp.dma_start(g_rows, dram["g_rows"]).then_inc(g_rows_in.sem, 16)
            with sp.Fori(0, PAIRS) as t:
                for u in (0, 1):
                    s = streams[u]
                    first = (t * 2 + u) * BT
                    who = sp.value_load(ids_row[0:1, bass.ds(first, 1)])
                    sp.wait_ge(out_stored[u].sem, out_stored[u].at(t, 0))
                    fetch(s.x, x2_dram, t * 2 + u, x2_in[u])
                    for b in range(BT):
                        if b:
                            who = sp.value_load(ids_row[0:1, bass.ds(first + b, 1)])

                        def own(dst, name, pattern, to=None):
                            src = dram[name][bass.ds(who, 1)].rearrange(pattern)
                            sp.dma_start(dst, src if to is None else src.broadcast_to(to)).then_inc(own_in[u].sem, 16)

                        own(s.adapt_down[:, b, :, :], "down_w", "a p c n -> (a p) c n")
                        own(s.adapt_up[:, b, :], "up_w", "a p n -> (a p) n")
                        own(s.adapt_bd[:, b:b + 1], "down_b", "a p n -> (a p) n")
                        own(s.adapt_bu[:, b, :], "up_b", "a b d -> (a b) d")
                        own(s.adapt_rows[:, 0, b, :], "ln_g", "a b d -> (a b) d", [P, D])
                        own(s.adapt_rows[:, 1, b, :], "ln_b", "a b d -> (a b) d", [P, D])
                        who = sp.value_load(ids_row[0:1, bass.ds(first + b + B, 1)])
                        own(s.cat_w[:, b, :, :], "cat_w", "a p c n -> (a p) c n")
                        own(s.cat_b[:, b, :], "cat_b", "a p c -> (a p) c")
                for u in (0, 1):
                    sp.wait_ge(out_ready.sem, out_ready.at(t, 1, u))
                    keep(out, t * 2 + u, streams[u].out_t, out_stored[u])
            for u in (0, 1):
                sp.wait_ge(out_stored[u].sem, out_stored[u].at(PAIRS, 0))

        @block.gpsimd
        def _(pool):
            for z in zpads:
                nc.gpsimd.memset(z[:, :, :, 0:TAPS - 1], 0.0).then_inc(setup_pool.sem, 1)
            nc.gpsimd.memset(tern_qk[:, :, :, :], 0.0).then_inc(setup_pool.sem, 1)
            nc.gpsimd.memset(zeros, 0.0).then_inc(zeros_ready.sem, 1)
            for e in range(5):
                pool.dma_start(expert_w[:, e, :], dram["expert_w"][e]).then_inc(expert_in.sem, 16)
            slot_in_rows = slot_in_dram.rearrange("n p d -> (n p) d")
            slot_out_rows = slot_out_dram.rearrange("n p d -> (n p) d")
            for t in range(PAIRS):
                for u in (0, 1):
                    pool.wait_ge(slots_now_ready.sem, slots_now_ready.at(t, u + 1))
                    pool.wait_ge(rows_got[u].sem, rows_got[u].at(t, 16))
                    pool.wait_ge(slots_zeroed.sem, 16)
                    for c in range(2):
                        for k in range(NS):
                            at = bass.IndirectOffsetOnAxis(ap=slots_now[u][:, c, k:k + 1], axis=0)
                            nc.gpsimd.indirect_dma_start(slot_in_rows, at, rows_in[u][:, k, :], None,
                                                         bounds_check=SLOTS * P - 1).then_inc(scattered[u].sem, 16)
            for t in range(PAIRS):
                for u in (0, 1):
                    pool.wait_ge(picked_slots.sem, picked_slots.at(t, 1, u))
                    for p in (0, 1):
                        pool.wait_ge(slot_stored[p].sem, slot_stored[p].at(SLOT_PAIRS, 0))
                    for c in range(2):
                        for k in range(NS):
                            at = bass.IndirectOffsetOnAxis(ap=slots_now[u][:, c, k:k + 1], axis=0)
                            nc.gpsimd.indirect_dma_start(streams[u].picked[c][:, k, :], None, slot_out_rows, at,
                                                         bounds_check=SLOTS * P - 1).then_inc(gathered[u].sem, 16)

        @block.scalar
        def _(act):
            a = nc.scalar.activation

            def setup(ins):
                setup_act.given += 1
                ins.then_inc(setup_act.sem, 1)
                act.wait_ge(setup_act.sem, setup_act.given)

            act.wait_ge(loads["early"].sem, 16 * N_EARLY)
            setup(a(decay[:, :], vecs[:, VEC["tau"][0]:VEC["tau"][0] + 1 + ND], ACT.Exp))
            setup(a(sm(0, 1, HEADS_B), col("slope", 0, HEADS_B), ACT.Abs))
            setup(a(sm(1, 1, HEADS_B), sm(0, 1, HEADS_B), ACT.Exp, scale=-1.0))
            act.wait_ge(setup_dve.sem, DVE_MAXIMA)
            setup(a(blend[:, :, :], blend[:, :, :], ACT.Exp))
            setup(a(deriv[:, 0:3], deriv[:, 0:3], ACT.Exp))
            act.wait_ge(setup_dve.sem, DVE_SLOPES)
            setup(a(time_w[:, :], time_w[:, :], ACT.Exp, scale=slope[:, 0:1]))

            chain = act_chain_1

            def step(t, ins, sig=None):
                sig = sig or chain
                sig.given += 1
                ins.then_inc(sig.sem, 1)
                act.wait_ge(sig.sem, t * period(sig) + (sig.before + sig.given))

            def condition(t):
                for u, s in enumerate(streams):
                    act.wait_ge(pe_soma.sem, pe_soma.at(t, 1, u))
                    step(t, a(s.h1, s.bank(0, p=HID), ACT.Gelu, bias=col("bn1", 0, HID)), h1_ready)
                    step(t, a(s.soma[:, 0, :], s.bank(1), ACT.Gelu, bias=col("bsoma", 0)))
                    step(t, a(s.soma[:, 1, :], s.bank(2), ACT.Gelu, bias=col("bsoma", 1)), soma_ready)
                for u, s in enumerate(streams):
                    act.wait_ge(pe_gate.sem, pe_gate.at(t, 1, u))
                    step(t, a(s.gate_t[:, 0, :], s.bank(3), ACT.Tanh, bias=half_b[:, 0:1], scale=0.5))
                    step(t, a(s.gate_t[:, 1, :], s.bank(0), ACT.Tanh, bias=half_b[:, 1:2], scale=0.5), gate_tanh)
                for u, s in enumerate(streams):
                    act.wait_ge(pe_mod.sem, pe_mod.at(t, 1, u))
                    step(t, a(s.mod, s.bank(1, p=ND), ACT.Tanh, bias=half_b[0:ND, 4:5], scale=0.5), mod_tanh)
                for u, s in enumerate(streams):
                    act.wait_ge(pe_trace_used.sem, pe_trace_used.at(t, ND, u))
                    step(t, a(s.temporal[:, :, :], s.bank(0, 2), ACT.Copy), temporal_ready)
                for u, s in enumerate(streams):
                    act.wait_ge(pe_temp.sem, pe_temp.at(t, 1, u))
                    step(t, a(s.gate_t[:, 0, :], s.bank(2), ACT.Tanh, bias=half_b[:, 2:3], scale=0.5))
                    step(t, a(s.gate_t[:, 1, :], s.bank(3), ACT.Tanh, bias=half_b[:, 3:4], scale=0.5), temp_tanh)
                for u, s in enumerate(streams):
                    act.wait_ge(cond_stats.sem, cond_stats.at(t, 1, u))
                    step(t, a(s.sm(0, NS), s.stat_var, ACT.Sqrt, bias=col("eps5"), scale=0.25), cond_std)
                for u, s in enumerate(streams):
                    act.wait_ge(pe_cond_t.sem, pe_cond_t.at(t, 1, u))
                    step(t, a(s.cond[:, 0, :], s.bank(2), ACT.Identity, bias=col("beta", 0), scale=col("gamma", 0)))
                    step(t, a(s.cond[:, 1, :], s.bank(3), ACT.Identity, bias=col("beta", 1), scale=col("gamma", 1)),
                         cond_ready)

            def z_out(t, s, bank, which, chunk, copied, p=P):
                step(t, a(s.conv[which][0:p, :], s.bank(bank, p=p), ACT.Identity,
                          bias=col("conv_b", chunk, p), scale=col("conv_k", TAPS * chunk + TAPS - 1, p)))
                step(t, a(s.zpad[0:p, which, :, TAPS - 1:], s.bank(bank, p=p).rearrange("p (b n) -> p b n", b=BT),
                          ACT.Copy), copied)

            def scan_attention(t):
                for u, s in enumerate(streams):
                    act.wait_ge(pe_s.sem, pe_s.at(t, 1, u))
                    z_out(t, s, 2, 0, 8, s_copied, HEADS_B)
                for u, s in enumerate(streams):
                    act.wait_ge(s_clipped.sem, s_clipped.at(t, 1, u))
                    step(t, a(s.p_t, s.conv[0][0:HEADS_B, :], ACT.Exp), p_exp)
                for c in range(IC):
                    for u, s in enumerate(streams):
                        if c == 0:
                            act.wait_ge(p_ready.sem, p_ready.at(t, 1, u))
                        else:
                            act.wait_ge(yg_ready.sem, yg_ready.at(t, c, u))
                        act.wait_ge(pe_val.sem, pe_val.at(t, c + 1, u))
                        z_out(t, s, 0, 0, c, val_copied)
                        act.wait_ge(pe_zg.sem, pe_zg.at(t, c + 1, u))
                        z_out(t, s, 1, 1, IC + c, zg_copied)
                    for u, s in enumerate(streams):
                        act.wait_ge(val_ready.sem, val_ready.at(t, c + 1, u))
                        step(t, a(s.phi, s.conv[0], ACT.Identity, bias=col("zero"), scale=col("theta", c)), phi_ready)
                        act.wait_ge(gconv_ready.sem, gconv_ready.at(t, c + 1, u))
                        step(t, a(s.gtanh, s.conv[1], ACT.Tanh, scale=0.5), gtanh_ready)
                    for u, s in enumerate(streams):
                        act.wait_ge(angle_ready.sem, angle_ready.at(t, c + 1, u))
                        step(t, a(s.sin_t, s.angle, ACT.Sin))
                        step(t, a(s.angle, s.angle, ACT.Abs))
                        step(t, a(s.cos_t, s.angle, ACT.Sin, bias=col("half_pi"), scale=-1.0), trig_ready)
                    for u, s in enumerate(streams):
                        act.wait_ge(mean_ready.sem, mean_ready.at(t, c + 1, u))
                        step(t, a(s.sin_t, s.mean_im, ACT.Square))
                        step(t, a(s.cos_t, s.mean_re, ACT.Square), sq_ready)
                for u, s in enumerate(streams):
                    act.wait_ge(pe_sq.sem, pe_sq.at(t, IC, u))
                    step(t, a(s.rms_b, s.bank(3, p=HEADS_B), ACT.Sqrt, bias=col("eps5", 0, HEADS_B)), rms_sqrt)

            def pool_prompt(t):
                for u, s in enumerate(streams):
                    act.wait_ge(pe_x1_rows.sem, pe_x1_rows.at(t, 1, u))
                    step(t, a(s.x1_rows, s.token_banks(2), ACT.Copy), x1_rows_ready)
                    act.wait_ge(pe_score_hid.sem, pe_score_hid.at(t, 1, u))
                    step(t, a(s.score_h, s.bank(0, p=HID), ACT.Tanh, bias=col("b1", 0, HID)), score_hid)
                for u, s in enumerate(streams):
                    act.wait_ge(score_max.sem, score_max.at(t, 1, u))
                    for g in range(4):
                        step(t, a(s.pool_w[:, g, :], s.masked[:, g, :], ACT.Exp, bias=s.sm(8 + g, 1),
                                  accum_out=s.sm(12 + g, 1)), pool_exp if g == 3 else None)
                for u, s in enumerate(streams):
                    act.wait_ge(pe_pool_t.sem, pe_pool_t.at(t, 1, u))
                    step(t, a(s.pool_wt, s.bank(2, 2), ACT.Copy), pool_t)
                for u, s in enumerate(streams):
                    act.wait_ge(pe_pool.sem, pe_pool.at(t, 1, u))
                    step(t, a(s.pooled, s.bank(0, 2), ACT.Copy), pool_ready)

                for u, s in enumerate(streams):
                    act.wait_ge(pe_pool_rows.sem, pe_pool_rows.at(t, 1, u))
                    step(t, a(s.pooled_rows, s.token_banks(2), ACT.Copy), pool_rows_ready)
                for u, s in enumerate(streams):
                    act.wait_ge(top_ready.sem, top_ready.at(t, 1, u))
                    step(t, a(s.sm(160, NS), s.sm(160, NS), ACT.Exp), route_exp)

            def shared_expert(t):
                for n in range(2 * FC):
                    act.wait_ge(pe_up.sem, pe_up.at(t, n + 1))
                    step(t, a(act_h[n % 2], psum[:, 3 + n % 2, :], ACT.Tanh, scale=0.5), h_tanh)

            def slot_tanh_of(i, k):
                q = k % 2
                act.wait_ge(pe_slot_h.sem, pe_slot_h.at(i, k + 1))
                a(slot_h[q], psum[:, q, :], ACT.Tanh, scale=0.5).then_inc(slot_tanh.sem, 1)

            def slot_out_of(i, k):
                q = k % 2
                act.wait_ge(pe_slot_g_t.sem, pe_slot_g_t.at(i, k + 1))
                a(slot_g_t[q], psum[:, 4, :].rearrange("p (c n) -> p c n", c=FC), ACT.Copy).then_inc(slot_g_t_ready.sem, 1)
                act.wait_ge(pe_slot_out.sem, pe_slot_out.at(i, k + 1))
                act.wait_ge(slot_stored[q].sem, slot_stored[q].at(i, 0))
                a(slot_out[:, q, :], psum[:, 6, 0:D], ACT.Copy).then_inc(slot_out_ready.sem, 1)
                act.wait_ge(slot_out_ready.sem, slot_out_ready.at(i, k + 1))
                act.dma_start(slot_out_dram[bass.ds(i * 2 + k, 1)].rearrange("a p d -> (a p) d"), slot_out[:, q, :]) \
                    .then_inc(slot_stored[q].sem, 16)

            def adapter(t):
                for u, s in enumerate(streams):
                    act.wait_ge(pe_bottle.sem, pe_bottle.at(t, 1, u))
                    for b in range(BT):
                        step(t, a(s.bottle[:, b * S:(b + 1) * S], s.bank(0)[:, b * S:(b + 1) * S], ACT.Relu,
                                  bias=s.adapt_bd[:, b:b + 1]), bottle_ready if b else None)
                for u, s in enumerate(streams):
                    act.wait_ge(adapt_stats.sem, adapt_stats.at(t, 1, u))
                    step(t, a(s.sm(0, NS), s.stat_var, ACT.Sqrt, bias=col("eps5")), adapt_std)

            def mean_square(t, s, rows, scratch, done):
                for k in range(NS):
                    step(t, a(scratch[:, k, :], rows[:, k, :], ACT.Square, accum_out=s.sm(200 + k, 1)))
                step(t, a(s.sm(204, NS), s.sm(200, NS), ACT.Sqrt, bias=col("eps6"), scale=1.0 / D), done)

            def attention(t):
                for u, s in enumerate(streams):
                    act.wait_ge(adapt_ready.sem, adapt_ready.at(t, 1, u))
                    mean_square(t, s, s.attn_in, s.adapt_y, rms_in)
                for g in range(3):
                    for u, s in enumerate(streams):
                        act.wait_ge(pe_int_t.sem, pe_int_t.at(t, g + 1, u))
                        step(t, a(s.int_tt, s.bank_b(0, 2), ACT.Copy), int_t)
                    for u, s in enumerate(streams):
                        if g == 0:
                            act.wait_ge(pe_q.sem, pe_q.at(t, 1, u))
                            step(t, a(s.q_t, s.bank(0, 4), ACT.Copy), q_ready)
                        if g == 1:
                            act.wait_ge(pe_scale.sem, pe_scale.at(t, 1, u))
                            step(t, a(s.kscale_b, s.bank(2), ACT.Copy), scale_ready)
                def probs_out(n, u, s):
                    g = group(n)
                    act.wait_ge(row_max.sem, row_max.at(t, n + 1, u))
                    if n >= 2:
                        act.wait_ge(pe_probs_t.sem, pe_probs_t.at(t, n - 1, u))
                    for j, head in enumerate(g.heads):
                        cols = slice(j * g.width, (j + 1) * g.width)
                        step(t, a(s.probs[n % 2][:, cols], s.bank(n % 2)[:, cols], ACT.Exp,
                                  bias=s.sm(320 + g.s * NH + head, 1), scale=s.sm(216 + g.s, 1),
                                  accum_out=s.sm(384 + g.s * NH + head, 1)), probs_ready if j == len(g.heads) - 1 else None)

                for n in range(NG):
                    for u, s in enumerate(streams):
                        probs_out(n, u, s)
                for u, s in enumerate(streams):
                    act.wait_ge(heads_ready.sem, heads_ready.at(t, 2 * BT, u))
                    mean_square(t, s, s.head_out, s.scaled_in, rms_in)
                for u, s in enumerate(streams):
                    act.wait_ge(pe_int_t.sem, pe_int_t.at(t, 4, u))
                    step(t, a(s.y_tt, s.bank_b(0, 2), ACT.Copy), int_t)
                    act.wait_ge(pe_scale.sem, pe_scale.at(t, 2, u))
                    step(t, a(s.yscale_b, s.bank(2), ACT.Copy), scale_ready)

            def last_ffn(t):
                for u, s in enumerate(streams):
                    act.wait_ge(pe_f8.sem, pe_f8.at(t, 1, u))
                    step(t, a(s.half_t, s.bank(2, 2), ACT.Copy), half_ready)

            with act.Fori(0, PAIRS) as t:
                condition(t)
                scan_attention(t)
                pool_prompt(t)
            with act.Fori(0, PAIRS) as t:
                shared_expert(t)
            slot_tanh_of(0, 0)
            with act.Fori(0, SLOT_PAIRS - 1) as i:
                for k in (1, 2):
                    slot_tanh_of(i, k)
                    slot_out_of(i, k - 1)
            slot_tanh_of(SLOT_PAIRS - 1, 1)
            slot_out_of(SLOT_PAIRS - 1, 0)
            slot_out_of(SLOT_PAIRS - 1, 1)
            chain = act_chain_3
            with act.Fori(0, PAIRS) as t:
                adapter(t)
                attention(t)
                last_ffn(t)

        @block.vector
        def _(dve):
            v = nc.vector

            def setup(ins):
                setup_dve.given += 1
                ins.then_inc(setup_dve.sem, 1)
                dve.wait_ge(setup_dve.sem, setup_dve.given)

            def round_to_even(dst, src):
                return v.tensor_scalar(dst, src, MAGIC, MAGIC, ALU.add, ALU.subtract)

            dve.wait_ge(loads["early"].sem, 16 * N_EARLY)
            at, n = VEC["blend"]
            raw_blend = vecs[:, at:at + n].rearrange("p (c d) -> p c d", c=DC)
            setup(v.tensor_reduce(out=sm(20, DC), in_=raw_blend, axis=AX.X, op=ALU.max))
            setup(v.tensor_tensor(blend[:, :, :], raw_blend, sm(20, DC)[:, :, None].broadcast_to([P, DC, ND]), ALU.subtract))
            at, n = VEC["deriv"]
            setup(v.tensor_reduce(out=sm(22, 1), in_=vecs[:, at:at + n], axis=AX.X, op=ALU.max))
            setup(v.tensor_scalar(deriv[:, 0:3], vecs[:, at:at + n], sm(22, 1), None, ALU.subtract))
            assert setup_dve.given == DVE_MAXIMA
            at = VEC["bg"][0]
            setup(v.tensor_scalar(half_b[:, 0:2 * DC], vecs[:, at:at + 2 * DC], 0.5, None, ALU.mult))
            setup(v.tensor_scalar(half_b[0:ND, 2 * DC:2 * DC + 1], col("bn2", 0, ND), 0.5, None, ALU.mult))
            act_u, s1, s2, acc, r = (sm(k, 1, HEADS_B) for k in (1, 2, 3, 4, 5))
            dve.wait_ge(setup_act.sem, 3)
            setup(v.tensor_scalar(s1, act_u, 2.0, None, ALU.add))
            setup(v.reciprocal(s1, s1))
            setup(v.tensor_tensor(s1, s1, act_u, ALU.mult))
            setup(v.tensor_tensor(s2, s1, s1, ALU.mult))
            setup(v.tensor_scalar(acc, s2, 1.0 / 19, 1.0 / 17, ALU.mult, ALU.add))
            for k in (15, 13, 11, 9, 7, 5, 3, 1):
                setup(v.tensor_scalar(acc, acc, s2, 1.0 / k, ALU.mult, ALU.add))
            setup(v.tensor_tensor(acc, acc, s1, ALU.mult))
            setup(v.tensor_scalar(r, col("slope", 0, HEADS_B), 0.0, None, ALU.max))
            setup(v.scalar_tensor_tensor(slope[:, :], acc, -2.0, r, ALU.mult, ALU.subtract))
            assert setup_dve.given == DVE_SLOPES
            setup(v.tensor_scalar(decay[:, :], decay[:, :], 1.0, None, ALU.add))
            setup(v.reciprocal(decay[:, :], decay[:, :]))
            dve.wait_ge(setup_act.sem, 5)
            setup(v.tensor_reduce(out=sm(20, DC), in_=blend[:, :, :], axis=AX.X, op=ALU.add))
            setup(v.reciprocal(sm(20, DC), sm(20, DC)))
            setup(v.tensor_tensor(blend[:, :, :], blend[:, :, :], sm(20, DC)[:, :, None].broadcast_to([P, DC, ND]),
                                  ALU.mult))
            setup(v.tensor_scalar(blend[:, :, :], blend[:, :, :], 0.5, None, ALU.mult))
            setup(v.tensor_reduce(out=sm(22, 1), in_=deriv[:, 0:3], axis=AX.X, op=ALU.add))
            setup(v.reciprocal(sm(22, 1), sm(22, 1)))
            setup(v.tensor_scalar(deriv[:, 0:3], deriv[:, 0:3], sm(22, 1), None, ALU.mult))
            setup(v.tensor_scalar(deriv[:, 3:4], deriv[:, 2:3], -1.0, None, ALU.mult))
            dve.wait_ge(loads["mid"].sem, 16 * N_MID)
            setup(v.tensor_scalar(w["w_re"][:, :], w["w_re"][:, :], col("norm_re"), 0.5, ALU.mult, ALU.mult))
            setup(v.tensor_scalar(w["w_im"][:, :], w["w_im"][:, :], col("norm_im"), 0.5, ALU.mult, ALU.mult))
            setup(v.tensor_copy(sm(40, B), kind_ids[:, :]))
            setup(v.tensor_scalar(kind[:, :, 0], sm(40, B), 0.0, None, ALU.is_equal))
            setup(v.tensor_scalar(kind[:, :, 1], sm(40, B), 1.0, None, ALU.is_equal))
            setup(v.tensor_tensor(kind[:, :, 2], kind[:, :, 0], kind[:, :, 1], ALU.add))
            setup(v.tensor_scalar(kind[:, :, 2], kind[:, :, 2], -1.0, 1.0, ALU.mult, ALU.add))
            setup(v.tensor_copy(ident_b[:, :], w["ident"][:, :]))
            dve.wait_ge(loads["attn"].sem, 16 * 4)
            setup(v.tensor_copy(pool_mask[:, :, :, :], raw_mask))
            dve.wait_ge(setup_pool.sem, 3)
            setup(v.tensor_copy(causal_a[:, :].rearrange("p (k n) -> p k n", k=4),
                                w["causal"][:, None, :].broadcast_to([P, 4, P])))
            setup(v.tensor_reduce(out=sm(44, 4), in_=raw_qkvo.rearrange("p k c d -> p k (c d)"), axis=AX.X, op=ALU.add,
                                  apply_absolute_value=True))
            assert setup_dve.given == DVE_SUMS
            dve.wait_ge(setup_pe.sem, 1)
            setup(v.tensor_scalar(w_scale[:, 0:4], psum[:, 0, 0:4], 1.0 / (D * D), 1e-5, ALU.mult, ALU.max))
            assert setup_dve.given == DVE_SUMS + 1
            setup(v.reciprocal(w_scale[:, 4:8], w_scale[:, 0:4]))
            setup(v.tensor_scalar(qk_scale[:, :], w_scale[:, 0:1], w_scale[:, 1:2], HD ** -0.5, ALU.mult, ALU.mult))
            for k in range(4):
                raw = raw_qkvo[:, k, :, :]
                setup(v.tensor_scalar(raw, raw, w_scale[:, 4 + k:5 + k], MAGIC, ALU.mult, ALU.add))
                setup(v.tensor_scalar(raw, raw, MAGIC, 1.0, ALU.subtract, ALU.min))
                if k < 2:
                    for c in range(DC):
                        setup(v.tensor_scalar(tern_qk[:, k, c, :].rearrange("p (h d) -> p h d", h=NH)[:, :, 0:HD],
                                              raw[:, c, :].rearrange("p (h d) -> p h d", h=NH), -1.0, None, ALU.max))
                else:
                    setup(v.tensor_scalar(tern_vo[:, k - 2, :, :], raw, -1.0, None, ALU.max))

            def float8_values(run, val, tmp, dst):
                run(v.tensor_scalar(val, val, 448.0, -448.0, ALU.min, ALU.max))
                run(v.tensor_scalar(tmp.bitcast(I32), val.bitcast(I32), 0x7F800000, None, ALU.bitwise_and))
                run(v.tensor_scalar(tmp, tmp, 2.0 ** -6, 1.5 * 2.0 ** 20, ALU.max, ALU.mult))
                run(v.tensor_tensor(val, val, tmp, ALU.add))
                run(v.tensor_tensor(dst, val, tmp, ALU.subtract))

            float8_values(setup, raw_f8, f8_tmp, f8_w[:, :, :].rearrange("p c d -> p (c d)"))

            chain = dve_chain_1

            def step(t, ins, sig=None, wait=True):
                sig = sig or chain
                sig.given += 1
                ins.then_inc(sig.sem, 1)
                if wait:
                    dve.wait_ge(sig.sem, t * period(sig) + (sig.before + sig.given))

            def averages(t, dst, src, decay_col, last):
                for c in range(DC):
                    for b in range(BT):
                        tokens = slice(b * S, (b + 1) * S)
                        end = (c, b) == (DC - 1, BT - 1)
                        step(t, v.tensor_tensor_scan(dst[:, c, tokens], decay_col.broadcast_to([P, S]), src[:, c, tokens],
                                                     0.0, ALU.mult, ALU.add), last if end else None, wait=end)

            def row_stats(t, s, rows, last):
                for k in range(NS):
                    step(t, v.bn_stats(s.sm(32 + 6 * k, 6), rows[:, k, :]), wait=k == NS - 1)
                step(t, v.memset(s.sm(620, 1), 0.0), wait=False)
                for k in range(NS):
                    end = k == NS - 1
                    step(t, v.bn_aggr(s.sm(24 + 2 * k, 2), s.sm(32 + 6 * k, 6)), last if end else None, wait=end)

            def condition(t):
                for u, s in enumerate(streams):
                    dve.wait_ge(x_in[u].sem, x_in[u].at(t, 16))
                    averages(t, s.ctx_t, s.x, decay[:, 0:1], ctx_ready)
                for u, s in enumerate(streams):
                    dve.wait_ge(gate_tanh.sem, gate_tanh.at(t, 1, u))
                    step(t, v.scalar_tensor_tensor(s.gated, s.gate_t, 1.0, s.x, ALU.add, ALU.mult), wait=False)
                for u, s in enumerate(streams):
                    dve.wait_ge(mod_tanh.sem, mod_tanh.at(t, 1, u))
                    step(t, v.tensor_scalar(s.mod, s.mod, 0.5, 1.0, ALU.mult, ALU.add), mod_ready)
                for d in range(ND):
                    for u, s in enumerate(streams):
                        dve.wait_ge(pe_mod_rows.sem, pe_mod_rows.at(t, d + 1, u))
                        for c in range(DC):
                            step(t, v.scalar_tensor_tensor(s.scaled[d % 2][:, c, :], s.gated[:, c, :], blend[:, c, d:d + 1],
                                                           s.bank(2 + d % 2), ALU.mult, ALU.mult), wait=c == DC - 1)
                        if d >= 2:
                            dve.wait_ge(pe_trace_used.sem, pe_trace_used.at(t, d - 1, u))
                        averages(t, s.trace[d % 2], s.scaled[d % 2], decay[:, 1 + d:2 + d], trace_ready)
                for u, s in enumerate(streams):
                    dve.wait_ge(temp_tanh.sem, temp_tanh.at(t, 1, u))
                    step(t, v.scalar_tensor_tensor(s.gate_t, s.gate_t, 1.0, s.soma, ALU.add, ALU.mult), mixed_ready)
                for u, s in enumerate(streams):
                    dve.wait_ge(pe_cond.sem, pe_cond.at(t, 1, u))
                    row_stats(t, s, s.token_banks(0), cond_stats)
                for u, s in enumerate(streams):
                    dve.wait_ge(cond_std.sem, cond_std.at(t, 1, u))
                    step(t, v.reciprocal(s.sm(4, NS), s.sm(0, NS)))
                    step(t, v.tensor_scalar(s.sm(4, NS), s.sm(4, NS), 0.5, None, ALU.mult))
                    for k in range(NS):
                        end = k == NS - 1
                        step(t, v.tensor_scalar(s.cond_rows[:, k, :], s.token_banks(0)[:, k, :], s.stat[:, k, 0:1],
                                                s.sm(4 + k, 1), ALU.subtract, ALU.mult), cond_norm if end else None, wait=end)

            def taps(t, s, which, chunk, p, last):
                acc = s.conv[which][0:p, :].rearrange("p (b n) -> p b n", b=BT)
                for j in range(TAPS - 1):
                    step(t, v.scalar_tensor_tensor(acc, s.zpad[0:p, which, :, j:j + S], col("conv_k", TAPS * chunk + j, p),
                                                   acc, ALU.mult, ALU.add), last if j == TAPS - 2 else None)

            def scan_attention(t):
                one = w["ones"][:, 0:1]
                for u, s in enumerate(streams):
                    raw = s.conv[0][0:HEADS_B, :]
                    dve.wait_ge(s_copied.sem, s_copied.at(t, 1, u))
                    taps(t, s, 0, 8, HEADS_B, None)
                    step(t, v.tensor_scalar(raw, raw, col("score_scale", 0, HEADS_B), 20.0, ALU.mult, ALU.min))
                    step(t, v.tensor_scalar(raw, raw, -20.0, None, ALU.max), s_clipped)
                for u, s in enumerate(streams):
                    dve.wait_ge(p_exp.sem, p_exp.at(t, 1, u))
                    by_batch = s.p_t.rearrange("p (b n) -> p b n", b=BT)
                    step(t, v.tensor_tensor(by_batch, by_batch, time_w[:, None, :].broadcast_to([HEADS_B, BT, S]), ALU.mult))
                    for b in range(BT):
                        tokens = slice(b * S, (b + 1) * S)
                        step(t, v.tensor_tensor_scan(s.inv_den[:, tokens], one[0:HEADS_B, :].broadcast_to([HEADS_B, S]),
                                                     s.p_t[:, tokens], 0.0, ALU.mult, ALU.add), wait=b == BT - 1)
                    step(t, v.tensor_scalar(s.inv_den, s.inv_den, 1e-4, None, ALU.max))
                    step(t, v.reciprocal(s.inv_den, s.inv_den), p_ready)
                for c in range(IC):
                    for u, s in enumerate(streams):
                        dve.wait_ge(val_copied.sem, val_copied.at(t, c + 1, u))
                        taps(t, s, 0, c, P, val_ready)
                        dve.wait_ge(zg_copied.sem, zg_copied.at(t, c + 1, u))
                        taps(t, s, 1, IC + c, P, gconv_ready)
                    for u, s in enumerate(streams):
                        dve.wait_ge(phi_ready.sem, phi_ready.at(t, c + 1, u))
                        step(t, v.tensor_scalar(s.turns, s.phi, 1.0 / TWO_PI, MAGIC, ALU.mult, ALU.add))
                        step(t, v.tensor_scalar(s.turns, s.turns, MAGIC, None, ALU.subtract))
                        step(t, v.scalar_tensor_tensor(s.phi, s.turns, -TWO_PI_HI, s.phi, ALU.mult, ALU.add))
                        step(t, v.scalar_tensor_tensor(s.angle, s.turns, -TWO_PI_LO, s.phi, ALU.mult, ALU.add))
                        step(t, v.tensor_scalar(s.angle, s.angle, PI_SAFE, -PI_SAFE, ALU.min, ALU.max), angle_ready)
                    for u, s in enumerate(streams):
                        val = s.conv[0]
                        step(t, v.tensor_scalar(s.turns, val, deriv[:, 3:4], deriv[:, 1:2], ALU.mult, ALU.add))
                        step(t, v.tensor_tensor(s.turns, s.turns, val, ALU.mult))
                        dve.wait_ge(pe_p_rows.sem, pe_p_rows.at(t, c + 1, u))
                        step(t, v.scalar_tensor_tensor(s.phi, s.turns, deriv[:, 0:1], s.bank(2), ALU.add, ALU.mult),
                             wait=False)
                        dve.wait_ge(gtanh_ready.sem, gtanh_ready.at(t, c + 1, u))
                        step(t, v.scalar_tensor_tensor(s.gate_s, s.gtanh, 1.0, s.conv[1], ALU.add, ALU.mult))
                        dve.wait_ge(trig_ready.sem, trig_ready.at(t, c + 1, u))
                        step(t, v.tensor_tensor(s.cos_t, s.phi, s.cos_t, ALU.mult), wait=False)
                        step(t, v.tensor_tensor(s.sin_t, s.phi, s.sin_t, ALU.mult))
                        for mean, part in ((s.mean_re, s.cos_t), (s.mean_im, s.sin_t)):
                            for b in range(BT):
                                tokens = slice(b * S, (b + 1) * S)
                                step(t, v.tensor_tensor_scan(mean[:, tokens], one.broadcast_to([P, S]), part[:, tokens],
                                                             0.0, ALU.mult, ALU.add),
                                     wait=mean is s.mean_im and b == BT - 1)
                        step(t, v.tensor_tensor(s.mean_re, s.mean_re, s.bank(0), ALU.mult), wait=False)
                        step(t, v.tensor_tensor(s.mean_im, s.mean_im, s.bank(0), ALU.mult), mean_ready)
                    for u, s in enumerate(streams):
                        dve.wait_ge(pe_y.sem, pe_y.at(t, c + 1, u))
                        step(t, v.tensor_tensor(s.yg[:, c, :], s.bank(1), s.gate_s, ALU.mult), yg_ready)
                for u, s in enumerate(streams):
                    dve.wait_ge(rms_sqrt.sem, rms_sqrt.at(t, 1, u))
                    step(t, v.reciprocal(s.rms_b, s.rms_b), rms_ready)
                for u, s in enumerate(streams):
                    dve.wait_ge(pe_rms_rows.sem, pe_rms_rows.at(t, 1, u))
                    step(t, v.tensor_tensor(s.yg, s.yg, s.bank(0, 4), ALU.mult), ynorm_ready)
                for u, s in enumerate(streams):
                    dve.wait_ge(pe_proj.sem, pe_proj.at(t, 1, u))
                    step(t, v.tensor_tensor(s.x, s.x, s.bank(0, 2), ALU.add), x1_ready)

            def pool_prompt(t):
                for u, s in enumerate(streams):
                    now = s.sm(600, 3 * BT)
                    step(t, v.tensor_copy(now.rearrange("p (b k) -> p b k", b=BT), kind[:, bass.ds((t * 2 + u) * BT, BT), :]))
                for u, s in enumerate(streams):
                    for b in range(BT):
                        cnt = s.sm(56 + 2 * b, 2)
                        step(t, v.tensor_scalar(cnt, w["pool_count"][:, 0, :], s.sm(600 + 3 * b, 1), None, ALU.mult))
                        for k in (1, 2):
                            step(t, v.scalar_tensor_tensor(cnt, w["pool_count"][:, k, :], s.sm(600 + 3 * b + k, 1), cnt,
                                                           ALU.mult, ALU.add))
                for u, s in enumerate(streams):
                    dve.wait_ge(pe_score.sem, pe_score.at(t, 1, u))
                    for b in range(BT):
                        dst = s.masked[:, 2 * b:2 * b + 2, :]
                        for k in range(3):
                            src = s.bank(1)[:, b * S:(b + 1) * S][:, None, :].broadcast_to([P, 2, S]) if k == 0 else dst
                            step(t, v.scalar_tensor_tensor(dst, pool_mask[:, k, :, :], s.sm(600 + 3 * b + k, 1), src,
                                                           ALU.mult, ALU.add))
                    step(t, v.tensor_reduce(out=s.sm(8, 4), in_=s.masked, axis=AX.X, op=ALU.max, negate=True), score_max)
                for u, s in enumerate(streams):
                    dve.wait_ge(pool_exp.sem, pool_exp.at(t, 1, u))
                    step(t, v.tensor_tensor(s.sm(12, 4), s.sm(12, 4), s.sm(56, 4), ALU.mult))
                    step(t, v.reciprocal(s.sm(12, 4), s.sm(12, 4)))
                    for g in range(4):
                        step(t, v.tensor_scalar(s.pool_w[:, g, :], s.pool_w[:, g, :], s.sm(12 + g, 1), None, ALU.mult),
                             pool_p if g == 3 else None)

            def route(t):
                number = w["expert_no"][:, :, :]
                top1, top2, which, e2, w1, w2 = 164, 168, 172, 160, 176, 180
                for u, s in enumerate(streams):
                    def cols(at):
                        return s.sm(at, NS * NE).rearrange("p (s e) -> p s e", s=NS)

                    def wide(at):
                        return s.sm(at, NS)[:, :, None].broadcast_to([P, NS, NE])

                    score, tmp, first, second = cols(64), cols(128), cols(256), cols(288)
                    dve.wait_ge(pe_route.sem, pe_route.at(t, 1, u))
                    step(t, v.tensor_copy(score, s.bank(0)[:, 0:NS * NE].rearrange("p (s e) -> p s e", s=NS)))
                    for top, onehot in ((top1, first), (top2, second)):
                        step(t, v.tensor_reduce(out=s.sm(top, NS), in_=score, axis=AX.X, op=ALU.max))
                        step(t, v.tensor_tensor(tmp, score, wide(top), ALU.is_lt))
                        step(t, v.scalar_tensor_tensor(tmp, tmp, float(NE), number, ALU.mult, ALU.add))
                        step(t, v.tensor_reduce(out=s.sm(which, NS), in_=tmp, axis=AX.X, op=ALU.min))
                        step(t, v.tensor_tensor(onehot, number, wide(which), ALU.is_equal))
                        if top == top1:
                            step(t, v.scalar_tensor_tensor(score, first, -3e38, score, ALU.mult, ALU.add))
                    step(t, v.tensor_tensor(s.sm(e2, NS), s.sm(top2, NS), s.sm(top1, NS), ALU.subtract), top_ready)
                for u, s in enumerate(streams):
                    dve.wait_ge(route_exp.sem, route_exp.at(t, 1, u))
                    step(t, v.tensor_scalar(s.sm(w1, NS), s.sm(e2, NS), 1.0, None, ALU.add))
                    step(t, v.reciprocal(s.sm(w1, NS), s.sm(w1, NS)))
                    step(t, v.tensor_tensor(s.sm(w2, NS), s.sm(e2, NS), s.sm(w1, NS), ALU.mult))
                for u, s in enumerate(streams):
                    at = bass.ds((t * 2 + u) * NS, NS)
                    step(t, v.tensor_copy(shares[:, :, at], s.sm(w1, 2 * NS)[:, 0:2 * NS].rearrange("p (c s) -> p c s", c=2)))
                    step(t, v.tensor_copy(picks[:, :, at, :],
                                          s.sm(256, 2 * NS * NE).rearrange("p (c s e) -> p c s e", c=2, s=NS)), picks_ready)

            def order():
                def sort(ins):
                    sort_dve.given += 1
                    ins.then_inc(sort_dve.sem, 1)
                    dve.wait_ge(sort_dve.sem, sort_dve.given)

                N = NE * BLOCKS
                a, b = streams[0].sm, streams[1].sm

                def cols(t):
                    return t.rearrange("p (e k) -> p e k", e=NE)

                both, count, run, tmp = a(0, N), a(N, N), a(2 * N, N), a(3 * N, N)
                total, blocks, end, shift = (b(NE * k, NE) for k in range(4))
                sort(v.tensor_tensor(both.rearrange("p (e k) -> p k e", e=NE), picks[:, 0, :, :], picks[:, 1, :, :], ALU.add))
                dve.wait_ge(sort_pe.sem, 2)
                sort(v.tensor_copy(count, psum[:, 1, 0:N]))
                one = w["ones"][:, 0:1].broadcast_to([P, N])
                sort(v.tensor_tensor_scan(run, one, count, 0.0, ALU.mult, ALU.add))
                sort(v.tensor_reduce(out=total, in_=cols(count), axis=AX.X, op=ALU.add))
                sort(v.tensor_scalar(blocks, total, 1.0 / P, (P - 1) / P - 0.5 + 0.5 / P, ALU.mult, ALU.add))
                sort(round_to_even(blocks, blocks))
                sort(v.tensor_tensor_scan(end, one[:, 0:NE], blocks, 0.0, ALU.mult, ALU.add))
                sort(v.tensor_tensor(shift, end, blocks, ALU.subtract))
                sort(v.tensor_scalar(shift, shift, float(P), None, ALU.mult))
                sort(v.tensor_tensor(shift, shift, total, ALU.add))
                sort(v.tensor_tensor(shift, shift, cols(run)[:, :, BLOCKS - 1], ALU.subtract))
                sort(v.tensor_tensor(run, run, count, ALU.subtract))
                sort(v.tensor_tensor(run, run, psum[:, 0, 0:N], ALU.add))
                sort(v.tensor_tensor(cols(run), cols(run), shift[:, :, None].broadcast_to([P, NE, BLOCKS]), ALU.add))
                for c in range(2):
                    sort(v.tensor_tensor(cols(tmp), cols(run), picks[:, c, :, :].rearrange("p k e -> p e k"), ALU.mult))
                    sort(v.tensor_reduce(out=b(64, BLOCKS), in_=tmp.rearrange("p (e k) -> p k e", e=NE), axis=AX.X, op=ALU.add))
                    sort(v.tensor_copy(slots[:, c, :], b(64, BLOCKS)))
                ended = b(128, SLOTS * (NE - 1), 1).rearrange("p (j e) -> p j e", j=SLOTS)
                dve.wait_ge(order_in.sem, 32)
                sort(v.tensor_tensor(ended, slot_block,
                                     end[0:1, None, 0:NE - 1].broadcast_to([1, SLOTS, NE - 1]), ALU.is_ge))
                sort(v.tensor_reduce(out=b(416, SLOTS, 1), in_=ended, axis=AX.X, op=ALU.add))
                sort(v.tensor_scalar(b(416, SLOTS, 1), b(416, SLOTS, 1), 1.0, None, ALU.add))
                sort(v.tensor_copy(slot_expert[:, :], b(416, SLOTS, 1)))

            def shared_expert(t):
                for u in (0, 1):
                    dve.wait_ge(rows_got[u].sem, rows_got[u].at(t, 16))
                    step(t, v.tensor_copy(slots_now[u][:, :, :], slots[:, :, bass.ds((t * 2 + u) * NS, NS)]), slots_now_ready)
                for u in (0, 1):
                    for m in range(FC):
                        n = u * FC + m
                        dve.wait_ge(h_tanh.sem, h_tanh.at(t, n + 1))
                        step(t, v.scalar_tensor_tensor(act_h[n % 2], act_h[n % 2], 1.0, psum[:, 3 + n % 2, :],
                                                       ALU.add, ALU.mult), h_read)
                        step(t, v.scalar_tensor_tensor(g_buf[:, m, :], act_h[n % 2], 0.5, psum[:, 5 + n % 2, :],
                                                       ALU.mult, ALU.mult), g_ready)
                    dve.wait_ge(pe_down.sem, pe_down.at(t, u + 1))
                    x1 = x1_in[u]
                    v.tensor_tensor(x1[:, 0, :], x1[:, 0, :], psum[:, 0, :], ALU.add)
                    step(t, v.tensor_tensor(x1[:, 1, :], x1[:, 1, :], psum[:, 7, :], ALU.add), x2_ready)

            def slot_gate(i, k):
                q = k % 2
                dve.wait_ge(slot_tanh.sem, slot_tanh.at(i, k + 1))
                v.scalar_tensor_tensor(slot_h[q], slot_h[q], 1.0, psum[:, q, :], ALU.add, ALU.mult) \
                    .then_inc(slot_h_ready.sem, 1)
                dve.wait_ge(slot_h_ready.sem, slot_h_ready.at(i, k + 1))
                dve.wait_ge(pe_slot_u.sem, pe_slot_u.at(i, k + 1))
                v.scalar_tensor_tensor(slot_g[q], slot_h[q], 0.5, psum[:, 2 + q, :], ALU.mult, ALU.mult) \
                    .then_inc(slot_g_ready.sem, 1)

            def slot_tokens(i, k):
                dve.wait_ge(pe_slot_t.sem, pe_slot_t.at(i, k + 1))
                v.tensor_copy(slot_t[:, k % 2, :, :], psum[:, 5, 0:D].rearrange("p (c n) -> p c n", c=DC)) \
                    .then_inc(slot_t_ready.sem, 1)

            def picked(t):
                for u, s in enumerate(streams):
                    at = bass.ds((t * 2 + u) * NS, NS)
                    step(t, v.tensor_copy(s.sm(608, 2 * NS).rearrange("p (c s) -> p c s", c=2), shares[:, :, at]))
                    step(t, v.tensor_copy(slots_now[u][:, :, :], slots[:, :, at]), picked_slots)
                for u, s in enumerate(streams):
                    dve.wait_ge(gathered[u].sem, gathered[u].at(t, 2 * NS * 16))
                    for c in range(2):
                        for k in range(NS):
                            row, share, end = s.picked[0][:, k, :], s.sm(608 + NS * c + k, 1), k == NS - 1
                            if c == 0:
                                step(t, v.tensor_scalar(row, row, share, None, ALU.mult), wait=end)
                            else:
                                step(t, v.scalar_tensor_tensor(row, s.picked[1][:, k, :], share, row, ALU.mult, ALU.add),
                                     picked_sum if end else None, wait=end)
                for u, s in enumerate(streams):
                    dve.wait_ge(pe_picked_t.sem, pe_picked_t.at(t, 1, u))
                    dve.wait_ge(x2_in[u].sem, x2_in[u].at(t, 16))
                    step(t, v.tensor_tensor(s.x, s.x, s.bank(0, 2), ALU.add), x2_whole)

            def adapter(t):
                for u, s in enumerate(streams):
                    dve.wait_ge(pe_adapt.sem, pe_adapt.at(t, 1, u))
                    row_stats(t, s, s.token_banks(1), adapt_stats)
                for u, s in enumerate(streams):
                    dve.wait_ge(adapt_std.sem, adapt_std.at(t, 1, u))
                    step(t, v.reciprocal(s.sm(4, NS), s.sm(0, NS)))
                    for k in range(NS):
                        step(t, v.tensor_scalar(s.attn_in[:, k, :], s.token_banks(1)[:, k, :], s.stat[:, k, 0:1],
                                                s.sm(4 + k, 1), ALU.subtract, ALU.mult), wait=k == NS - 1)
                    dve.wait_ge(own_in[u].sem, own_in[u].at(t, 8 * BT * 16))
                    for k, op in ((0, ALU.mult), (1, ALU.add)):
                        for b in range(BT):
                            mine = s.attn_in[:, 2 * b:2 * b + 2, :]
                            row = s.adapt_rows[:, k, b, :][:, None, :].broadcast_to([P, 2, D])
                            step(t, v.tensor_tensor(mine, mine, row, op), adapt_ready if (b, k) == (1, 1) else None)

            def to_integers(t, s, rows, g, dst, scale_at, last):
                row = g_rows[:, g, :][:, None, :].broadcast_to([P, NS, D])
                step(t, v.tensor_tensor(s.scaled_in, rows, row, ALU.mult))
                top, scale, r = s.sm(212, NS), s.sm(scale_at, NS), s.sm(208, NS)
                step(t, v.tensor_reduce(out=top, in_=s.scaled_in, axis=AX.X, op=ALU.max, apply_absolute_value=True))
                step(t, v.tensor_tensor(top, top, r, ALU.mult))
                step(t, v.tensor_scalar(scale, top, 1e-5, 1.0 / 127, ALU.max, ALU.mult))
                step(t, v.reciprocal(top, scale))
                step(t, v.tensor_tensor(top, top, r, ALU.mult))
                step(t, v.tensor_tensor(s.scaled_in, s.scaled_in, top[:, :, None].broadcast_to([P, NS, D]), ALU.mult))
                step(t, round_to_even(dst, s.scaled_in), last)

            def diagonals(t, s, at, last):
                for k in range(NS):
                    end = k == NS - 1
                    step(t, v.tensor_scalar(s.row_diag[:, k, :], w["ident"][:, :], s.sm(at + k, 1), None, ALU.mult),
                         last if end else None, wait=end)

            def attention(t):
                dve.wait_ge(g_rows_in.sem, 16)
                for g in range(3):
                    for u, s in enumerate(streams):
                        if g == 0:
                            dve.wait_ge(rms_in.sem, rms_in.at(t, 1, u))
                            step(t, v.reciprocal(s.sm(208, NS), s.sm(204, NS)))
                        else:
                            dve.wait_ge(pe_int_t.sem, pe_int_t.at(t, g, u))
                        to_integers(t, s, s.attn_in, g, s.int_rows, 224 + 4 * g, int_ready)
                        if g == 0:
                            step(t, v.tensor_scalar(s.sm(216, NS), s.sm(224, NS), qk_scale[:, 0:1], None, ALU.mult))
                            step(t, v.tensor_scalar(s.sm(220, NS), s.sm(216, NS), -1.0, None, ALU.mult))
                        if g == 1:
                            diagonals(t, s, 228, diag_ready)
                        if g == 2:
                            step(t, v.tensor_scalar(s.sm(232, NS), s.sm(232, NS), w_scale[:, 2:3], None, ALU.mult))
                for u, s in enumerate(streams):
                    dve.wait_ge(pe_k.sem, pe_k.at(t, 1, u))
                    dve.wait_ge(scale_ready.sem, scale_ready.at(t, 1, u))
                    step(t, v.tensor_tensor(s.k_t, s.bank(0, 4), s.kscale_b[:, None, :].broadcast_to([P, 4, T]), ALU.mult),
                         k_ready)
                for u, s in enumerate(streams):
                    dve.wait_ge(pe_v.sem, pe_v.at(t, 1, u))
                    for k in range(NS):
                        end = k == NS - 1
                        step(t, v.tensor_scalar(s.v_rows[:, k, :], s.token_banks(2)[:, k, :], s.sm(232 + k, 1), None,
                                                ALU.mult), v_ready if end else None, wait=end)

                def maxima(n, u, s):
                    g = group(n)
                    dve.wait_ge(pe_logits.sem, pe_logits.at(t, n + 1, u))
                    at, per = g.s * NH, len(g.heads)
                    raw = s.sm(448 + at, NH)[:, g.heads[0]:g.heads[-1] + 1:4]
                    step(t, v.tensor_reduce(out=raw, in_=s.bank(n % 2).rearrange("p (j k) -> p j k", j=per),
                                            axis=AX.X, op=ALU.max))
                    step(t, v.tensor_scalar(s.sm(320 + at, NH)[:, g.heads[0]:g.heads[-1] + 1:4], raw,
                                            s.sm(220 + g.s, 1), None, ALU.mult), row_max)

                def probs_t_out(n, u, s):
                    g = group(n)
                    dve.wait_ge(pe_probs_t.sem, pe_probs_t.at(t, n + 1, u))
                    if n >= 2:
                        dve.wait_ge(pe_heads.sem, pe_heads.at(t, n - 1, u))
                    step(t, v.tensor_copy(s.probs_tt[n % 2], s.bank(2)), probs_t)

                def quotients(n, u, s):
                    g = group(n)
                    if g.last:
                        dve.wait_ge(pe_heads.sem, pe_heads.at(t, n + 1, u))
                        sums = s.sm(512 + g.s * NH, NH)
                        step(t, v.reciprocal(sums, s.sm(384 + g.s * NH, NH)))
                        step(t, v.tensor_tensor(s.head_out[:, g.s, :].rearrange("p (h d) -> p h d", h=NH),
                                                s.bank(3)[:, (g.s % 2) * D:(g.s % 2 + 1) * D].rearrange("p (h d) -> p h d", h=NH),
                                                sums[:, :, None].broadcast_to([P, NH, HD]), ALU.mult), heads_ready)

                for u, s in enumerate(streams):
                    maxima(0, u, s)
                for n in range(NG):
                    if n + 1 < NG:
                        for u, s in enumerate(streams):
                            maxima(n + 1, u, s)
                    for u, s in enumerate(streams):
                        probs_t_out(n, u, s)
                    if n:
                        for u, s in enumerate(streams):
                            quotients(n - 1, u, s)
                for u, s in enumerate(streams):
                    quotients(NG - 1, u, s)
                for u, s in enumerate(streams):
                    dve.wait_ge(rms_in.sem, rms_in.at(t, 2, u))
                    step(t, v.reciprocal(s.sm(208, NS), s.sm(204, NS)))
                    to_integers(t, s, s.head_out, 3, s.y_rows, 236, int_ready)
                    step(t, v.tensor_scalar(s.sm(236, NS), s.sm(236, NS), w_scale[:, 3:4], None, ALU.mult))
                    diagonals(t, s, 236, diag_ready)
                for u, s in enumerate(streams):
                    dve.wait_ge(scale_ready.sem, scale_ready.at(t, 2, u))
                    dve.wait_ge(pe_o.sem, pe_o.at(t, 1, u))
                    step(t, v.tensor_tensor(s.f8_a[:, 0, :], s.bank(3), s.yscale_b, ALU.mult), wait=False)
                    step(t, v.tensor_tensor(s.f8_a[:, 1, :], s.bank(0), s.yscale_b, ALU.mult))
                    step(t, v.tensor_tensor(s.x, s.x, s.f8_a, ALU.add), x3_ready)

            def last_ffn(t):
                for u, s in enumerate(streams):
                    dve.wait_ge(pe_cat.sem, pe_cat.at(t, 1, u))
                    for c in range(DC):
                        for b in range(BT):
                            tokens = slice(b * S, (b + 1) * S)
                            step(t, v.tensor_scalar(s.f8_a[:, c, tokens], s.bank(1 + c)[:, tokens], s.cat_b[:, b, c:c + 1],
                                                    None, ALU.add), wait=(c, b) == (DC - 1, BT - 1))
                    given = []

                    def run(ins):
                        given.append(ins)
                        step(t, ins, f8_ready if len(given) == 5 else None)

                    float8_values(run, *(z.rearrange("p c n -> p (c n)") for z in (s.f8_a, s.f8_b, s.f8_q)))
                for u, s in enumerate(streams):
                    dve.wait_ge(half_ready.sem, half_ready.at(t, 1, u))
                    for c in range(DC):
                        end = c == DC - 1
                        step(t, v.scalar_tensor_tensor(s.out_t[:, c, :], s.half_t[:, c, :], col("fbias", c), s.x[:, c, :],
                                                       ALU.add, ALU.add), out_ready if end else None, wait=end)

            with dve.Fori(0, PAIRS) as t:
                condition(t)
                scan_attention(t)
                pool_prompt(t)
                route(t)
            order()
            with dve.Fori(0, PAIRS) as t:
                shared_expert(t)
            slot_tokens(0, 0)
            slot_gate(0, 0)
            slot_tokens(0, 1)
            with dve.Fori(0, SLOT_PAIRS - 1) as i:
                for k in (1, 2):
                    slot_gate(i, k)
                    slot_tokens(i, k + 1)
            slot_gate(SLOT_PAIRS - 1, 1)
            chain = dve_chain_3
            with dve.Fori(0, PAIRS) as t:
                picked(t)
                adapter(t)
                attention(t)
                last_ffn(t)

        @block.tensor
        def _(pe):
            mm = nc.tensor.matmul

            def add_up(dst, pairs):
                for k, (lhs, rhs) in enumerate(pairs):
                    ins = mm(dst, lhs, rhs, start=k == 0, stop=k == len(pairs) - 1)
                return ins

            dve_sums = setup_dve
            pe.wait_ge(dve_sums.sem, DVE_SUMS)
            pe.wait_ge(loads["early"].sem, 16 * N_EARLY)
            mm(psum[:, 0, 0:4], w["ones"][:, 0:1].broadcast_to([P, P]), sm(44, 4), start=True, stop=True).then_inc(setup_pe.sem, 1)
            pe.wait_ge(setup_dve.sem, DVE_SUMS + 1)

            def condition(t):
                for u, s in enumerate(streams):
                    pe.wait_ge(x_in[u].sem, x_in[u].at(t, 16))
                    pe.wait_ge(picks_ready.sem, picks_ready.at(t, 0, u))
                    add_up(s.bank(0, p=HID), [(w["w_n1"][:, c, :], s.x[:, c, :]) for c in range(DC)])
                    for e in range(DC):
                        ins = add_up(s.bank(1 + e), [(w["w_soma"][:, c, e * P:(e + 1) * P], s.x[:, c, :]) for c in range(DC)])
                    ins.then_inc(pe_soma.sem, 1)
                for u, s in enumerate(streams):
                    pe.wait_ge(ctx_ready.sem, ctx_ready.at(t, 1, u))
                    pe.wait_ge(h1_ready.sem, h1_ready.at(t, 1, u))
                    for e, bank in ((0, 3), (1, 0)):
                        cols = slice(e * P, (e + 1) * P)
                        if e == 1:
                            pe.wait_ge(soma_ready.sem, soma_ready.at(t, 1, u))
                        ins = add_up(s.bank(bank), [(w["w_g"][:, c, cols], s.x[:, c, :]) for c in range(DC)]
                                     + [(w["w_g"][:, DC + c, cols], s.ctx_t[:, c, :]) for c in range(DC)])
                    ins.then_inc(pe_gate.sem, 1)
                    mm(s.bank(1, p=ND), w["w_n2"][:, :], s.h1, start=True, stop=True).then_inc(pe_mod.sem, 1)

                def mod_rows(s, d):
                    mm(s.bank(2 + d % 2), w["ident"][0:ND, d:d + 1].broadcast_to([ND, P]), s.mod,
                       start=True, stop=True).then_inc(pe_mod_rows.sem, 1)

                for u, s in enumerate(streams):
                    pe.wait_ge(mod_ready.sem, mod_ready.at(t, 1, u))
                    mod_rows(s, 0)
                for s in streams:
                    mod_rows(s, 1)
                for d in range(ND):
                    for u, s in enumerate(streams):
                        pe.wait_ge(trace_ready.sem, trace_ready.at(t, d + 1, u))
                        for c in range(DC):
                            ins = mm(s.bank(c), w["ident"][:, :], s.trace[d % 2][:, c, :], start=d == 0, stop=d == ND - 1,
                                     skip_group_check=True)
                        ins.then_inc(pe_trace_used.sem, 1)
                        if d + 2 < ND:
                            mod_rows(s, d + 2)
                for u, s in enumerate(streams):
                    pe.wait_ge(temporal_ready.sem, temporal_ready.at(t, 1, u))
                    for e in range(DC):
                        ins = add_up(s.bank(2 + e),
                                     [(w["w_temp"][:, c, e * P:(e + 1) * P], s.temporal[:, c, :]) for c in range(DC)])
                    ins.then_inc(pe_temp.sem, 1)
                for u, s in enumerate(streams):
                    pe.wait_ge(mixed_ready.sem, mixed_ready.at(t, 1, u))
                    for k in range(NS):
                        ins = add_up(s.token_banks(0)[:, k, :],
                                     [(s.gate_t[:, c, k * P:(k + 1) * P], w["w_out"][:, c, :]) for c in range(DC)])
                    ins.then_inc(pe_cond.sem, 1)
                for u, s in enumerate(streams):
                    pe.wait_ge(cond_norm.sem, cond_norm.at(t, 1, u))
                    for c in range(DC):
                        for k in range(NS):
                            ins = nc.tensor.transpose(s.bank(2 + c)[:, k * P:(k + 1) * P],
                                                      s.cond_rows[:, k, c * P:(c + 1) * P], w["ident"][:, :])
                    ins.then_inc(pe_cond_t.sem, 1)

            def scan_attention(t):
                def z_part(s, bank, at, width, done):
                    add_up(s.bank(bank, p=width), [(w["w_in"][:, c, at:at + width], s.cond[:, c, :]) for c in range(DC)]) \
                        .then_inc(done.sem, 1)

                def head_rows(s, bank, c, src):
                    return mm(s.bank(bank), w["head_sel"][:, c, :], src, start=True, stop=True)

                for u, s in enumerate(streams):
                    pe.wait_ge(cond_ready.sem, cond_ready.at(t, 1, u))
                    z_part(s, 2, 2 * INNER, HEADS_B, pe_s)
                    z_part(s, 0, 0, P, pe_val)
                    z_part(s, 1, INNER, P, pe_zg)
                for c in range(IC):
                    for u, s in enumerate(streams):
                        if c == 0:
                            pe.wait_ge(p_ready.sem, p_ready.at(t, 1, u))
                        head_rows(s, 2, c, s.p_t)
                        pe.wait_ge(val_copied.sem, val_copied.at(t, c + 1, u))
                        head_rows(s, 0, c, s.inv_den).then_inc(pe_p_rows.sem, 1)
                    for u, s in enumerate(streams):
                        pe.wait_ge(zg_copied.sem, zg_copied.at(t, c + 1, u))
                        pe.wait_ge(mean_ready.sem, mean_ready.at(t, c + 1, u))
                        add_up(s.bank(1), [(w["w_re"][:, :], s.mean_re), (w["w_im"][:, :], s.mean_im)]) \
                            .then_inc(pe_y.sem, 1)
                        if c + 1 < IC:
                            z_part(s, 0, (c + 1) * P, P, pe_val)
                        pe.wait_ge(sq_ready.sem, sq_ready.at(t, c + 1, u))
                        for k, part in enumerate((s.cos_t, s.sin_t)):
                            ins = mm(s.bank(3, p=HEADS_B), w["head_sum"][:, c, :], part, start=c == 0 and k == 0,
                                     stop=c == IC - 1 and k == 1, skip_group_check=True)
                        ins.then_inc(pe_sq.sem, 1)
                        pe.wait_ge(yg_ready.sem, yg_ready.at(t, c + 1, u))
                        if c + 1 < IC:
                            z_part(s, 1, INNER + (c + 1) * P, P, pe_zg)
                for u, s in enumerate(streams):
                    pe.wait_ge(rms_ready.sem, rms_ready.at(t, 1, u))
                    for c in range(IC):
                        ins = head_rows(s, c, c, s.rms_b)
                    ins.then_inc(pe_rms_rows.sem, 1)
                for u, s in enumerate(streams):
                    pe.wait_ge(ynorm_ready.sem, ynorm_ready.at(t, 1, u))
                    for e in range(DC):
                        ins = add_up(s.bank(e), [(w["w_proj"][:, c, e * P:(e + 1) * P], s.yg[:, c, :]) for c in range(IC)])
                    ins.then_inc(pe_proj.sem, 1)

            def pool_prompt(t):
                for u, s in enumerate(streams):
                    pe.wait_ge(x1_ready.sem, x1_ready.at(t, 1, u))
                    for k in range(NS):
                        for c in range(DC):
                            ins = nc.tensor.transpose(s.token_banks(2)[:, k, c * P:(c + 1) * P],
                                                      s.x[:, c, k * P:(k + 1) * P], w["ident"][:, :])
                    ins.then_inc(pe_x1_rows.sem, 1)
                    add_up(s.bank(0, p=HID), [(w["w_1"][:, c, :], s.x[:, c, :]) for c in range(DC)]) \
                        .then_inc(pe_score_hid.sem, 1)
                for u, s in enumerate(streams):
                    pe.wait_ge(score_hid.sem, score_hid.at(t, 1, u))
                    mm(s.bank(1), w["v_col"][:, 0:1].broadcast_to([HID, P]), s.score_h, start=True, stop=True) \
                        .then_inc(pe_score.sem, 1)
                for u, s in enumerate(streams):
                    pe.wait_ge(pool_p.sem, pool_p.at(t, 1, u))
                    for b in range(BT):
                        for l in range(2):
                            for j in range(2):
                                at = l * S + j * P
                                ins = nc.tensor.transpose(s.bank(2 + b)[:, at:at + P],
                                                          s.pool_w[:, 2 * b + j, l * P:(l + 1) * P], w["ident"][:, :])
                    ins.then_inc(pe_pool_t.sem, 1)
                for u, s in enumerate(streams):
                    pe.wait_ge(pool_t.sem, pool_t.at(t, 1, u))
                    for c in range(DC):
                        for b in range(BT):
                            ins = add_up(s.bank(c)[:, b * S:(b + 1) * S],
                                         [(s.x1_rows[:, 2 * b + l, c * P:(c + 1) * P], s.pool_wt[:, b, l * S:(l + 1) * S])
                                          for l in range(2)])
                    ins.then_inc(pe_pool.sem, 1)
                    for k in range(NS):
                        b, at = k // 2, (k % 2) * P
                        ins = add_up(s.token_banks(2)[:, k, :],
                                     [(s.pool_wt[:, b, l * S + at:l * S + at + P], s.x1_rows[:, 2 * b + l, :])
                                      for l in range(2)])
                    ins.then_inc(pe_pool_rows.sem, 1)
                for u, s in enumerate(streams):
                    pe.wait_ge(pool_ready.sem, pool_ready.at(t, 1, u))
                    for k in range(NS):
                        ins = add_up(s.bank(0)[:, k * NE:(k + 1) * NE],
                                     [(s.pooled[:, c, k * P:(k + 1) * P], w["w_route"][:, c, :]) for c in range(DC)])
                    ins.then_inc(pe_route.sem, 1)

            def order():
                both = streams[0].sm(0, NE * BLOCKS)
                pe.wait_ge(order_in.sem, 32)
                pe.wait_ge(sort_dve.sem, 1)
                for bank, what in ((0, earlier), (1, w["ones"][:, 0:1].broadcast_to([P, P]))):
                    mm(psum[:, bank, 0:NE * BLOCKS], what, both, start=True, stop=True).then_inc(sort_pe.sem, 1)

            def shared_expert(t):
                for u in (0, 1):
                    x = pooled_in[u]
                    pe.wait_ge(ffn_in[u].sem, ffn_in[u].at(t, 32))
                    for m in range(FC):
                        n = u * FC + m
                        if n >= 2:
                            pe.wait_ge(h_read.sem, h_read.at(t, n - 1))
                        add_up(psum[:, 3 + n % 2, :], [(up_weight(0, c, m), x[:, c, :]) for c in range(DC)])
                        if n >= 2:
                            pe.wait_ge(g_ready.sem, g_ready.at(t, n - 1))
                        add_up(psum[:, 5 + n % 2, :], [(up_weight(1, c, m), x[:, c, :]) for c in range(DC)]) \
                            .then_inc(pe_up.sem, 1)
                    pe.wait_ge(x2_ready.sem, x2_ready.at(t, u))
                    pe.wait_ge(g_ready.sem, g_ready.at(t, (u + 1) * FC))
                    for c, bank in ((0, 0), (1, 7)):
                        ins = add_up(psum[:, bank, :], [(down_weight(m, c), g_buf[:, m, :]) for m in range(FC)])
                    ins.then_inc(pe_down.sem, 1)

            def slot_turn(i, k):
                pe.wait_ge(slot_rows_in[k % 2].sem, slot_rows_in[k % 2].at(i, 16 * (k // 2 + 1)))
                for c in range(DC):
                    ins = nc.tensor.transpose(psum[:, 5, c * P:(c + 1) * P], slot_rows[:, k % 2, c * P:(c + 1) * P],
                                              w["ident"][:, :])
                ins.then_inc(pe_slot_t.sem, 1)

            def slot_up(i, k, which, done):
                expert = pe.value_load(slot_expert[0:1, bass.ds(i * 2 + k, 1)])
                if which == 0:
                    pe.wait_ge(slot_t_ready.sem, slot_t_ready.at(i, k + 1))
                add_up(psum[:, 2 * which + k % 2, :],
                       [(slot_t[:, k % 2, c, :], routed_weight(expert, (which * DC + c) * FF, FF)) for c in range(DC)]) \
                    .then_inc(done.sem, 1)

            def slot_turn_g(i, k):
                pe.wait_ge(slot_g_ready.sem, slot_g_ready.at(i, k + 1))
                for m in range(FC):
                    ins = nc.tensor.transpose(psum[:, 4, m * P:(m + 1) * P], slot_g[k % 2][:, m * P:(m + 1) * P],
                                              w["ident"][:, :])
                ins.then_inc(pe_slot_g_t.sem, 1)

            def slot_down(i, k):
                expert = pe.value_load(slot_expert[0:1, bass.ds(i * 2 + k, 1)])
                pe.wait_ge(slot_out_ready.sem, slot_out_ready.at(i, k))
                pe.wait_ge(slot_g_t_ready.sem, slot_g_t_ready.at(i, k + 1))
                add_up(psum[:, 6, 0:D],
                       [(slot_g_t[k % 2][:, m, :], routed_weight(expert, 2 * DC * FF + m * D, D)) for m in range(FC)]) \
                    .then_inc(pe_slot_out.sem, 1)

            def slot_step(i, k, last=False):
                slot_up(i, k, 0, pe_slot_h)
                slot_turn_g(i, k - 1)
                slot_up(i, k, 1, pe_slot_u)
                if not last:
                    slot_turn(i, k + 1)
                slot_down(i, k - 1)

            def picked(t):
                for u, s in enumerate(streams):
                    pe.wait_ge(out_ready.sem, out_ready.at(t, 0, u))
                    pe.wait_ge(picked_sum.sem, picked_sum.at(t, 1, u))
                    for c in range(DC):
                        for k in range(NS):
                            ins = nc.tensor.transpose(s.bank(c)[:, k * P:(k + 1) * P],
                                                      s.picked[0][:, k, c * P:(c + 1) * P], w["ident"][:, :])
                    ins.then_inc(pe_picked_t.sem, 1)

            def adapter(t):
                for u, s in enumerate(streams):
                    pe.wait_ge(x2_whole.sem, x2_whole.at(t, 1, u))
                    pe.wait_ge(own_in[u].sem, own_in[u].at(t, 8 * BT * 16))
                    for b in range(BT):
                        tokens = slice(b * S, (b + 1) * S)
                        ins = add_up(s.bank(0)[:, tokens], [(s.adapt_down[:, b, c, :], s.x[:, c, tokens]) for c in range(DC)])
                    ins.then_inc(pe_bottle.sem, 1)
                for u, s in enumerate(streams):
                    pe.wait_ge(bottle_ready.sem, bottle_ready.at(t, 1, u))
                    for k in range(NS):
                        tokens = slice(k * P, (k + 1) * P)
                        dst = s.token_banks(1)[:, k, :]
                        for c in range(DC):
                            mm(dst[:, c * P:(c + 1) * P], s.x[:, c, tokens], w["ident"][:, :], start=c == 0, stop=False,
                               skip_group_check=True)
                        mm(dst, w["ones"][0:1, 0:1].broadcast_to([1, P]), s.adapt_bu[:, k // 2, :], start=False, stop=False,
                           skip_group_check=True)
                        ins = mm(dst, s.bottle[:, tokens], s.adapt_up[:, k // 2, :], start=False, stop=True,
                                 skip_group_check=True)
                    ins.then_inc(pe_adapt.sem, 1)

            def integers_t(s, rows):
                for c in range(DC):
                    for k in range(NS):
                        ins = nc.tensor.transpose(s.bank_b(c, 1)[:, 0, k * P:(k + 1) * P], rows[:, k, c * P:(c + 1) * P],
                                                  ident_b[:, :])
                return ins

            def attention(t):
                for g in range(3):
                    for u, s in enumerate(streams):
                        pe.wait_ge(int_ready.sem, int_ready.at(t, g + 1, u))
                        if g == 1:
                            pe.wait_ge(q_ready.sem, q_ready.at(t, 1, u))
                        if g == 2:
                            pe.wait_ge(k_ready.sem, k_ready.at(t, 1, u))
                        integers_t(s, s.int_rows).then_inc(pe_int_t.sem, 1)
                        if g == 1:
                            pe.wait_ge(diag_ready.sem, diag_ready.at(t, 1, u))
                            mm(s.bank(2), w["ones"][:, 0:1].broadcast_to([P, P]), s.row_diag.rearrange("p s q -> p (s q)"),
                               start=True, stop=True).then_inc(pe_scale.sem, 1)
                    for u, s in enumerate(streams):
                        pe.wait_ge(int_t.sem, int_t.at(t, g + 1, u))
                        if g == 1:
                            pe.wait_ge(scale_ready.sem, scale_ready.at(t, 1, u))
                        if g < 2:
                            for k in range(4):
                                ins = add_up(s.bank(k), [(tern_qk[:, g, c, k * P:(k + 1) * P], s.int_tt[:, c, :])
                                                         for c in range(DC)])
                            ins.then_inc((pe_q, pe_k)[g].sem, 1)
                        else:
                            for k in range(NS):
                                ins = add_up(s.token_banks(2)[:, k, :],
                                             [(s.int_tt[:, c, k * P:(k + 1) * P], tern_vo[:, 0, c, :]) for c in range(DC)])
                            ins.then_inc(pe_v.sem, 1)

                def logits(n, u, s):
                    g = group(n)
                    if n == 0:
                        pe.wait_ge(v_ready.sem, v_ready.at(t, 1, u))
                    if n >= 2:
                        pe.wait_ge(probs_ready.sem, probs_ready.at(t, n - 1, u))
                    bank = s.bank(n % 2)
                    per = len(g.heads)
                    mm(bank.rearrange("p (j k) -> p j k", j=per)[:, :, g.width - P:], ident_b[:, :],
                       causal_a[:, 0:per * P].rearrange("p (j k) -> p j k", j=per), start=True, stop=False,
                       skip_group_check=True)
                    for j, head in enumerate(g.heads):
                        lanes = slice(32 * (head % 4), 32 * (head % 4) + 32)
                        ins = mm(bank[:, j * g.width:(j + 1) * g.width], s.q_t[lanes, head // 4, g.s * P:(g.s + 1) * P],
                                 s.k_t[lanes, head // 4, g.b * S:g.b * S + g.width], start=False, stop=j == per - 1,
                                 skip_group_check=True)
                    ins.then_inc(pe_logits.sem, 1)

                def transposed(n, u, s):
                    pe.wait_ge(probs_ready.sem, probs_ready.at(t, n + 1, u))
                    if n:
                        pe.wait_ge(probs_t.sem, probs_t.at(t, n, u))
                    for k in range(4):
                        ins = nc.tensor.transpose(s.bank(2)[:, k * P:(k + 1) * P], s.probs[n % 2][:, k * P:(k + 1) * P],
                                                  w["ident"][:, :])
                    ins.then_inc(pe_probs_t.sem, 1)

                def weighted(n, u, s):
                    g = group(n)
                    pe.wait_ge(probs_t.sem, probs_t.at(t, n + 1, u))
                    if g.first and g.s:
                        pe.wait_ge(heads_ready.sem, heads_ready.at(t, g.s, u))
                    for j, head in enumerate(g.heads):
                        for kc in range(g.width // P):
                            at = j * g.width + kc * P
                            col0 = (g.s % 2) * D + head * HD
                            ins = mm(s.bank(3)[:, col0:col0 + HD], s.probs_tt[n % 2][:, at:at + P],
                                     s.v_rows[:, 2 * g.b + kc, head * HD:(head + 1) * HD], start=kc == 0,
                                     stop=kc == g.width // P - 1)
                    ins.then_inc(pe_heads.sem, 1)

                for u, s in enumerate(streams):
                    logits(0, u, s)
                for n in range(NG):
                    if n + 1 < NG:
                        for u, s in enumerate(streams):
                            logits(n + 1, u, s)
                    for u, s in enumerate(streams):
                        transposed(n, u, s)
                    for u, s in enumerate(streams):
                        weighted(n, u, s)
                for u, s in enumerate(streams):
                    pe.wait_ge(int_ready.sem, int_ready.at(t, 4, u))
                    integers_t(s, s.y_rows).then_inc(pe_int_t.sem, 1)
                    pe.wait_ge(diag_ready.sem, diag_ready.at(t, 2, u))
                    mm(s.bank(2), w["ones"][:, 0:1].broadcast_to([P, P]), s.row_diag.rearrange("p s q -> p (s q)"),
                       start=True, stop=True).then_inc(pe_scale.sem, 1)
                for u, s in enumerate(streams):
                    pe.wait_ge(int_t.sem, int_t.at(t, 4, u))
                    for e, bank in ((0, 3), (1, 0)):
                        ins = add_up(s.bank(bank), [(tern_vo[:, 1, c, e * P:(e + 1) * P], s.y_tt[:, c, :]) for c in range(DC)])
                    ins.then_inc(pe_o.sem, 1)

            def last_ffn(t):
                for u, s in enumerate(streams):
                    pe.wait_ge(x3_ready.sem, x3_ready.at(t, 1, u))
                    for e in range(DC):
                        for b in range(BT):
                            tokens = slice(b * S, (b + 1) * S)
                            ins = add_up(s.bank(1 + e)[:, tokens],
                                         [(s.cat_w[:, b, c, e * P:(e + 1) * P], s.x[:, c, tokens]) for c in range(DC)])
                    ins.then_inc(pe_cat.sem, 1)
                for u, s in enumerate(streams):
                    pe.wait_ge(f8_ready.sem, f8_ready.at(t, 1, u))
                    for e in range(DC):
                        ins = add_up(s.bank(2 + e), [(f8_w[:, c, e * P:(e + 1) * P], s.f8_q[:, c, :]) for c in range(DC)])
                    ins.then_inc(pe_f8.sem, 1)

            with pe.Fori(0, PAIRS) as t:
                condition(t)
                scan_attention(t)
                pool_prompt(t)
            order()
            pe.wait_ge(expert_in.sem, 5 * 16)
            with pe.Fori(0, PAIRS) as t:
                shared_expert(t)
            pe.wait_ge(late_expert_in.sem, (EXPERTS - 5) * 16)
            pe.wait_ge(sort_dve.sem, ORDER_STEPS)
            pe.wait_ge(x2_ready.sem, x2_ready.at(PAIRS, 0))
            slot_turn(0, 0)
            slot_up(0, 0, 0, pe_slot_h)
            slot_up(0, 0, 1, pe_slot_u)
            slot_turn(0, 1)
            with pe.Fori(0, SLOT_PAIRS - 1) as i:
                for k in (1, 2):
                    slot_step(i, k)
            slot_step(SLOT_PAIRS - 1, 1, last=True)
            slot_turn_g(SLOT_PAIRS - 1, 1)
            slot_down(SLOT_PAIRS - 1, 1)
            with pe.Fori(0, PAIRS) as t:
                picked(t)
                adapter(t)
                attention(t)
                last_ffn(t)

        for name, s in signals:
            per = period(s)
            assert not s.given or not per or per == s.given, (name, per, s.given)


def setup_arrays(inputs):
    f = {n: np.asarray(a) for n, a in inputs.items()}

    def rows(a, k):
        return a.reshape(k, P, -1).transpose(1, 0, 2)

    def lhs(a, k):
        return rows(a.T, k)

    vecs = np.zeros((P, NVEC), np.float32)

    def put(name, a):
        at, n = VEC[name]
        a = np.asarray(a)
        vecs[:a.shape[0], at:at + n] = a.reshape(a.shape[0], n)

    def chunk_cols(a, k):
        return a.reshape(k, P).T

    put("tau", np.broadcast_to(np.concatenate([f["L0_cond_tau_ctx"].reshape(1), f["condB_tauraws"]]), (P, 1 + ND)))
    put("deriv", np.broadcast_to(f["L0_attn_deriv_logits"], (P, 3)))
    for name, key in (("bg", "bg"), ("btemp", "btemp"), ("bsoma", "bsoma"), ("gamma", "gamma"), ("beta", "beta")):
        put(name, chunk_cols(f["L0_cond_" + key], DC))
    put("bn1", f["L0_cond_bn1"].reshape(HID, 1))
    put("bn2", f["condB_bn2"].reshape(ND, 1))
    put("blend", f["cond_1024"].reshape(ND, DC, P).transpose(2, 1, 0))
    taps = np.zeros((TAPS, 9 * P), np.float32)
    taps[:, :C_IN] = f["L0_attn_conv_k"][:, 0, :]
    put("conv_k", taps.reshape(TAPS, 9, P).transpose(2, 1, 0))
    cb = np.zeros(9 * P, np.float32)
    cb[:C_IN] = f["L0_attn_conv_b"]
    put("conv_b", chunk_cols(cb, 9))
    put("theta", chunk_cols(f["L0_attn_theta"].reshape(-1), IC))
    put("slope", np.concatenate([f["L0_attn_decay_slopes"], f["L0_attn_anchor_slopes"]]).reshape(-1, 1))
    put("score_scale", f["L0_attn_score_scale"].reshape(-1, 1))
    put("norm_re", np.tile(f["L0_attn_norm_scale"][:HD_B], P // HD_B).reshape(-1, 1))
    put("norm_im", np.tile(f["L0_attn_norm_scale"][HD_B:], P // HD_B).reshape(-1, 1))
    put("b1", f["L0_cond2_b1"].reshape(-1, 1))
    put("fbias", chunk_cols(f["L1_ffn_bias"], DC))
    for name, value in (("eps5", 1e-5), ("eps6", 1e-6), ("half_pi", np.pi / 2), ("zero", 0.0)):
        put(name, np.full((P, 1), value, np.float32))

    def block_diagonal(a):
        out = np.zeros((P, P), np.float32)
        for k in range(P // HD_B):
            out[k * HD_B:(k + 1) * HD_B, k * HD_B:(k + 1) * HD_B] = a
        return out

    x = f["x"].reshape(TILES, T, DC, P).transpose(0, 3, 2, 1)
    a = {
        "x_t": x, "vecs": vecs,
        "w_g": lhs(f["L0_cond_Wg"], 2 * DC), "w_n1": lhs(f["L0_cond_Wn1"], DC), "w_n2": f["cond_256"].T,
        "w_soma": lhs(f["L0_cond_Wsoma"], DC), "w_temp": lhs(f["L0_cond_Wtemp"], DC),
        "w_out": lhs(f["L0_cond_Wout"], DC), "w_in": rows(f["L0_attn_in_proj_w"], DC),
        "w_re": block_diagonal(f["L0_attn_W_re"]), "w_im": block_diagonal(f["L0_attn_W_im"]),
        "w_proj": rows(f["L0_attn_out_proj_w"], IC), "w_1": rows(f["L0_cond2_W1"], DC),
        "v_col": f["L0_cond2_v"].reshape(HID, 1),
        "w_route": rows(f["L0_ffn_gate_w"], DC),
        "qkvo": np.stack([lhs(f["L1_attn_" + n], DC) for n in ("wq", "wk", "wv", "wo")], 1),
        "w_f8": lhs(f["L1_ffn_weight"], DC),
        "g_rows": np.broadcast_to(np.stack([f["L1_attn_" + n] for n in ("gq", "gk", "gv", "go")]), (P, 4, D)),
        "ids_row": np.concatenate([f["itok_B_0_6"], f["itok_B_0_63"]]).reshape(1, 2 * B),
        "kind_ids": np.broadcast_to(f["itok_B_0_2"], (P, B)),
        "down_w": f["L1_cond_down_w"].reshape(8, DC, P, P).transpose(0, 2, 1, 3),
        "down_b": f["L1_cond_down_b"].reshape(8, P, 1),
        "up_w": f["L1_cond_up_w"], "up_b": f["L1_cond_up_b"].reshape(8, 1, D),
        "ln_g": f["L1_cond_ln_g"].reshape(8, 1, D), "ln_b": f["L1_cond_ln_b"].reshape(8, 1, D),
        "cat_w": f["L1_cond2_W"].reshape(64, DC, P, D).transpose(0, 2, 1, 3),
        "cat_b": f["L1_cond2_b"].reshape(64, DC, P).transpose(0, 2, 1),
    }
    up = np.stack([np.concatenate([f["L0_ffn_sw1"][None], f["L0_ffn_ew1"]]),
                   np.concatenate([f["L0_ffn_sw2"][None], f["L0_ffn_ew2"]])], 1)
    up = up.reshape(EXPERTS, 2, DC, P, FF).transpose(0, 3, 1, 2, 4).reshape(EXPERTS, P, -1)
    down = np.concatenate([f["L0_ffn_sw3"][None], f["L0_ffn_ew3"]])
    down = down.reshape(EXPERTS, FC, P, D).transpose(0, 2, 1, 3).reshape(EXPERTS, P, -1)
    a["expert_w"] = np.concatenate([up, down], 2)

    a["ident"] = np.eye(P, dtype=np.float32)
    a["ones"] = np.ones((P, 1), np.float32)
    head = np.arange(INNER) // HD_B
    sel = (np.arange(HEADS_B)[:, None] == head[None, :]).astype(np.float32)
    a["head_sel"] = sel.reshape(HEADS_B, IC, P)
    a["head_sum"] = sel.T.reshape(IC, P, HEADS_B).transpose(1, 0, 2) / np.float32(2 * HD_B)
    j, l = np.arange(S)[:, None], np.arange(S)[None, :]
    mask = np.stack([np.where(m, 0.0, NEG) for m in (l <= j, l >= j, l != j)]).astype(np.float32)
    a["pool_mask"] = mask.reshape(3, 2, P, S).transpose(2, 0, 1, 3)
    count = np.stack([np.arange(S) + 1, S - np.arange(S), np.full(S, S - 1)]).astype(np.float32)
    a["pool_count"] = count.reshape(3, 2, P).transpose(2, 0, 1)
    pos = np.arange(S, dtype=np.float32)
    a["dist"] = np.where(np.arange(HEADS_B)[:, None] < HEADS_B - 4, S - 1 - pos, pos).astype(np.float32)
    q, k = np.arange(P)[:, None], np.arange(P)[None, :]
    a["causal"] = np.where(k <= q, 0.0, NEG).astype(np.float32)
    a["earlier"] = (q < k).astype(np.float32)
    a["slot_block"] = np.broadcast_to(np.arange(SLOTS, dtype=np.float32)[:, None], (SLOTS, NE - 1))[None]
    a["expert_no"] = np.broadcast_to(np.arange(NE, dtype=np.float32), (P, NS, NE))
    return {n: np.ascontiguousarray(v) for n, v in a.items()}


def kernel(**inputs):
    import concourse.bacc as bacc
    from concourse.bass_utils import run_bass_kernel_spmd

    nc = bacc.Bacc("TRN2", target_bir_lowering=False, num_devices=1)
    arrays = setup_arrays(inputs)
    dram = {n: nc.dram_tensor("in_" + n, a.shape, mybir.dt.from_np(a.dtype), kind="ExternalInput").ap()
            for n, a in arrays.items()}
    out = nc.dram_tensor("out_t", (TILES, P, DC, T), F32, kind="ExternalOutput").ap()
    adaln_attention_ffn(nc, dram, out)
    r = run_bass_kernel_spmd(nc, [{"in_" + n: a for n, a in arrays.items()}], core_ids=[0])
    y = np.asarray(r.results[0]["out_t"])
    return y.transpose(0, 3, 2, 1).reshape(B, S, D)
```

```python
from contextlib import ExitStack

import concourse.bass as bass
import numpy as np
from concourse import mybir

F32 = mybir.dt.float32
BF16 = mybir.dt.bfloat16
F16 = mybir.dt.float16
I32 = mybir.dt.int32
ACT = mybir.ActivationFunctionType
ALU = mybir.AluOpType
AX = mybir.AxisListType

P = 128
B, S, D = 8, 256, 256
BT = 2
T = BT * S
TILES = B // BT
NS = T // P
DC = D // P
ND = 8
HID = 64
HEADS_B, HD_B = 32, 16
INNER = HEADS_B * HD_B
IC = INNER // P
C_IN = 2 * INNER + HEADS_B
TAPS = 4
NE, FF = 8, 512
EXPERTS = NE + 1
FC = FF // P
BLOCKS = TILES * NS
SLOTS = 2 * BLOCKS + NE
SLOT_PAIRS = SLOTS // 2
NH, HD = 16, 16
MAGIC = 12582912.0
TWO_PI = 6.283185307179586
TWO_PI_HI = 6.28125
TWO_PI_LO = TWO_PI - TWO_PI_HI
PI_SAFE = 3.1415925
NEG = -1e30

VEC_COLS = [("tau", 1 + ND), ("deriv", 3), ("bg", DC), ("btemp", DC), ("bsoma", DC), ("gamma", DC), ("beta", DC),
            ("bn1", 1), ("bn2", 1), ("blend", DC * ND), ("conv_k", TAPS * 9), ("conv_b", 9), ("theta", IC),
            ("slope", 1), ("score_scale", 1), ("norm_re", 1), ("norm_im", 1), ("b1", 1), ("fbias", DC),
            ("eps5", 1), ("eps6", 1), ("half_pi", 1), ("zero", 1)]
VEC = {}
_at = 0
for _name, _n in VEC_COLS:
    VEC[_name] = (_at, _n)
    _at += _n
NVEC = _at

WEIGHTS = {
    "w_g": (P, (2 * DC, D)), "w_n1": (P, (DC, HID)), "w_n2": (HID, (ND,)), "w_soma": (P, (DC, D)),
    "w_temp": (P, (DC, D)), "w_out": (P, (DC, D)), "w_in": (P, (DC, C_IN)), "w_re": (P, (P,)), "w_im": (P, (P,)),
    "w_proj": (P, (IC, D)), "w_1": (P, (DC, HID)), "v_col": (HID, (1,)), "w_route": (P, (DC, NE)),
    
}
CONSTS = {
    "ident": (P, (P,)), "ones": (P, (1,)), "head_sum": (P, (IC, HEADS_B)),
    "pool_count": (P, (3, 2)), "dist": (HEADS_B, (S,)), "head_sel": (HEADS_B, (IC, P)),
    "causal": (P, (P,)), "expert_no": (P, (NS, NE)),
}


EARLY = ["ident", "ones", "w_n1", "w_soma", "w_g", "w_n2", "dist", "w_temp", "w_out"]
MID = ["w_in", "head_sel", "head_sum", "w_re", "w_im", "w_proj", "w_1", "v_col", "pool_count", "w_route",
       "expert_no"]
N_EARLY, N_MID = len(EARLY) + 1, len(MID) + 1
DVE_MAXIMA, DVE_SLOPES, DVE_SUMS = 4, 23, 44
SLOT_STEPS, ORDER_STEPS = 20, 24
CHAIN = {"dve_1": 326, "act_1": 64, "dve_3": 220, "act_3": 98}
PAIRS = TILES // 2


class Signal:

    def __init__(self, sem, per_tile, before):
        self.sem, self.per_tile, self.before, self.given = sem, per_tile, before, 0

    def at(self, t, k, u=None):
        if u is None:
            return t * self.per_tile + (self.before + k)
        return t * (2 * self.per_tile) + (self.before + 2 * (k - 1) + u + 1)


def adaln_attention_ffn(nc, dram, out):
    with ExitStack() as ctx:
        def sb(name, shape, dt=F32):
            return ctx.enter_context(nc.sbuf_tensor(name, shape, dt))

        signals = []

        def signal(name, per_tile=1, before=0):
            signals.append((name, Signal(ctx.enter_context(nc.semaphore(name)), per_tile, before)))
            return signals[-1][1]

        def further(last, n, per_tile):
            signals.append((signals[0][0], Signal(last.sem, per_tile, last.before + n * last.per_tile)))
            return signals[-1][1]

        w = {n: sb(n, [p, *shape]) for n, (p, shape) in (WEIGHTS | CONSTS).items()}
        vecs = sb("vecs", [P, NVEC])

        def col(name, k=0, p=P):
            at = VEC[name][0] + k
            return vecs[0:p, at:at + 1]

        expert_w = sb("expert_w", [P, EXPERTS, 2 * DC * FF + FC * D])

        def up_weight(which, c, m):
            at = (which * DC + c) * FF + m * P
            return expert_w[:, 0, at:at + P]

        def down_weight(m, c):
            at = 2 * DC * FF + m * D + c * P
            return expert_w[:, 0, at:at + P]

        def routed_weight(e, at, n):
            return expert_w[:, bass.ds(e, 1), at:at + n].rearrange("p e n -> p (e n)")

        ids_row = sb("ids_row", [1, 2 * B], I32)
        kind_ids = sb("kind_ids", [P, B], I32)

        decay = sb("decay", [P, 1 + ND])
        blend = sb("blend", [P, DC, ND])
        deriv = sb("deriv_w", [P, 4])
        half_b = sb("half_b", [P, 2 * DC + 1])
        theta_turns = sb("theta_turns", [P, IC])
        slope = sb("slope_sb", [HEADS_B, 1])
        time_w = w["dist"]
        pool_mask = sb("pool_mask", [P, 3, 2, S], BF16)
        tern_qk = sb("tern_qk", [P, 2, DC, 4 * P], BF16)
        tern_vo = sb("tern_vo", [P, 2, DC, D], BF16)
        w_scale = sb("w_scale", [P, 8])
        qk_scale = sb("qk_scale", [P, 1])
        f8_w = sb("f8_w", [P, DC, D], BF16)
        ident_b = sb("ident_b", [P, P], BF16)
        causal_a = sb("causal_a", [P, 4 * P], BF16)
        kind = sb("kind", [P, B, 3])
        picks = sb("picks", [P, 2, BLOCKS, NE])
        shares = sb("shares", [P, 2, BLOCKS])
        slots = sb("slots", [P, 2, BLOCKS], I32)
        slot_expert = sb("slot_expert", [1, SLOTS], I32)
        smalls = [sb("small_a", [P, 640]), sb("small_b", [P, 640])]

        UNITS = 22
        arena_a = sb("arena", [P, UNITS * T])
        spare = expert_w[:, :, :].rearrange("p e n -> p (e n)")
        EXPERT = 2 * DC * FF + FC * D
        arena_b = spare[:, 5 * EXPERT:5 * EXPERT + UNITS * T]

        class Stream:

            def __init__(self, u, arena):
                def unit(a, n=1, p=P):
                    return arena[0:p, a * T:(a + n) * T]

                def chunks(a, n, units=None):
                    return unit(a, units or n).rearrange("p (c n) -> p c n", c=n)

                def rows(a, n=2):
                    return unit(a, n).rearrange("p (s d) -> p s d", s=NS)

                self.unit, self.chunk, self.rows = unit, chunks, rows
                self.small, self.bank0 = smalls[u], 4 * u
                self.stat = smalls[u][:, 24:32].rearrange("p (s k) -> p s k", k=2)
                self.stat_mean, self.stat_var = self.stat[:, :, 0], self.stat[:, :, 1]
                self.x = chunks(0, 2)
                self.ctx_t, self.gated = chunks(2, 2), chunks(4, 2)
                self.scaled = [chunks(6, 2), chunks(8, 2)]
                self.trace = [chunks(10, 2), chunks(12, 2)]
                self.gate_t, self.soma = chunks(14, 2), chunks(16, 2)
                self.mod, self.h1 = unit(18, 1, ND), unit(19, 1, HID)
                self.temporal, self.cond_rows = chunks(2, 2), rows(4)
                self.cond = chunks(20, 2)
                self.conv = [unit(2), unit(3)]
                self.p_t, self.inv_den = unit(4, 1, HEADS_B), unit(5, 1, HEADS_B)
                self.phi, self.turns, self.angle, self.sin_t, self.cos_t, self.mean_re, self.mean_im = \
                    (unit(6 + k) for k in range(7))
                self.gtanh, self.gate_s, self.yg = unit(13), unit(14), chunks(15, 4)
                self.rms_b = unit(19, 1, HEADS_B)
                self.zpad = zpads[u]
                self.score_h = unit(2, 1, HID)
                self.masked = unit(3, 2).rearrange("p (g l) -> p g l", g=4)
                self.pool_w = unit(5, 2).rearrange("p (g l) -> p g l", g=4)
                self.pool_wt = unit(7, 2).rearrange("p (b n) -> p b n", b=BT)
                self.x1_rows, self.pooled, self.pooled_rows = rows(9), chunks(20, 2), rows(11)
                self.picked = [rows(5), rows(7)] if u else \
                    [spare[:, 13 * 1024 + k * 1024:][:, 0:1024].rearrange("p (s d) -> p s d", s=NS) for k in (0, 1)]
                self.bottle, self.adapt_y = unit(2), rows(3)
                self.attn_in, self.scaled_in = rows(5), rows(7)
                self.int_rows = unit(9).bitcast(BF16).rearrange("p (s d) -> p s d", s=NS)
                self.int_tt = unit(10).bitcast(BF16).rearrange("p (c n) -> p c n", c=DC)
                self.q_t, self.k_t, self.v_rows = chunks(11, 4), chunks(15, 4), rows(19)
                self.row_diag = unit(21).rearrange("p (s q) -> p s q", s=NS)
                self.kscale_b = unit(3)
                self.probs, self.probs_tt = [unit(2), unit(4)], [unit(7), unit(8)]
                self.heads_t = unit(5)
                self.head_out, self.yscale_b = rows(9), unit(3)
                self.y_rows = unit(11).bitcast(BF16).rearrange("p (s d) -> p s d", s=NS)
                self.y_tt = unit(12).bitcast(BF16).rearrange("p (c n) -> p c n", c=DC)
                self.f8_t, self.f8_a, self.f8_b = chunks(4, 2), chunks(6, 2), chunks(8, 2)
                self.f8_q = unit(15).bitcast(BF16).rearrange("p (c n) -> p c n", c=DC)
                self.half_t = unit(13).bitcast(F16).rearrange("p (c n) -> p c n", c=DC)
                self.out_t = chunks(16, 2)
                own = spare[:, (1 + 6 * u) * 1024:(7 + 6 * u) * 1024]

                def part(at, n, pattern, **sizes):
                    return own[:, at:at + n].rearrange(pattern, **sizes)

                self.adapt_down = part(0, 512, "p (b c n) -> p b c n", b=BT, c=DC)
                self.adapt_up = part(512, 512, "p (b n) -> p b n", b=BT)
                self.adapt_rows = part(1024, 1024, "p (g b d) -> p g b d", g=2, b=BT)
                self.cat_w = part(2048, 1024, "p (b c n) -> p b c n", b=BT, c=DC)
                self.adapt_bu = own[0:1, 3072:3584].rearrange("p (b d) -> p b d", b=BT)
                self.adapt_bd = own[:, 3584:3584 + BT]
                self.cat_b = own[:, 3586:3586 + BT * DC].rearrange("p (b c) -> p b c", b=BT)

            def sm(self, at, n, p=P):
                return self.small[0:p, at:at + n]

            def bank(self, k, n=1, p=P):
                b = self.bank0 + k
                return psum[0:p, b, :] if n == 1 else psum[0:p, b:b + n, :]

            def bank_b(self, k, n):
                return psum_b[:, self.bank0 + k:self.bank0 + k + n, 0:T]

            def token_banks(self, k):
                return self.bank(k, 2).rearrange("p a (k d) -> p (a k) d", k=2)

        zpads = [sb("zpad_a", [P, 2, BT, TAPS - 1 + S]), sb("zpad_b", [P, 2, BT, TAPS - 1 + S])]
        psum = ctx.enter_context(nc.psum_tensor("psum", [P, 8, T], F32))
        psum_b = psum[:, :, :].rearrange("p a n -> p (a n)").bitcast(BF16).rearrange("p (a n) -> p a n", a=8)
        streams = [Stream(0, arena_a), Stream(1, arena_b)]
        A = streams[0]
        sm = A.sm
        g_rows = spare[:, 0:1024].rearrange("p (k d) -> p k d", k=4)
        raw_qkvo = A.unit(2, 4).rearrange("p (k c d) -> p k c d", k=4, c=DC)
        raw_f8, f8_tmp = A.unit(6), A.unit(7)
        raw_mask = A.unit(8, 3).rearrange("p (k j l) -> p k j l", k=3, j=2)
        earlier = A.unit(21)[:, 0:P]
        slot_block = A.unit(21, 1, 1)[:, P:P + SLOTS * (NE - 1)].rearrange("p (j e) -> p j e", j=SLOTS)
        zeros = spare[:, 5 * EXPERT + UNITS * T:5 * EXPERT + UNITS * T + D]
        pooled_in, x1_in = [A.chunk(0, 2), A.chunk(2, 2)], [A.chunk(4, 2), A.chunk(6, 2)]
        rows_in = [A.rows(8), A.rows(10)]
        g_buf, act_h = A.chunk(12, 4), [A.unit(16), A.unit(17)]
        slot_rows = A.unit(18).rearrange("p (q d) -> p q d", q=2)
        slot_t = A.unit(19).rearrange("p (q c n) -> p q c n", q=2, c=DC)
        slot_out = A.unit(20).rearrange("p (q d) -> p q d", q=2)
        slot_h, slot_g = [A.unit(16), A.unit(17)], [A.unit(12), A.unit(13)]
        slot_g_t = [A.chunk(14, 4, 1), A.chunk(15, 4, 1)]

        x1_dram = nc.dram_tensor("x1_scratch", (TILES, P, DC, T), F32).ap()
        pooled_dram = nc.dram_tensor("pooled_scratch", (TILES, P, DC, T), F32).ap()
        rows_dram = nc.dram_tensor("rows_scratch", (TILES, P, NS, D), F32).ap()
        slot_in_dram = nc.dram_tensor("slot_in_scratch", (SLOTS, P, D), F32).ap()
        slot_out_dram = nc.dram_tensor("slot_out_scratch", (SLOTS, P, D), F32).ap()
        x2_dram = nc.dram_tensor("x2_scratch", (TILES, P, DC, T), F32).ap()

        loads = {n: signal(n + "_in", 0) for n in ("early", "mid", "attn")}
        ids_in = signal("ids_in", 0)
        expert_in = signal("expert_in", 0)
        late_expert_in = signal("late_expert_in", 0)
        g_rows_in = signal("g_rows_in", 0)
        zeros_ready = signal("zeros_ready", 0)
        slots_zeroed = signal("slots_zeroed", 0)
        setup_dve = signal("setup_dve", 0)
        setup_act = signal("setup_act", 0)
        setup_pe = signal("setup_pe", 0)
        setup_pool = signal("setup_pool", 0)

        x_in = [signal(f"x_in_{u}", 16) for u in (0, 1)]
        dve_chain_1 = signal("dve_chain_1", CHAIN["dve_1"])
        act_chain_1 = signal("act_chain_1", CHAIN["act_1"])
        ctx_ready = signal("ctx_ready")
        pe_soma = signal("pe_soma")
        h1_ready = signal("h1_ready")
        soma_ready = signal("soma_ready")
        pe_gate = signal("pe_gate")
        gate_tanh = signal("gate_tanh")
        pe_mod = signal("pe_mod")
        mod_tanh = signal("mod_tanh")
        mod_ready = signal("mod_ready")
        pe_mod_rows = signal("pe_mod_rows", ND)
        trace_ready = signal("trace_ready", ND)
        pe_trace_used = signal("pe_trace_used", ND)
        temporal_ready = signal("temporal_ready")
        pe_temp = signal("pe_temp")
        temp_tanh = signal("temp_tanh")
        mixed_ready = signal("mixed_ready")
        pe_cond = signal("pe_cond")
        cond_stats = signal("cond_stats")
        cond_std = signal("cond_std")
        cond_norm = signal("cond_norm")
        pe_cond_t = signal("pe_cond_t")
        cond_ready = signal("cond_ready")
        pe_s = signal("pe_s")
        s_copied = signal("s_copied")
        s_clipped = signal("s_clipped")
        p_exp = signal("p_exp")
        p_ready = signal("p_ready")
        pe_val = signal("pe_val", IC)
        val_copied = signal("val_copied", IC)
        pe_zg = signal("pe_zg", IC)
        zg_copied = signal("zg_copied", IC)
        pe_p_rows = signal("pe_p_rows", IC)
        val_ready = signal("val_ready", IC)
        gconv_ready = signal("gconv_ready", IC)
        phi_ready = signal("phi_ready", IC)
        gtanh_ready = signal("gtanh_ready", IC)
        angle_ready = signal("angle_ready", IC)
        linear_ready = signal("linear_ready", IC)
        product_ready = signal("product_ready", IC)
        trig_ready = signal("trig_ready", IC)
        mean_ready = signal("mean_ready", IC)
        sq_ready = signal("sq_ready", IC)
        pe_sq = signal("pe_sq", IC)
        pe_y = signal("pe_y", IC)
        yg_ready = signal("yg_ready", IC)
        rms_sqrt = signal("rms_sqrt")
        rms_ready = signal("rms_ready")
        pe_rms_rows = signal("pe_rms_rows")
        ynorm_ready = signal("ynorm_ready")
        pe_proj = signal("pe_proj")
        x1_ready = signal("x1_ready")
        pe_x1_rows = signal("pe_x1_rows")
        pe_score_hid = signal("pe_score_hid")
        x1_rows_ready = signal("x1_rows_ready")
        score_hid = signal("score_hid")
        pe_score = signal("pe_score")
        score_max = signal("score_max")
        pool_exp = signal("pool_exp")
        pool_p = signal("pool_p")
        pe_pool_t = signal("pe_pool_t")
        pool_t = signal("pool_t")
        pe_pool = signal("pe_pool")
        pool_ready = signal("pool_ready")
        pe_pool_rows = signal("pe_pool_rows")
        pool_rows_ready = signal("pool_rows_ready", 1, before=2)
        pe_route = signal("pe_route")
        top_ready = signal("top_ready")
        route_exp = signal("route_exp")
        picks_ready = signal("picks_ready", 1, before=2)
        x1_stored = [signal(f"x1_stored_{u}", 16, before=16) for u in (0, 1)]
        pooled_stored = [signal(f"pooled_stored_{u}", 32, before=16) for u in (0, 1)]
        order_in = signal("order_in", 0)
        sort_dve = signal("sort_dve", 0)
        sort_pe = signal("sort_pe", 0)
        ffn_in = [further(x_in[u], PAIRS, 32) for u in (0, 1)]
        rows_got = [signal(f"rows_got_{u}", 16) for u in (0, 1)]
        x2_stored = [further(x1_stored[u], PAIRS, 16) for u in (0, 1)]
        scattered = [signal(f"scattered_{u}", 2 * NS * 16) for u in (0, 1)]
        pe_up = signal("pe_up", 2 * FC)
        h_tanh = signal("h_tanh", 2 * FC)
        h_read = signal("h_read", 2 * FC)
        g_ready = signal("g_ready", 2 * FC)
        pe_down = signal("pe_down", 2)
        x2_ready = signal("x2_ready", 2, before=1)
        slot_rows_in = [signal(f"slot_rows_in_{p}", 16) for p in (0, 1)]
        slot_stored = [signal(f"slot_stored_{p}", 16, before=16) for p in (0, 1)]
        pe_slot_t = signal("pe_slot_t", 2, before=2)
        slot_t_ready = signal("slot_t_ready", 2)
        pe_slot_h = further(pe_up, PAIRS, 2)
        pe_slot_u = signal("pe_slot_u", 2)
        slot_tanh = further(h_tanh, PAIRS, 2)
        slot_h_ready = further(h_read, PAIRS, 2)
        slot_g_ready = further(g_ready, PAIRS, 2)
        pe_slot_g_t = signal("pe_slot_g_t", 2)
        slot_g_t_ready = signal("slot_g_t_ready", 2)
        pe_slot_out = further(pe_down, PAIRS, 2)
        slot_out_ready = signal("slot_out_ready", 2, before=1)
        x2_in = [further(ffn_in[u], PAIRS, 16) for u in (0, 1)]
        own_in = [signal(f"own_in_{u}", 8 * BT * 16) for u in (0, 1)]
        out_stored = [further(x2_stored[u], PAIRS, 16) for u in (0, 1)]
        gathered = [further(scattered[u], PAIRS, 2 * NS * 16) for u in (0, 1)]
        picked_sum = signal("picked_sum")
        pe_picked_t = signal("pe_picked_t")
        x2_whole = signal("x2_whole")
        dve_chain_3 = further(dve_chain_1, PAIRS, CHAIN["dve_3"])
        act_chain_3 = further(act_chain_1, PAIRS, CHAIN["act_3"])
        NG = 12 * BT
        pe_bottle = signal("pe_bottle")
        bottle_ready = signal("bottle_ready")
        pe_adapt = signal("pe_adapt")
        adapt_stats = further(cond_stats, TILES, 1)
        adapt_std = further(cond_std, TILES, 1)
        adapt_ready = signal("adapt_ready")
        rms_in = signal("rms_in", 2)
        int_ready = signal("int_ready", 4)
        pe_int_t = signal("pe_int_t", 4)
        int_t = signal("int_t", 4)
        pe_scale = signal("pe_scale", 2)
        diag_ready = signal("diag_ready", 2)
        scale_ready = signal("scale_ready", 2)
        pe_q = signal("pe_q")
        q_ready = signal("q_ready")
        pe_k = signal("pe_k")
        k_ready = signal("k_ready")
        pe_v = signal("pe_v")
        v_ready = signal("v_ready")
        pe_logits = signal("pe_logits", NG)
        row_max = signal("row_max", NG)
        probs_ready = signal("probs_ready", NG)
        pe_probs_t = signal("pe_probs_t", NG)
        probs_t = signal("probs_t", NG)
        pe_heads = signal("pe_heads", NG)
        heads_t_ready = signal("heads_t_ready", 2 * BT)
        pe_heads_rows = signal("pe_heads_rows", 2 * BT)
        heads_ready = signal("heads_ready", 2 * BT)
        pe_o = signal("pe_o")
        x3_ready = signal("x3_ready")
        pe_cat = signal("pe_cat")
        f8_ready = signal("f8_ready")
        pe_f8 = signal("pe_f8")
        half_ready = signal("half_ready")
        out_ready = signal("out_ready", 1, before=2)

        class Group:

            def __init__(self, n):
                self.b, k = divmod(n, 12)
                self.s = 2 * self.b + (k >= 4)
                r = k % 4
                self.heads = [r, r + 4, r + 8, r + 12] if k < 4 else [r, r + 4] if k < 8 else [r + 8, r + 12]
                self.width = P if k < 4 else S
                self.first, self.last = k in (0, 4), k in (3, 11)

        def group(n):
            return Group(n)

        def period(sig):
            return sig.per_tile if sig in once else 2 * sig.per_tile

        once = [dve_chain_1, act_chain_1, dve_chain_3, act_chain_3, h_tanh, h_read, g_ready, x2_ready,
                setup_dve, setup_act, setup_pe, setup_pool]

        block = ctx.enter_context(nc.Block())

        @block.sync
        def _(sp):
            def load(name, dst, sig):
                sp.dma_start(dst, dram[name]).then_inc(sig.sem, 16)

            def fetch(dst, src, t, sig):
                sp.dma_start(dst, src[bass.ds(t, 1)].rearrange("a p c n -> (a p) c n")).then_inc(sig.sem, 16)

            def keep(dst, t, src, sig):
                sp.dma_start(dst[bass.ds(t, 1)].rearrange("a p c n -> (a p) c n"), src).then_inc(sig.sem, 16)

            load("vecs", vecs[:, :], loads["early"])
            for s in (pool_rows_ready, picks_ready, x2_ready, pe_slot_t, slot_out_ready, out_ready, *x1_stored, *pooled_stored,
                      *slot_stored):
                sp.sem_inc(s.sem, s.before)
            for n in EARLY:
                load(n, w[n][...], loads["early"])
            load("ids_row", ids_row[:, :], ids_in)
            for n in MID:
                load(n, w[n][...], loads["mid"])
            load("kind_ids", kind_ids[:, :], loads["mid"])
            load("qkvo", raw_qkvo, loads["attn"])
            load("pool_mask", raw_mask, loads["attn"])
            load("w_f8", raw_f8, loads["attn"])
            load("causal", w["causal"][...], loads["attn"])
            sp.wait_ge(zeros_ready.sem, 1)
            sp.dma_start(slot_in_dram.rearrange("n p d -> p n d"),
                         zeros[:, None, :].broadcast_to([P, SLOTS, D])).then_inc(slots_zeroed.sem, 16)
            def pair_out(t, more):
                for u in (0, 1):
                    sp.wait_ge(x1_ready.sem, x1_ready.at(t, 1, u))
                    keep(x1_dram, t * 2 + u, streams[u].x, x1_stored[u])
                if more:
                    for u in (0, 1):
                        sp.wait_ge(x1_stored[u].sem, x1_stored[u].at(t, 16))
                        sp.wait_ge(pe_score_hid.sem, pe_score_hid.at(t, 1, u))
                        fetch(streams[u].x, dram["x_t"], t * 2 + 2 + u, x_in[u])
                for u in (0, 1):
                    sp.wait_ge(pool_ready.sem, pool_ready.at(t, 1, u))
                    keep(pooled_dram, t * 2 + u, streams[u].pooled, pooled_stored[u])
                for u in (0, 1):
                    sp.wait_ge(pool_rows_ready.sem, pool_rows_ready.at(t, 1, u))
                    keep(rows_dram, t * 2 + u, streams[u].pooled_rows, pooled_stored[u])

            for u in (0, 1):
                fetch(streams[u].x, dram["x_t"], u, x_in[u])
            with sp.Fori(0, PAIRS - 1) as t:
                pair_out(t, True)
            pair_out(PAIRS - 1, False)

            def shared_in(t):
                u = t % 2
                fetch(pooled_in[u], pooled_dram, t, ffn_in[u])
                fetch(x1_in[u], x1_dram, t, ffn_in[u])
                fetch(rows_in[u], rows_dram, t, rows_got[u])

            for u in (0, 1):
                sp.wait_ge(x1_stored[u].sem, x1_stored[u].at(PAIRS, 0))
                sp.wait_ge(pooled_stored[u].sem, pooled_stored[u].at(PAIRS, 0))
            sp.wait_ge(picks_ready.sem, picks_ready.at(PAIRS - 1, 1, 1))
            load("earlier", earlier, order_in)
            load("slot_block", slot_block, order_in)
            shared_in(0)
            shared_in(1)
            sp.wait_ge(slots_zeroed.sem, 16)
            for e in range(5, EXPERTS):
                sp.dma_start(expert_w[:, e, :], dram["expert_w"][e]).then_inc(late_expert_in.sem, 16)
            for t in range(TILES):
                u = t % 2
                sp.wait_ge(x2_ready.sem, x2_ready.at(0, t + 1))
                keep(x2_dram, t, x1_in[u], x2_stored[u])
                if t + 2 < TILES:
                    sp.wait_ge(x2_stored[u].sem, x2_stored[u].at(t // 2 + 1, 0))
                    sp.wait_ge(scattered[u].sem, scattered[u].at(t // 2 + 1, 0))
                    shared_in(t + 2)
            for u in (0, 1):
                sp.wait_ge(scattered[u].sem, scattered[u].at(PAIRS, 0))
            with sp.Fori(0, SLOT_PAIRS) as i:
                for p in (0, 1):
                    sp.wait_ge(pe_slot_t.sem, pe_slot_t.at(i, p - 1))
                    sp.dma_start(slot_rows[:, p, :], slot_in_dram[bass.ds(i * 2 + p, 1)].rearrange("a p d -> (a p) d")) \
                        .then_inc(slot_rows_in[p].sem, 16)
            for u in (0, 1):
                sp.wait_ge(x2_stored[u].sem, x2_stored[u].at(PAIRS, 0))
            for p in (0, 1):
                sp.wait_ge(slot_stored[p].sem, slot_stored[p].at(SLOT_PAIRS, 0))
            sp.wait_ge(ids_in.sem, 16)
            sp.dma_start(g_rows, dram["g_rows"]).then_inc(g_rows_in.sem, 16)
            with sp.Fori(0, PAIRS) as t:
                for u in (0, 1):
                    s = streams[u]
                    first = (t * 2 + u) * BT
                    who = sp.value_load(ids_row[0:1, bass.ds(first, 1)])
                    sp.wait_ge(out_ready.sem, out_ready.at(t, 0, u))
                    fetch(s.x, x2_dram, t * 2 + u, x2_in[u])
                    for b in range(BT):
                        if b:
                            who = sp.value_load(ids_row[0:1, bass.ds(first + b, 1)])

                        def own(dst, name, pattern, to=None):
                            src = dram[name][bass.ds(who, 1)].rearrange(pattern)
                            sp.dma_start(dst, src if to is None else src.broadcast_to(to)).then_inc(own_in[u].sem, 16)

                        own(s.adapt_down[:, b, :, :], "down_w", "a p c n -> (a p) c n")
                        own(s.adapt_up[:, b, :], "up_w", "a p n -> (a p) n")
                        own(s.adapt_bd[:, b:b + 1], "down_b", "a p n -> (a p) n")
                        own(s.adapt_bu[:, b, :], "up_b", "a b d -> (a b) d")
                        own(s.adapt_rows[:, 0, b, :], "ln_g", "a b d -> (a b) d", [P, D])
                        own(s.adapt_rows[:, 1, b, :], "ln_b", "a b d -> (a b) d", [P, D])
                        who = sp.value_load(ids_row[0:1, bass.ds(first + b + B, 1)])
                        own(s.cat_w[:, b, :, :], "cat_w", "a p c n -> (a p) c n")
                        own(s.cat_b[:, b, :], "cat_b", "a p c -> (a p) c")
                for u in (0, 1):
                    sp.wait_ge(out_ready.sem, out_ready.at(t, 1, u))
                    keep(out, t * 2 + u, streams[u].out_t, out_stored[u])
            for u in (0, 1):
                sp.wait_ge(out_stored[u].sem, out_stored[u].at(PAIRS, 0))

        @block.gpsimd
        def _(pool):
            for z in zpads:
                nc.gpsimd.memset(z[:, :, :, 0:TAPS - 1], 0.0).then_inc(setup_pool.sem, 1)
            nc.gpsimd.memset(tern_qk[:, :, :, :], 0.0).then_inc(setup_pool.sem, 1)
            nc.gpsimd.memset(zeros, 0.0).then_inc(zeros_ready.sem, 1)
            for e in range(5):
                pool.dma_start(expert_w[:, e, :], dram["expert_w"][e]).then_inc(expert_in.sem, 16)
            slot_in_rows = slot_in_dram.rearrange("n p d -> (n p) d")
            slot_out_rows = slot_out_dram.rearrange("n p d -> (n p) d")
            pool.wait_ge(slots_zeroed.sem, 16)
            pool.wait_ge(sort_dve.sem, SLOT_STEPS)
            for t in range(TILES):
                pool.wait_ge(rows_got[t % 2].sem, rows_got[t % 2].at(t // 2, 16))
                for c in range(2):
                    for k in range(NS):
                        at = bass.IndirectOffsetOnAxis(ap=slots[:, c, t * NS + k:t * NS + k + 1], axis=0)
                        nc.gpsimd.indirect_dma_start(slot_in_rows, at, rows_in[t % 2][:, k, :], None,
                                                     bounds_check=SLOTS * P - 1).then_inc(scattered[t % 2].sem, 16)
            for p in (0, 1):
                pool.wait_ge(slot_stored[p].sem, slot_stored[p].at(SLOT_PAIRS, 0))
            for t in range(TILES):
                u = t % 2
                if t == 2:
                    pool.wait_ge(pe_picked_t.sem, pe_picked_t.at(0, 1, 0))
                if t == 3:
                    pool.wait_ge(out_ready.sem, out_ready.at(0, 1, 1))
                for c in range(2):
                    for k in range(NS):
                        at = bass.IndirectOffsetOnAxis(ap=slots[:, c, t * NS + k:t * NS + k + 1], axis=0)
                        nc.gpsimd.indirect_dma_start(streams[u].picked[c][:, k, :], None, slot_out_rows, at,
                                                     bounds_check=SLOTS * P - 1).then_inc(gathered[u].sem, 16)

        @block.scalar
        def _(act):
            a = nc.scalar.activation

            def setup(ins):
                setup_act.given += 1
                ins.then_inc(setup_act.sem, 1)
                act.wait_ge(setup_act.sem, setup_act.given)

            act.wait_ge(loads["early"].sem, 16 * N_EARLY)
            setup(a(decay[:, :], vecs[:, VEC["tau"][0]:VEC["tau"][0] + 1 + ND], ACT.Exp))
            setup(a(sm(0, 1, HEADS_B), col("slope", 0, HEADS_B), ACT.Abs))
            setup(a(sm(1, 1, HEADS_B), sm(0, 1, HEADS_B), ACT.Exp, scale=-1.0))
            act.wait_ge(setup_dve.sem, DVE_MAXIMA)
            setup(a(blend[:, :, :], blend[:, :, :], ACT.Exp))
            setup(a(deriv[:, 0:3], deriv[:, 0:3], ACT.Exp))
            act.wait_ge(setup_dve.sem, DVE_SLOPES)
            setup(a(time_w[:, :], time_w[:, :], ACT.Exp, scale=slope[:, 0:1]))

            chain = act_chain_1

            def step(t, ins, sig=None):
                sig = sig or chain
                sig.given += 1
                ins.then_inc(sig.sem, 1)
                act.wait_ge(sig.sem, t * period(sig) + (sig.before + sig.given))

            def condition(t):
                for u, s in enumerate(streams):
                    act.wait_ge(pe_soma.sem, pe_soma.at(t, 1, u))
                    step(t, a(s.h1, s.bank(0, p=HID), ACT.Gelu, bias=col("bn1", 0, HID)), h1_ready)
                    step(t, a(s.soma[:, 0, :], s.bank(1), ACT.Gelu, bias=col("bsoma", 0)))
                    step(t, a(s.soma[:, 1, :], s.bank(2), ACT.Gelu, bias=col("bsoma", 1)), soma_ready)
                for u, s in enumerate(streams):
                    act.wait_ge(pe_gate.sem, pe_gate.at(t, 1, u))
                    step(t, a(s.gate_t[:, 0, :], s.bank(3), ACT.Tanh, bias=half_b[:, 0:1], scale=0.5))
                    step(t, a(s.gate_t[:, 1, :], s.bank(0), ACT.Tanh, bias=half_b[:, 1:2], scale=0.5), gate_tanh)
                for u, s in enumerate(streams):
                    act.wait_ge(pe_mod.sem, pe_mod.at(t, 1, u))
                    step(t, a(s.mod, s.bank(1, p=ND), ACT.Tanh, bias=half_b[0:ND, 4:5], scale=0.5), mod_tanh)
                for u, s in enumerate(streams):
                    act.wait_ge(pe_trace_used.sem, pe_trace_used.at(t, ND, u))
                    step(t, a(s.temporal[:, :, :], s.bank(0, 2), ACT.Copy), temporal_ready)
                for u, s in enumerate(streams):
                    act.wait_ge(pe_temp.sem, pe_temp.at(t, 1, u))
                    step(t, a(s.gate_t[:, 0, :], s.bank(2), ACT.Tanh, bias=half_b[:, 2:3], scale=0.5))
                    step(t, a(s.gate_t[:, 1, :], s.bank(3), ACT.Tanh, bias=half_b[:, 3:4], scale=0.5), temp_tanh)
                for u, s in enumerate(streams):
                    act.wait_ge(cond_stats.sem, cond_stats.at(t, 1, u))
                    step(t, a(s.sm(0, NS), s.stat_var, ACT.Sqrt, bias=col("eps5"), scale=0.25), cond_std)
                for u, s in enumerate(streams):
                    act.wait_ge(pe_cond_t.sem, pe_cond_t.at(t, 1, u))
                    step(t, a(s.cond[:, 0, :], s.bank(2), ACT.Identity, bias=col("beta", 0), scale=col("gamma", 0)))
                    step(t, a(s.cond[:, 1, :], s.bank(3), ACT.Identity, bias=col("beta", 1), scale=col("gamma", 1)),
                         cond_ready)

            def z_out(t, s, bank, which, chunk, copied, p=P):
                step(t, a(s.conv[which][0:p, :], s.bank(bank, p=p), ACT.Identity,
                          bias=col("conv_b", chunk, p), scale=col("conv_k", TAPS * chunk + TAPS - 1, p)))
                step(t, a(s.zpad[0:p, which, :, TAPS - 1:], s.bank(bank, p=p).rearrange("p (b n) -> p b n", b=BT),
                          ACT.Copy), copied)

            def scan_attention(t):
                for u, s in enumerate(streams):
                    act.wait_ge(pe_s.sem, pe_s.at(t, 1, u))
                    z_out(t, s, 2, 0, 8, s_copied, HEADS_B)
                for u, s in enumerate(streams):
                    act.wait_ge(s_clipped.sem, s_clipped.at(t, 1, u))
                    step(t, a(s.p_t, s.conv[0][0:HEADS_B, :], ACT.Exp), p_exp)
                for u, s in enumerate(streams):
                    act.wait_ge(p_ready.sem, p_ready.at(t, 1, u))
                    act.wait_ge(pe_val.sem, pe_val.at(t, 1, u))
                    z_out(t, s, 0, 0, 0, val_copied)
                    act.wait_ge(pe_zg.sem, pe_zg.at(t, 1, u))
                    z_out(t, s, 1, 1, IC, zg_copied)
                for c in range(IC):
                    for u, s in enumerate(streams):
                        act.wait_ge(val_ready.sem, val_ready.at(t, c + 1, u))
                        step(t, a(s.turns, s.conv[0], ACT.Identity, bias=col("zero"), scale=theta_turns[:, c:c + 1]))
                        step(t, a(s.phi, s.conv[0], ACT.Identity, bias=col("zero"), scale=col("theta", c)), phi_ready)
                    for u, s in enumerate(streams):
                        act.wait_ge(gconv_ready.sem, gconv_ready.at(t, c + 1, u))
                        step(t, a(s.gtanh, s.conv[1], ACT.Tanh, scale=0.5), gtanh_ready)
                    for u, s in enumerate(streams):
                        act.wait_ge(angle_ready.sem, angle_ready.at(t, c + 1, u))
                        step(t, a(s.turns, s.conv[0], ACT.Identity, bias=deriv[:, 1:2], scale=deriv[:, 3:4]), linear_ready)
                    for u, s in enumerate(streams):
                        if c:
                            act.wait_ge(pe_sq.sem, pe_sq.at(t, c, u))
                        step(t, a(s.sin_t, s.angle, ACT.Sin))
                        step(t, a(s.angle, s.angle, ACT.Abs))
                        step(t, a(s.cos_t, s.angle, ACT.Sin, bias=col("half_pi"), scale=-1.0), trig_ready)
                    if c + 1 < IC:
                        for u, s in enumerate(streams):
                            act.wait_ge(pe_val.sem, pe_val.at(t, c + 2, u))
                            z_out(t, s, 2, 0, c + 1, val_copied)
                        for u, s in enumerate(streams):
                            z_out(t, s, 1, 1, IC + c + 1, zg_copied)
                    for u, s in enumerate(streams):
                        act.wait_ge(mean_ready.sem, mean_ready.at(t, c + 1, u))
                        step(t, a(s.sin_t, s.mean_im, ACT.Square))
                        step(t, a(s.cos_t, s.mean_re, ACT.Square), sq_ready)
                for u, s in enumerate(streams):
                    act.wait_ge(pe_sq.sem, pe_sq.at(t, IC, u))
                    step(t, a(s.rms_b, s.bank(3, p=HEADS_B), ACT.Sqrt, bias=col("eps5", 0, HEADS_B)), rms_sqrt)

            def pool_prompt(t):
                for u, s in enumerate(streams):
                    act.wait_ge(pe_x1_rows.sem, pe_x1_rows.at(t, 1, u))
                    step(t, a(s.x1_rows, s.token_banks(2), ACT.Copy), x1_rows_ready)
                    act.wait_ge(pe_score_hid.sem, pe_score_hid.at(t, 1, u))
                    step(t, a(s.score_h, s.bank(0, p=HID), ACT.Tanh, bias=col("b1", 0, HID)), score_hid)
                for u, s in enumerate(streams):
                    act.wait_ge(score_max.sem, score_max.at(t, 1, u))
                    for g in range(4):
                        step(t, a(s.pool_w[:, g, :], s.masked[:, g, :], ACT.Exp, bias=s.sm(8 + g, 1),
                                  accum_out=s.sm(12 + g, 1)), pool_exp if g == 3 else None)
                for u, s in enumerate(streams):
                    act.wait_ge(pe_pool_t.sem, pe_pool_t.at(t, 1, u))
                    step(t, a(s.pool_wt, s.bank(2, 2), ACT.Copy), pool_t)
                for u, s in enumerate(streams):
                    act.wait_ge(pe_pool.sem, pe_pool.at(t, 1, u))
                    step(t, a(s.pooled, s.bank(0, 2), ACT.Copy), pool_ready)

                for u, s in enumerate(streams):
                    act.wait_ge(top_ready.sem, top_ready.at(t, 1, u))
                    step(t, a(s.sm(160, NS), s.sm(160, NS), ACT.Exp), route_exp)
                for u, s in enumerate(streams):
                    act.wait_ge(pe_pool_rows.sem, pe_pool_rows.at(t, 1, u))
                    step(t, a(s.pooled_rows, s.token_banks(2), ACT.Copy), pool_rows_ready)

            def shared_expert(t):
                for n in range(2 * FC):
                    act.wait_ge(pe_up.sem, pe_up.at(t, n + 1))
                    step(t, a(act_h[n % 2], psum[:, 3 + n % 2, :], ACT.Tanh, scale=0.5), h_tanh)

            def slot_tanh_of(i, k):
                q = k % 2
                act.wait_ge(pe_slot_h.sem, pe_slot_h.at(i, k + 1))
                a(slot_h[q], psum[:, q, :], ACT.Tanh, scale=0.5).then_inc(slot_tanh.sem, 1)

            def slot_out_of(i, k):
                q = k % 2
                act.wait_ge(pe_slot_g_t.sem, pe_slot_g_t.at(i, k + 1))
                a(slot_g_t[q], psum[:, 4, :].rearrange("p (c n) -> p c n", c=FC), ACT.Copy).then_inc(slot_g_t_ready.sem, 1)
                act.wait_ge(pe_slot_out.sem, pe_slot_out.at(i, k + 1))
                act.wait_ge(slot_stored[q].sem, slot_stored[q].at(i, 0))
                a(slot_out[:, q, :], psum[:, 6, 0:D], ACT.Copy).then_inc(slot_out_ready.sem, 1)
                act.wait_ge(slot_out_ready.sem, slot_out_ready.at(i, k + 1))
                act.dma_start(slot_out_dram[bass.ds(i * 2 + k, 1)].rearrange("a p d -> (a p) d"), slot_out[:, q, :]) \
                    .then_inc(slot_stored[q].sem, 16)

            def adapter(t):
                for u, s in enumerate(streams):
                    act.wait_ge(pe_bottle.sem, pe_bottle.at(t, 1, u))
                    for b in range(BT):
                        step(t, a(s.bottle[:, b * S:(b + 1) * S], s.bank(0)[:, b * S:(b + 1) * S], ACT.Relu,
                                  bias=s.adapt_bd[:, b:b + 1]), bottle_ready if b else None)
                for u, s in enumerate(streams):
                    act.wait_ge(adapt_stats.sem, adapt_stats.at(t, 1, u))
                    step(t, a(s.sm(0, NS), s.stat_var, ACT.Sqrt, bias=col("eps5")), adapt_std)

            def mean_square(t, s, rows, scratch, done):
                for k in range(NS):
                    step(t, a(scratch[:, k, :], rows[:, k, :], ACT.Square, accum_out=s.sm(200 + k, 1)))
                step(t, a(s.sm(204, NS), s.sm(200, NS), ACT.Sqrt, bias=col("eps6"), scale=1.0 / D), done)

            def attention(t):
                for u, s in enumerate(streams):
                    act.wait_ge(adapt_ready.sem, adapt_ready.at(t, 1, u))
                    mean_square(t, s, s.attn_in, s.adapt_y, rms_in)
                for g in range(3):
                    for u, s in enumerate(streams):
                        act.wait_ge(pe_int_t.sem, pe_int_t.at(t, g + 1, u))
                        step(t, a(s.int_tt, s.bank_b(0, 2), ACT.Copy), int_t)
                    for u, s in enumerate(streams):
                        if g == 0:
                            act.wait_ge(pe_q.sem, pe_q.at(t, 1, u))
                            step(t, a(s.q_t, s.bank(0, 4), ACT.Copy), q_ready)
                        if g == 1:
                            act.wait_ge(pe_scale.sem, pe_scale.at(t, 1, u))
                            step(t, a(s.kscale_b, s.bank(2), ACT.Copy), scale_ready)
                def probs_out(n, u, s):
                    g = group(n)
                    act.wait_ge(row_max.sem, row_max.at(t, n + 1, u))
                    if n >= 2:
                        act.wait_ge(pe_probs_t.sem, pe_probs_t.at(t, n - 1, u))
                    for j, head in enumerate(g.heads):
                        cols = slice(j * g.width, (j + 1) * g.width)
                        step(t, a(s.probs[n % 2][:, cols], s.bank(n % 2)[:, cols], ACT.Exp,
                                  bias=s.sm(320 + g.s * NH + head, 1), scale=s.sm(216 + g.s, 1),
                                  accum_out=s.sm(384 + g.s * NH + head, 1)), probs_ready if j == len(g.heads) - 1 else None)

                for n in range(NG + 1):
                    if n < NG:
                        for u, s in enumerate(streams):
                            probs_out(n, u, s)
                    if n and group(n - 1).last:
                        for u, s in enumerate(streams):
                            act.wait_ge(pe_heads.sem, pe_heads.at(t, n, u))
                            step(t, a(s.heads_t, s.bank(3), ACT.Copy), heads_t_ready)
                for u, s in enumerate(streams):
                    act.wait_ge(heads_ready.sem, heads_ready.at(t, 2 * BT, u))
                    mean_square(t, s, s.head_out, s.scaled_in, rms_in)
                for u, s in enumerate(streams):
                    act.wait_ge(pe_int_t.sem, pe_int_t.at(t, 4, u))
                    step(t, a(s.y_tt, s.bank_b(0, 2), ACT.Copy), int_t)
                    act.wait_ge(pe_scale.sem, pe_scale.at(t, 2, u))
                    step(t, a(s.yscale_b, s.bank(2), ACT.Copy), scale_ready)

            def last_ffn(t):
                for u, s in enumerate(streams):
                    act.wait_ge(pe_f8.sem, pe_f8.at(t, 1, u))
                    step(t, a(s.half_t, s.bank(2, 2), ACT.Copy), half_ready)

            with act.Fori(0, PAIRS) as t:
                condition(t)
                scan_attention(t)
                pool_prompt(t)
            with act.Fori(0, PAIRS) as t:
                shared_expert(t)
            slot_tanh_of(0, 0)
            with act.Fori(0, SLOT_PAIRS - 1) as i:
                for k in (1, 2):
                    slot_tanh_of(i, k)
                    slot_out_of(i, k - 1)
            slot_tanh_of(SLOT_PAIRS - 1, 1)
            slot_out_of(SLOT_PAIRS - 1, 0)
            slot_out_of(SLOT_PAIRS - 1, 1)
            chain = act_chain_3
            with act.Fori(0, PAIRS) as t:
                adapter(t)
                attention(t)
                last_ffn(t)

        @block.vector
        def _(dve):
            v = nc.vector

            def setup(ins):
                setup_dve.given += 1
                ins.then_inc(setup_dve.sem, 1)
                dve.wait_ge(setup_dve.sem, setup_dve.given)

            def round_to_even(dst, src):
                return v.tensor_scalar(dst, src, MAGIC, MAGIC, ALU.add, ALU.subtract)

            dve.wait_ge(loads["early"].sem, 16 * N_EARLY)
            at, n = VEC["blend"]
            raw_blend = vecs[:, at:at + n].rearrange("p (c d) -> p c d", c=DC)
            setup(v.tensor_reduce(out=sm(20, DC), in_=raw_blend, axis=AX.X, op=ALU.max))
            setup(v.tensor_tensor(blend[:, :, :], raw_blend, sm(20, DC)[:, :, None].broadcast_to([P, DC, ND]), ALU.subtract))
            at, n = VEC["deriv"]
            setup(v.tensor_reduce(out=sm(22, 1), in_=vecs[:, at:at + n], axis=AX.X, op=ALU.max))
            setup(v.tensor_scalar(deriv[:, 0:3], vecs[:, at:at + n], sm(22, 1), None, ALU.subtract))
            assert setup_dve.given == DVE_MAXIMA
            at = VEC["bg"][0]
            setup(v.tensor_scalar(half_b[:, 0:2 * DC], vecs[:, at:at + 2 * DC], 0.5, None, ALU.mult))
            setup(v.tensor_scalar(half_b[0:ND, 2 * DC:2 * DC + 1], col("bn2", 0, ND), 0.5, None, ALU.mult))
            at = VEC["theta"][0]
            setup(v.tensor_scalar(theta_turns[:, :], vecs[:, at:at + IC], 1.0 / TWO_PI, None, ALU.mult))
            act_u, s1, s2, acc, r = (sm(k, 1, HEADS_B) for k in (1, 2, 3, 4, 5))
            dve.wait_ge(setup_act.sem, 3)
            setup(v.tensor_scalar(s1, act_u, 2.0, None, ALU.add))
            setup(v.reciprocal(s1, s1))
            setup(v.tensor_tensor(s1, s1, act_u, ALU.mult))
            setup(v.tensor_tensor(s2, s1, s1, ALU.mult))
            setup(v.tensor_scalar(acc, s2, 1.0 / 19, 1.0 / 17, ALU.mult, ALU.add))
            for k in (15, 13, 11, 9, 7, 5, 3, 1):
                setup(v.tensor_scalar(acc, acc, s2, 1.0 / k, ALU.mult, ALU.add))
            setup(v.tensor_tensor(acc, acc, s1, ALU.mult))
            setup(v.tensor_scalar(r, col("slope", 0, HEADS_B), 0.0, None, ALU.max))
            setup(v.scalar_tensor_tensor(slope[:, :], acc, -2.0, r, ALU.mult, ALU.subtract))
            assert setup_dve.given == DVE_SLOPES
            setup(v.tensor_scalar(decay[:, :], decay[:, :], 1.0, None, ALU.add))
            setup(v.reciprocal(decay[:, :], decay[:, :]))
            dve.wait_ge(setup_act.sem, 5)
            setup(v.tensor_reduce(out=sm(20, DC), in_=blend[:, :, :], axis=AX.X, op=ALU.add))
            setup(v.reciprocal(sm(20, DC), sm(20, DC)))
            setup(v.tensor_tensor(blend[:, :, :], blend[:, :, :], sm(20, DC)[:, :, None].broadcast_to([P, DC, ND]),
                                  ALU.mult))
            setup(v.tensor_scalar(blend[:, :, :], blend[:, :, :], 0.5, None, ALU.mult))
            setup(v.tensor_reduce(out=sm(22, 1), in_=deriv[:, 0:3], axis=AX.X, op=ALU.add))
            setup(v.reciprocal(sm(22, 1), sm(22, 1)))
            setup(v.tensor_scalar(deriv[:, 0:3], deriv[:, 0:3], sm(22, 1), None, ALU.mult))
            setup(v.tensor_scalar(deriv[:, 3:4], deriv[:, 2:3], -1.0, None, ALU.mult))
            dve.wait_ge(loads["mid"].sem, 16 * N_MID)
            setup(v.tensor_scalar(w["w_re"][:, :], w["w_re"][:, :], col("norm_re"), 0.5, ALU.mult, ALU.mult))
            setup(v.tensor_scalar(w["w_im"][:, :], w["w_im"][:, :], col("norm_im"), 0.5, ALU.mult, ALU.mult))
            setup(v.tensor_copy(sm(40, B), kind_ids[:, :]))
            setup(v.tensor_scalar(kind[:, :, 0], sm(40, B), 0.0, None, ALU.is_equal))
            setup(v.tensor_scalar(kind[:, :, 1], sm(40, B), 1.0, None, ALU.is_equal))
            setup(v.tensor_tensor(kind[:, :, 2], kind[:, :, 0], kind[:, :, 1], ALU.add))
            setup(v.tensor_scalar(kind[:, :, 2], kind[:, :, 2], -1.0, 1.0, ALU.mult, ALU.add))
            setup(v.tensor_copy(ident_b[:, :], w["ident"][:, :]))
            dve.wait_ge(loads["attn"].sem, 16 * 4)
            setup(v.tensor_copy(pool_mask[:, :, :, :], raw_mask))
            dve.wait_ge(setup_pool.sem, 3)
            setup(v.tensor_copy(causal_a[:, :].rearrange("p (k n) -> p k n", k=4),
                                w["causal"][:, None, :].broadcast_to([P, 4, P])))
            setup(v.tensor_reduce(out=sm(44, 4), in_=raw_qkvo.rearrange("p k c d -> p k (c d)"), axis=AX.X, op=ALU.add,
                                  apply_absolute_value=True))
            assert setup_dve.given == DVE_SUMS
            dve.wait_ge(setup_pe.sem, 1)
            setup(v.tensor_scalar(w_scale[:, 0:4], psum[:, 0, 0:4], 1.0 / (D * D), 1e-5, ALU.mult, ALU.max))
            assert setup_dve.given == DVE_SUMS + 1
            setup(v.reciprocal(w_scale[:, 4:8], w_scale[:, 0:4]))
            setup(v.tensor_scalar(qk_scale[:, :], w_scale[:, 0:1], w_scale[:, 1:2], HD ** -0.5, ALU.mult, ALU.mult))
            for k in range(4):
                raw = raw_qkvo[:, k, :, :]
                setup(v.tensor_scalar(raw, raw, w_scale[:, 4 + k:5 + k], MAGIC, ALU.mult, ALU.add))
                setup(v.tensor_scalar(raw, raw, MAGIC, 1.0, ALU.subtract, ALU.min))
                if k < 2:
                    for c in range(DC):
                        setup(v.tensor_scalar(tern_qk[:, k, c, :].rearrange("p (h d) -> p h d", h=NH)[:, :, 0:HD],
                                              raw[:, c, :].rearrange("p (h d) -> p h d", h=NH), -1.0, None, ALU.max))
                else:
                    setup(v.tensor_scalar(tern_vo[:, k - 2, :, :], raw, -1.0, None, ALU.max))

            def float8_values(run, val, tmp, dst):
                run(v.tensor_scalar(val, val, 448.0, -448.0, ALU.min, ALU.max))
                run(v.tensor_scalar(tmp.bitcast(I32), val.bitcast(I32), 0x7F800000, None, ALU.bitwise_and))
                run(v.tensor_scalar(tmp, tmp, 2.0 ** -6, 1.5 * 2.0 ** 20, ALU.max, ALU.mult))
                run(v.tensor_tensor(val, val, tmp, ALU.add))
                run(v.tensor_tensor(dst, val, tmp, ALU.subtract))

            float8_values(setup, raw_f8, f8_tmp, f8_w[:, :, :].rearrange("p c d -> p (c d)"))

            chain = dve_chain_1

            def step(t, ins, sig=None, wait=True):
                sig = sig or chain
                sig.given += 1
                ins.then_inc(sig.sem, 1)
                at = (sig.sem, t * period(sig) + (sig.before + sig.given))
                if wait:
                    dve.wait_ge(*at)
                return at

            def averages(t, dst, src, decay_col, last):
                for c in range(DC):
                    for b in range(BT):
                        tokens = slice(b * S, (b + 1) * S)
                        end = (c, b) == (DC - 1, BT - 1)
                        step(t, v.tensor_tensor_scan(dst[:, c, tokens], decay_col.broadcast_to([P, S]), src[:, c, tokens],
                                                     0.0, ALU.mult, ALU.add), last if end else None, wait=end)

            def row_stats(t, s, rows, last):
                for k in range(NS):
                    step(t, v.bn_stats(s.sm(32 + 6 * k, 6), rows[:, k, :]), wait=k == NS - 1)
                step(t, v.memset(s.sm(620, 1), 0.0), wait=False)
                for k in range(NS):
                    end = k == NS - 1
                    step(t, v.bn_aggr(s.sm(24 + 2 * k, 2), s.sm(32 + 6 * k, 6)), last if end else None, wait=end)

            def condition(t):
                for u, s in enumerate(streams):
                    dve.wait_ge(x_in[u].sem, x_in[u].at(t, 16))
                    averages(t, s.ctx_t, s.x, decay[:, 0:1], ctx_ready)
                for u, s in enumerate(streams):
                    dve.wait_ge(gate_tanh.sem, gate_tanh.at(t, 1, u))
                    step(t, v.scalar_tensor_tensor(s.gated, s.gate_t, 1.0, s.x, ALU.add, ALU.mult), wait=False)
                for u, s in enumerate(streams):
                    dve.wait_ge(mod_tanh.sem, mod_tanh.at(t, 1, u))
                    step(t, v.tensor_scalar(s.mod, s.mod, 0.5, 1.0, ALU.mult, ALU.add), mod_ready)
                for d in range(ND):
                    for u, s in enumerate(streams):
                        dve.wait_ge(pe_mod_rows.sem, pe_mod_rows.at(t, d + 1, u))
                        for c in range(DC):
                            step(t, v.scalar_tensor_tensor(s.scaled[d % 2][:, c, :], s.gated[:, c, :], blend[:, c, d:d + 1],
                                                           s.bank(2 + d % 2), ALU.mult, ALU.mult), wait=c == DC - 1)
                        if d == 0:
                            dve.wait_ge(pooled_stored[u].sem, pooled_stored[u].at(t, 0))
                        if d >= 2:
                            dve.wait_ge(pe_trace_used.sem, pe_trace_used.at(t, d - 1, u))
                        averages(t, s.trace[d % 2], s.scaled[d % 2], decay[:, 1 + d:2 + d], trace_ready)
                for u, s in enumerate(streams):
                    dve.wait_ge(temp_tanh.sem, temp_tanh.at(t, 1, u))
                    step(t, v.scalar_tensor_tensor(s.gate_t, s.gate_t, 1.0, s.soma, ALU.add, ALU.mult), mixed_ready)
                for u, s in enumerate(streams):
                    dve.wait_ge(pe_cond.sem, pe_cond.at(t, 1, u))
                    row_stats(t, s, s.token_banks(0), cond_stats)
                for u, s in enumerate(streams):
                    dve.wait_ge(cond_std.sem, cond_std.at(t, 1, u))
                    step(t, v.reciprocal(s.sm(4, NS), s.sm(0, NS)))
                    step(t, v.tensor_scalar(s.sm(4, NS), s.sm(4, NS), 0.5, None, ALU.mult))
                    for k in range(NS):
                        end = k == NS - 1
                        step(t, v.tensor_scalar(s.cond_rows[:, k, :], s.token_banks(0)[:, k, :], s.stat[:, k, 0:1],
                                                s.sm(4 + k, 1), ALU.subtract, ALU.mult), cond_norm if end else None, wait=end)

            def tap(t, s, which, chunk, p, j, last):
                acc = s.conv[which][0:p, :].rearrange("p (b n) -> p b n", b=BT)
                return step(t, v.scalar_tensor_tensor(acc, s.zpad[0:p, which, :, j:j + S],
                                                      col("conv_k", TAPS * chunk + j, p), acc, ALU.mult, ALU.add),
                            last if j == TAPS - 2 else None, wait=False)

            def scan_attention(t):
                one = w["ones"][:, 0:1]
                done = [None, None]
                for j in range(TAPS - 1):
                    for u, s in enumerate(streams):
                        if j:
                            dve.wait_ge(*done[u])
                        else:
                            dve.wait_ge(s_copied.sem, s_copied.at(t, 1, u))
                        done[u] = tap(t, s, 0, 8, HEADS_B, j, None)
                for u, s in enumerate(streams):
                    raw = s.conv[0][0:HEADS_B, :]
                    dve.wait_ge(*done[u])
                    done[u] = step(t, v.tensor_scalar(raw, raw, col("score_scale", 0, HEADS_B), 20.0, ALU.mult, ALU.min),
                                   wait=False)
                for u, s in enumerate(streams):
                    raw = s.conv[0][0:HEADS_B, :]
                    dve.wait_ge(*done[u])
                    step(t, v.tensor_scalar(raw, raw, -20.0, None, ALU.max), s_clipped, wait=False)
                for u, s in enumerate(streams):
                    dve.wait_ge(p_exp.sem, p_exp.at(t, 1, u))
                    by_batch = s.p_t.rearrange("p (b n) -> p b n", b=BT)
                    step(t, v.tensor_tensor(by_batch, by_batch, time_w[:, None, :].broadcast_to([HEADS_B, BT, S]), ALU.mult))
                    for b in range(BT):
                        tokens = slice(b * S, (b + 1) * S)
                        step(t, v.tensor_tensor_scan(s.inv_den[:, tokens], one[0:HEADS_B, :].broadcast_to([HEADS_B, S]),
                                                     s.p_t[:, tokens], 0.0, ALU.mult, ALU.add), wait=b == BT - 1)
                    step(t, v.tensor_scalar(s.inv_den, s.inv_den, 1e-4, None, ALU.max))
                    step(t, v.reciprocal(s.inv_den, s.inv_den), p_ready)
                def convolutions(c):
                    for u, s in enumerate(streams):
                        done = [None, None]
                        dve.wait_ge(val_copied.sem, val_copied.at(t, c + 1, u))
                        for j in range(TAPS - 1):
                            for which, chunk, last in ((0, c, val_ready), (1, IC + c, gconv_ready)):
                                if j:
                                    dve.wait_ge(*done[which])
                                elif which:
                                    dve.wait_ge(zg_copied.sem, zg_copied.at(t, c + 1, u))
                                done[which] = tap(t, s, which, chunk, P, j, last)

                convolutions(0)
                for c in range(IC):
                    done = [None, None]
                    for u, s in enumerate(streams):
                        dve.wait_ge(phi_ready.sem, phi_ready.at(t, c + 1, u))
                        done[u] = step(t, round_to_even(s.turns, s.turns), wait=False)
                    for part in (TWO_PI_HI, TWO_PI_LO):
                        for u, s in enumerate(streams):
                            dve.wait_ge(*done[u])
                            done[u] = step(t, v.scalar_tensor_tensor(s.phi, s.turns, -part, s.phi, ALU.mult, ALU.add),
                                           wait=False)
                    for u, s in enumerate(streams):
                        dve.wait_ge(*done[u])
                        step(t, v.tensor_scalar(s.angle, s.phi, PI_SAFE, -PI_SAFE, ALU.min, ALU.max), angle_ready, wait=False)
                    for u, s in enumerate(streams):
                        dve.wait_ge(gtanh_ready.sem, gtanh_ready.at(t, c + 1, u))
                        step(t, v.scalar_tensor_tensor(s.gate_s, s.gtanh, 1.0, s.conv[1], ALU.add, ALU.mult), wait=False)
                    for u, s in enumerate(streams):
                        dve.wait_ge(linear_ready.sem, linear_ready.at(t, c + 1, u))
                        done[u] = step(t, v.tensor_tensor(s.turns, s.turns, s.conv[0], ALU.mult), wait=False)
                    for u, s in enumerate(streams):
                        dve.wait_ge(pe_p_rows.sem, pe_p_rows.at(t, c + 1, u))
                        dve.wait_ge(*done[u])
                        step(t, v.scalar_tensor_tensor(s.phi, s.turns, deriv[:, 0:1], s.bank(2), ALU.add, ALU.mult),
                             product_ready, wait=False)
                    for u, s in enumerate(streams):
                        dve.wait_ge(product_ready.sem, product_ready.at(t, c + 1, u))
                        dve.wait_ge(trig_ready.sem, trig_ready.at(t, c + 1, u))
                        weighed = [step(t, v.tensor_tensor(part, s.phi, part, ALU.mult), wait=False)
                                   for part in (s.cos_t, s.sin_t)]
                        summed = []
                        for mean, part, at in ((s.mean_re, s.cos_t, weighed[0]), (s.mean_im, s.sin_t, weighed[1])):
                            dve.wait_ge(*at)
                            for b in range(BT):
                                tokens = slice(b * S, (b + 1) * S)
                                at = step(t, v.tensor_tensor_scan(mean[:, tokens], one.broadcast_to([P, S]), part[:, tokens],
                                                                  0.0, ALU.mult, ALU.add), wait=False)
                            summed.append(at)
                        for mean, at in zip((s.mean_re, s.mean_im), summed):
                            dve.wait_ge(*at)
                            step(t, v.tensor_tensor(mean, mean, s.bank(0), ALU.mult), mean_ready if mean is s.mean_im else None,
                                 wait=False)
                    if c + 1 < IC:
                        convolutions(c + 1)
                    for u, s in enumerate(streams):
                        dve.wait_ge(pe_y.sem, pe_y.at(t, c + 1, u))
                        step(t, v.tensor_tensor(s.yg[:, c, :], s.bank(0), s.gate_s, ALU.mult), yg_ready, wait=False)
                for u, s in enumerate(streams):
                    dve.wait_ge(rms_sqrt.sem, rms_sqrt.at(t, 1, u))
                    step(t, v.reciprocal(s.rms_b, s.rms_b), rms_ready)
                for u, s in enumerate(streams):
                    dve.wait_ge(pe_rms_rows.sem, pe_rms_rows.at(t, 1, u))
                    step(t, v.tensor_tensor(s.yg, s.yg, s.bank(0, 4), ALU.mult), ynorm_ready)
                for u, s in enumerate(streams):
                    dve.wait_ge(pe_proj.sem, pe_proj.at(t, 1, u))
                    step(t, v.tensor_tensor(s.x, s.x, s.bank(0, 2), ALU.add), x1_ready)

            def pool_prompt(t):
                for u, s in enumerate(streams):
                    now = s.sm(600, 3 * BT)
                    step(t, v.tensor_copy(now.rearrange("p (b k) -> p b k", b=BT), kind[:, bass.ds((t * 2 + u) * BT, BT), :]))
                for u, s in enumerate(streams):
                    for b in range(BT):
                        cnt = s.sm(56 + 2 * b, 2)
                        step(t, v.tensor_scalar(cnt, w["pool_count"][:, 0, :], s.sm(600 + 3 * b, 1), None, ALU.mult))
                        for k in (1, 2):
                            step(t, v.scalar_tensor_tensor(cnt, w["pool_count"][:, k, :], s.sm(600 + 3 * b + k, 1), cnt,
                                                           ALU.mult, ALU.add))
                for u, s in enumerate(streams):
                    dve.wait_ge(pe_score.sem, pe_score.at(t, 1, u))
                    done = [None, None]
                    for k in range(3):
                        for b in range(BT):
                            dst = s.masked[:, 2 * b:2 * b + 2, :]
                            if k:
                                dve.wait_ge(*done[b])
                            src = dst if k else s.bank(1)[:, b * S:(b + 1) * S][:, None, :].broadcast_to([P, 2, S])
                            done[b] = step(t, v.scalar_tensor_tensor(dst, pool_mask[:, k, :, :], s.sm(600 + 3 * b + k, 1), src,
                                                                     ALU.mult, ALU.add), wait=k == 2 and b == 1)
                    step(t, v.tensor_reduce(out=s.sm(8, 4), in_=s.masked, axis=AX.X, op=ALU.max, negate=True), score_max)
                for u, s in enumerate(streams):
                    dve.wait_ge(pool_exp.sem, pool_exp.at(t, 1, u))
                    step(t, v.tensor_tensor(s.sm(12, 4), s.sm(12, 4), s.sm(56, 4), ALU.mult))
                    step(t, v.reciprocal(s.sm(12, 4), s.sm(12, 4)))
                    for g in range(4):
                        step(t, v.tensor_scalar(s.pool_w[:, g, :], s.pool_w[:, g, :], s.sm(12 + g, 1), None, ALU.mult),
                             pool_p if g == 3 else None, wait=g == 3)

            def route(t):
                number = w["expert_no"][:, :, :]
                top1, top2, which, e2, w1, w2 = 164, 168, 172, 160, 176, 180
                done = [None, None]

                def cols(s, at):
                    return s.sm(at, NS * NE).rearrange("p (s e) -> p s e", s=NS)

                def wide(s, at):
                    return s.sm(at, NS)[:, :, None].broadcast_to([P, NS, NE])

                score, tmp = 64, 128
                for u, s in enumerate(streams):
                    dve.wait_ge(pe_route.sem, pe_route.at(t, 1, u))
                    done[u] = step(t, v.tensor_copy(cols(s, score), s.bank(0)[:, 0:NS * NE].rearrange("p (s e) -> p s e", s=NS)),
                                   wait=False)
                for top, onehot in ((top1, 256), (top2, 288)):
                    for u, s in enumerate(streams):
                        dve.wait_ge(*done[u])
                        done[u] = step(t, v.tensor_reduce(out=s.sm(top, NS), in_=cols(s, score), axis=AX.X, op=ALU.max),
                                       wait=False)
                    for u, s in enumerate(streams):
                        dve.wait_ge(*done[u])
                        done[u] = step(t, v.tensor_tensor(cols(s, tmp), cols(s, score), wide(s, top), ALU.is_lt), wait=False)
                    for u, s in enumerate(streams):
                        dve.wait_ge(*done[u])
                        done[u] = step(t, v.scalar_tensor_tensor(cols(s, tmp), cols(s, tmp), float(NE), number,
                                                                 ALU.mult, ALU.add), wait=False)
                    for u, s in enumerate(streams):
                        dve.wait_ge(*done[u])
                        done[u] = step(t, v.tensor_reduce(out=s.sm(which, NS), in_=cols(s, tmp), axis=AX.X, op=ALU.min),
                                       wait=False)
                    for u, s in enumerate(streams):
                        dve.wait_ge(*done[u])
                        done[u] = step(t, v.tensor_tensor(cols(s, onehot), number, wide(s, which), ALU.is_equal), wait=False)
                    if top == top1:
                        for u, s in enumerate(streams):
                            dve.wait_ge(*done[u])
                            done[u] = step(t, v.scalar_tensor_tensor(cols(s, score), cols(s, onehot), -3e38, cols(s, score),
                                                                     ALU.mult, ALU.add), wait=False)
                for u, s in enumerate(streams):
                    step(t, v.tensor_tensor(s.sm(e2, NS), s.sm(top2, NS), s.sm(top1, NS), ALU.subtract), top_ready, wait=False)
                for u, s in enumerate(streams):
                    dve.wait_ge(route_exp.sem, route_exp.at(t, 1, u))
                    done[u] = step(t, v.tensor_scalar(s.sm(w1, NS), s.sm(e2, NS), 1.0, None, ALU.add), wait=False)
                for u, s in enumerate(streams):
                    dve.wait_ge(*done[u])
                    done[u] = step(t, v.reciprocal(s.sm(w1, NS), s.sm(w1, NS)), wait=False)
                for u, s in enumerate(streams):
                    dve.wait_ge(*done[u])
                    step(t, v.tensor_tensor(s.sm(w2, NS), s.sm(e2, NS), s.sm(w1, NS), ALU.mult))
                for u, s in enumerate(streams):
                    at = bass.ds((t * 2 + u) * NS, NS)
                    step(t, v.tensor_copy(shares[:, :, at], s.sm(w1, 2 * NS)[:, 0:2 * NS].rearrange("p (c s) -> p c s", c=2)))
                    step(t, v.tensor_copy(picks[:, :, at, :],
                                          s.sm(256, 2 * NS * NE).rearrange("p (c s e) -> p c s e", c=2, s=NS)), picks_ready)

            def order():
                def sort(ins):
                    sort_dve.given += 1
                    ins.then_inc(sort_dve.sem, 1)
                    dve.wait_ge(sort_dve.sem, sort_dve.given)

                N = NE * BLOCKS
                a, b = streams[0].sm, streams[1].sm

                def cols(t):
                    return t.rearrange("p (e k) -> p e k", e=NE)

                both, count, run, tmp = a(0, N), a(N, N), a(2 * N, N), a(3 * N, N)
                total, blocks, end, shift = (b(NE * k, NE) for k in range(4))
                sort(v.tensor_tensor(both.rearrange("p (e k) -> p k e", e=NE), picks[:, 0, :, :], picks[:, 1, :, :], ALU.add))
                dve.wait_ge(sort_pe.sem, 2)
                sort(v.tensor_copy(count, psum[:, 1, 0:N]))
                one = w["ones"][:, 0:1].broadcast_to([P, N])
                sort(v.tensor_tensor_scan(run, one, count, 0.0, ALU.mult, ALU.add))
                sort(v.tensor_reduce(out=total, in_=cols(count), axis=AX.X, op=ALU.add))
                sort(v.tensor_scalar(blocks, total, 1.0 / P, (P - 1) / P - 0.5 + 0.5 / P, ALU.mult, ALU.add))
                sort(round_to_even(blocks, blocks))
                sort(v.tensor_tensor_scan(end, one[:, 0:NE], blocks, 0.0, ALU.mult, ALU.add))
                sort(v.tensor_tensor(shift, end, blocks, ALU.subtract))
                sort(v.tensor_scalar(shift, shift, float(P), None, ALU.mult))
                sort(v.tensor_tensor(shift, shift, total, ALU.add))
                sort(v.tensor_tensor(shift, shift, cols(run)[:, :, BLOCKS - 1], ALU.subtract))
                sort(v.tensor_tensor(run, run, count, ALU.subtract))
                sort(v.tensor_tensor(run, run, psum[:, 0, 0:N], ALU.add))
                sort(v.tensor_tensor(cols(run), cols(run), shift[:, :, None].broadcast_to([P, NE, BLOCKS]), ALU.add))
                for c in range(2):
                    sort(v.tensor_tensor(cols(tmp), cols(run), picks[:, c, :, :].rearrange("p k e -> p e k"), ALU.mult))
                    sort(v.tensor_reduce(out=b(64, BLOCKS), in_=tmp.rearrange("p (e k) -> p k e", e=NE), axis=AX.X, op=ALU.add))
                    sort(v.tensor_copy(slots[:, c, :], b(64, BLOCKS)))
                assert sort_dve.given == SLOT_STEPS
                ended = b(128, SLOTS * (NE - 1), 1).rearrange("p (j e) -> p j e", j=SLOTS)
                dve.wait_ge(order_in.sem, 32)
                sort(v.tensor_tensor(ended, slot_block,
                                     end[0:1, None, 0:NE - 1].broadcast_to([1, SLOTS, NE - 1]), ALU.is_ge))
                sort(v.tensor_reduce(out=b(416, SLOTS, 1), in_=ended, axis=AX.X, op=ALU.add))
                sort(v.tensor_scalar(b(416, SLOTS, 1), b(416, SLOTS, 1), 1.0, None, ALU.add))
                sort(v.tensor_copy(slot_expert[:, :], b(416, SLOTS, 1)))

            def shared_expert(t):
                for u in (0, 1):
                    for m in range(FC):
                        n = u * FC + m
                        dve.wait_ge(h_tanh.sem, h_tanh.at(t, n + 1))
                        step(t, v.scalar_tensor_tensor(act_h[n % 2], act_h[n % 2], 1.0, psum[:, 3 + n % 2, :],
                                                       ALU.add, ALU.mult), h_read)
                        step(t, v.scalar_tensor_tensor(g_buf[:, m, :], act_h[n % 2], 0.5, psum[:, 5 + n % 2, :],
                                                       ALU.mult, ALU.mult), g_ready)
                    dve.wait_ge(pe_down.sem, pe_down.at(t, u + 1))
                    x1 = x1_in[u]
                    v.tensor_tensor(x1[:, 0, :], x1[:, 0, :], psum[:, 0, :], ALU.add)
                    step(t, v.tensor_tensor(x1[:, 1, :], x1[:, 1, :], psum[:, 7, :], ALU.add), x2_ready)

            def slot_gate(i, k):
                q = k % 2
                dve.wait_ge(slot_tanh.sem, slot_tanh.at(i, k + 1))
                v.scalar_tensor_tensor(slot_h[q], slot_h[q], 1.0, psum[:, q, :], ALU.add, ALU.mult) \
                    .then_inc(slot_h_ready.sem, 1)
                dve.wait_ge(slot_h_ready.sem, slot_h_ready.at(i, k + 1))
                dve.wait_ge(pe_slot_u.sem, pe_slot_u.at(i, k + 1))
                v.scalar_tensor_tensor(slot_g[q], slot_h[q], 0.5, psum[:, 2 + q, :], ALU.mult, ALU.mult) \
                    .then_inc(slot_g_ready.sem, 1)

            def slot_tokens(i, k):
                dve.wait_ge(pe_slot_t.sem, pe_slot_t.at(i, k + 1))
                v.tensor_copy(slot_t[:, k % 2, :, :], psum[:, 5, 0:D].rearrange("p (c n) -> p c n", c=DC)) \
                    .then_inc(slot_t_ready.sem, 1)

            def picked(t):
                for u, s in enumerate(streams):
                    at = bass.ds((t * 2 + u) * NS, NS)
                    step(t, v.tensor_copy(s.sm(608, 2 * NS).rearrange("p (c s) -> p c s", c=2), shares[:, :, at]))
                for u, s in enumerate(streams):
                    dve.wait_ge(gathered[u].sem, gathered[u].at(t, 2 * NS * 16))
                    for c in range(2):
                        for k in range(NS):
                            row, share, end = s.picked[0][:, k, :], s.sm(608 + NS * c + k, 1), k == NS - 1
                            if c == 0:
                                step(t, v.tensor_scalar(row, row, share, None, ALU.mult), wait=end)
                            else:
                                step(t, v.scalar_tensor_tensor(row, s.picked[1][:, k, :], share, row, ALU.mult, ALU.add),
                                     picked_sum if end else None, wait=end)
                    dve.wait_ge(pe_picked_t.sem, pe_picked_t.at(t, 1, u))
                    dve.wait_ge(x2_in[u].sem, x2_in[u].at(t, 16))
                    step(t, v.tensor_tensor(s.x, s.x, s.bank(0, 2), ALU.add), x2_whole)

            def adapter(t):
                for u, s in enumerate(streams):
                    dve.wait_ge(pe_adapt.sem, pe_adapt.at(t, 1, u))
                    row_stats(t, s, s.token_banks(1), adapt_stats)
                for u, s in enumerate(streams):
                    dve.wait_ge(adapt_std.sem, adapt_std.at(t, 1, u))
                    step(t, v.reciprocal(s.sm(4, NS), s.sm(0, NS)))
                    for k in range(NS):
                        step(t, v.tensor_scalar(s.attn_in[:, k, :], s.token_banks(1)[:, k, :], s.stat[:, k, 0:1],
                                                s.sm(4 + k, 1), ALU.subtract, ALU.mult), wait=k == NS - 1)
                    dve.wait_ge(own_in[u].sem, own_in[u].at(t, 8 * BT * 16))
                    for k, op in ((0, ALU.mult), (1, ALU.add)):
                        for b in range(BT):
                            mine = s.attn_in[:, 2 * b:2 * b + 2, :]
                            row = s.adapt_rows[:, k, b, :][:, None, :].broadcast_to([P, 2, D])
                            step(t, v.tensor_tensor(mine, mine, row, op), adapt_ready if (b, k) == (1, 1) else None)

            def to_integers(t, g, rows, dst, at):
                row = g_rows[:, g, :][:, None, :].broadcast_to([P, NS, D])
                done = [None, None]
                for u, s in enumerate(streams):
                    done[u] = step(t, v.tensor_tensor(s.scaled_in, rows(s), row, ALU.mult), wait=False)
                for u, s in enumerate(streams):
                    dve.wait_ge(*done[u])
                    done[u] = step(t, v.tensor_reduce(out=s.sm(212, NS), in_=s.scaled_in, axis=AX.X, op=ALU.max,
                                                     apply_absolute_value=True), wait=False)
                for u, s in enumerate(streams):
                    dve.wait_ge(*done[u])
                    done[u] = step(t, v.tensor_tensor(s.sm(212, NS), s.sm(212, NS), s.sm(208, NS), ALU.mult), wait=False)
                for u, s in enumerate(streams):
                    dve.wait_ge(*done[u])
                    done[u] = step(t, v.tensor_scalar(s.sm(at, NS), s.sm(212, NS), 1e-5, 1.0 / 127, ALU.max, ALU.mult), wait=False)
                for u, s in enumerate(streams):
                    dve.wait_ge(*done[u])
                    done[u] = step(t, v.reciprocal(s.sm(212, NS), s.sm(at, NS)), wait=False)
                for u, s in enumerate(streams):
                    dve.wait_ge(*done[u])
                    done[u] = step(t, v.tensor_tensor(s.sm(212, NS), s.sm(212, NS), s.sm(208, NS), ALU.mult), wait=False)
                for u, s in enumerate(streams):
                    dve.wait_ge(*done[u])
                    done[u] = step(t, v.tensor_tensor(s.scaled_in, s.scaled_in,
                                                     s.sm(212, NS)[:, :, None].broadcast_to([P, NS, D]), ALU.mult), wait=False)
                for u, s in enumerate(streams):
                    dve.wait_ge(*done[u])
                    if g in (1, 2):
                        dve.wait_ge(pe_int_t.sem, pe_int_t.at(t, g, u))
                    step(t, round_to_even(dst(s), s.scaled_in), int_ready)

            def diagonals(t, s, at, last):
                for k in range(NS):
                    end = k == NS - 1
                    step(t, v.tensor_scalar(s.row_diag[:, k, :], w["ident"][:, :], s.sm(at + k, 1), None, ALU.mult),
                         last if end else None, wait=end)

            def attention(t):
                dve.wait_ge(g_rows_in.sem, 16)
                for u, s in enumerate(streams):
                    dve.wait_ge(rms_in.sem, rms_in.at(t, 1, u))
                    step(t, v.reciprocal(s.sm(208, NS), s.sm(204, NS)))
                for g in range(3):
                    to_integers(t, g, lambda s: s.attn_in, lambda s: s.int_rows, 224 + 4 * g)
                    for u, s in enumerate(streams):
                        if g == 0:
                            step(t, v.tensor_scalar(s.sm(216, NS), s.sm(224, NS), qk_scale[:, 0:1], None, ALU.mult))
                            step(t, v.tensor_scalar(s.sm(220, NS), s.sm(216, NS), -1.0, None, ALU.mult))
                        if g == 1:
                            diagonals(t, s, 228, diag_ready)
                        if g == 2:
                            step(t, v.tensor_scalar(s.sm(232, NS), s.sm(232, NS), w_scale[:, 2:3], None, ALU.mult))
                for u, s in enumerate(streams):
                    dve.wait_ge(pe_k.sem, pe_k.at(t, 1, u))
                    dve.wait_ge(scale_ready.sem, scale_ready.at(t, 1, u))
                    dve.wait_ge(out_stored[u].sem, out_stored[u].at(t, 0))
                    step(t, v.tensor_tensor(s.k_t, s.bank(0, 4), s.kscale_b[:, None, :].broadcast_to([P, 4, T]), ALU.mult),
                         k_ready)
                for u, s in enumerate(streams):
                    dve.wait_ge(pe_v.sem, pe_v.at(t, 1, u))
                    for k in range(NS):
                        end = k == NS - 1
                        step(t, v.tensor_scalar(s.v_rows[:, k, :], s.token_banks(2)[:, k, :], s.sm(232 + k, 1), None,
                                                ALU.mult), v_ready if end else None, wait=end)

                def maxima(n, u, s):
                    g = group(n)
                    dve.wait_ge(pe_logits.sem, pe_logits.at(t, n + 1, u))
                    at, per = g.s * NH, len(g.heads)
                    raw = s.sm(448 + at, NH)[:, g.heads[0]:g.heads[-1] + 1:4]
                    step(t, v.tensor_reduce(out=raw, in_=s.bank(n % 2).rearrange("p (j k) -> p j k", j=per),
                                            axis=AX.X, op=ALU.max))
                    step(t, v.tensor_scalar(s.sm(320 + at, NH)[:, g.heads[0]:g.heads[-1] + 1:4], raw,
                                            s.sm(220 + g.s, 1), None, ALU.mult), row_max)

                def probs_t_out(n, u, s):
                    g = group(n)
                    dve.wait_ge(pe_probs_t.sem, pe_probs_t.at(t, n + 1, u))
                    if n >= 2:
                        dve.wait_ge(pe_heads.sem, pe_heads.at(t, n - 1, u))
                    step(t, v.tensor_copy(s.probs_tt[n % 2], s.bank(2)), probs_t)

                def quotients(n, u, s):
                    g = group(n)
                    if g.last:
                        dve.wait_ge(pe_heads_rows.sem, pe_heads_rows.at(t, g.s + 1, u))
                        sums = s.sm(512 + g.s * NH, NH)
                        step(t, v.reciprocal(sums, s.sm(384 + g.s * NH, NH)))
                        for odd in (0, 1):
                            two = s.bank(2).rearrange("p (g x) -> p g x", g=NH // 2)[:, :, odd * 48:odd * 48 + HD]
                            out = s.head_out[:, g.s, :].rearrange("p (g o d) -> p g o d", g=NH // 2, o=2)[:, :, odd, :]
                            share = sums[:, odd:NH:2][:, :, None].broadcast_to([P, NH // 2, HD])
                            step(t, v.tensor_tensor(out, two, share, ALU.mult), heads_ready if odd else None, wait=odd)

                for u, s in enumerate(streams):
                    maxima(0, u, s)
                for n in range(NG):
                    for u, s in enumerate(streams):
                        if n + 1 < NG:
                            maxima(n + 1, u, s)
                        if n >= 2:
                            quotients(n - 2, u, s)
                    for u, s in enumerate(streams):
                        probs_t_out(n, u, s)
                for u, s in enumerate(streams):
                    quotients(NG - 1, u, s)
                for u, s in enumerate(streams):
                    dve.wait_ge(rms_in.sem, rms_in.at(t, 2, u))
                    step(t, v.reciprocal(s.sm(208, NS), s.sm(204, NS)))
                to_integers(t, 3, lambda s: s.head_out, lambda s: s.y_rows, 236)
                for u, s in enumerate(streams):
                    step(t, v.tensor_scalar(s.sm(236, NS), s.sm(236, NS), w_scale[:, 3:4], None, ALU.mult))
                    diagonals(t, s, 236, diag_ready)
                for u, s in enumerate(streams):
                    dve.wait_ge(scale_ready.sem, scale_ready.at(t, 2, u))
                    dve.wait_ge(pe_o.sem, pe_o.at(t, 1, u))
                    step(t, v.tensor_tensor(s.f8_a[:, 0, :], s.bank(3), s.yscale_b, ALU.mult), wait=False)
                    step(t, v.tensor_tensor(s.f8_a[:, 1, :], s.bank(0), s.yscale_b, ALU.mult))
                    step(t, v.tensor_tensor(s.x, s.x, s.f8_a, ALU.add), x3_ready)

            def last_ffn(t):
                for u, s in enumerate(streams):
                    dve.wait_ge(pe_cat.sem, pe_cat.at(t, 1, u))
                    for c in range(DC):
                        for b in range(BT):
                            tokens = slice(b * S, (b + 1) * S)
                            step(t, v.tensor_scalar(s.f8_a[:, c, tokens], s.bank(1 + c)[:, tokens], s.cat_b[:, b, c:c + 1],
                                                    None, ALU.add), wait=(c, b) == (DC - 1, BT - 1))
                    given = []

                    def run(ins):
                        given.append(ins)
                        step(t, ins, f8_ready if len(given) == 5 else None)

                    float8_values(run, *(z.rearrange("p c n -> p (c n)") for z in (s.f8_a, s.f8_b, s.f8_q)))
                for u, s in enumerate(streams):
                    dve.wait_ge(half_ready.sem, half_ready.at(t, 1, u))
                    for c in range(DC):
                        end = c == DC - 1
                        step(t, v.scalar_tensor_tensor(s.out_t[:, c, :], s.half_t[:, c, :], col("fbias", c), s.x[:, c, :],
                                                       ALU.add, ALU.add), out_ready if end else None, wait=end)

            with dve.Fori(0, PAIRS) as t:
                condition(t)
                scan_attention(t)
                pool_prompt(t)
                route(t)
            order()
            with dve.Fori(0, PAIRS) as t:
                shared_expert(t)
            slot_tokens(0, 0)
            slot_gate(0, 0)
            slot_tokens(0, 1)
            with dve.Fori(0, SLOT_PAIRS - 1) as i:
                for k in (1, 2):
                    slot_gate(i, k)
                    slot_tokens(i, k + 1)
            slot_gate(SLOT_PAIRS - 1, 1)
            chain = dve_chain_3
            with dve.Fori(0, PAIRS) as t:
                picked(t)
                adapter(t)
                attention(t)
                last_ffn(t)

        @block.tensor
        def _(pe):
            mm = nc.tensor.matmul

            def add_up(dst, pairs):
                for k, (lhs, rhs) in enumerate(pairs):
                    ins = mm(dst, lhs, rhs, start=k == 0, stop=k == len(pairs) - 1)
                return ins

            dve_sums = setup_dve
            pe.wait_ge(dve_sums.sem, DVE_SUMS)
            pe.wait_ge(loads["early"].sem, 16 * N_EARLY)
            mm(psum[:, 0, 0:4], w["ones"][:, 0:1].broadcast_to([P, P]), sm(44, 4), start=True, stop=True).then_inc(setup_pe.sem, 1)
            pe.wait_ge(setup_dve.sem, DVE_SUMS + 1)

            def condition(t):
                for u, s in enumerate(streams):
                    pe.wait_ge(x_in[u].sem, x_in[u].at(t, 16))
                    pe.wait_ge(picks_ready.sem, picks_ready.at(t, 0, u))
                    pe.wait_ge(pool_rows_ready.sem, pool_rows_ready.at(t, 0, u))
                    add_up(s.bank(0, p=HID), [(w["w_n1"][:, c, :], s.x[:, c, :]) for c in range(DC)])
                    for e in range(DC):
                        ins = add_up(s.bank(1 + e), [(w["w_soma"][:, c, e * P:(e + 1) * P], s.x[:, c, :]) for c in range(DC)])
                    ins.then_inc(pe_soma.sem, 1)
                for u, s in enumerate(streams):
                    pe.wait_ge(ctx_ready.sem, ctx_ready.at(t, 1, u))
                    pe.wait_ge(h1_ready.sem, h1_ready.at(t, 1, u))
                    for e, bank in ((0, 3), (1, 0)):
                        cols = slice(e * P, (e + 1) * P)
                        if e == 1:
                            pe.wait_ge(soma_ready.sem, soma_ready.at(t, 1, u))
                        ins = add_up(s.bank(bank), [(w["w_g"][:, c, cols], s.x[:, c, :]) for c in range(DC)]
                                     + [(w["w_g"][:, DC + c, cols], s.ctx_t[:, c, :]) for c in range(DC)])
                    ins.then_inc(pe_gate.sem, 1)
                    mm(s.bank(1, p=ND), w["w_n2"][:, :], s.h1, start=True, stop=True).then_inc(pe_mod.sem, 1)

                def mod_rows(s, d):
                    mm(s.bank(2 + d % 2), w["ident"][0:ND, d:d + 1].broadcast_to([ND, P]), s.mod,
                       start=True, stop=True).then_inc(pe_mod_rows.sem, 1)

                for u, s in enumerate(streams):
                    pe.wait_ge(mod_ready.sem, mod_ready.at(t, 1, u))
                    mod_rows(s, 0)
                for s in streams:
                    mod_rows(s, 1)
                for d in range(ND):
                    for u, s in enumerate(streams):
                        pe.wait_ge(trace_ready.sem, trace_ready.at(t, d + 1, u))
                        for c in range(DC):
                            ins = mm(s.bank(c), w["ident"][:, :], s.trace[d % 2][:, c, :], start=d == 0, stop=d == ND - 1,
                                     skip_group_check=True)
                        ins.then_inc(pe_trace_used.sem, 1)
                        if d + 2 < ND:
                            mod_rows(s, d + 2)
                for u, s in enumerate(streams):
                    pe.wait_ge(temporal_ready.sem, temporal_ready.at(t, 1, u))
                    for e in range(DC):
                        ins = add_up(s.bank(2 + e),
                                     [(w["w_temp"][:, c, e * P:(e + 1) * P], s.temporal[:, c, :]) for c in range(DC)])
                    ins.then_inc(pe_temp.sem, 1)
                for u, s in enumerate(streams):
                    pe.wait_ge(mixed_ready.sem, mixed_ready.at(t, 1, u))
                    for k in range(NS):
                        ins = add_up(s.token_banks(0)[:, k, :],
                                     [(s.gate_t[:, c, k * P:(k + 1) * P], w["w_out"][:, c, :]) for c in range(DC)])
                    ins.then_inc(pe_cond.sem, 1)
                for u, s in enumerate(streams):
                    pe.wait_ge(cond_norm.sem, cond_norm.at(t, 1, u))
                    for c in range(DC):
                        for k in range(NS):
                            ins = nc.tensor.transpose(s.bank(2 + c)[:, k * P:(k + 1) * P],
                                                      s.cond_rows[:, k, c * P:(c + 1) * P], w["ident"][:, :])
                    ins.then_inc(pe_cond_t.sem, 1)

            def scan_attention(t):
                def z_part(s, bank, at, width, done):
                    add_up(s.bank(bank, p=width), [(w["w_in"][:, c, at:at + width], s.cond[:, c, :]) for c in range(DC)]) \
                        .then_inc(done.sem, 1)

                def head_rows(s, bank, c, src):
                    return mm(s.bank(bank), w["head_sel"][:, c, :], src, start=True, stop=True)

                for u, s in enumerate(streams):
                    pe.wait_ge(cond_ready.sem, cond_ready.at(t, 1, u))
                    z_part(s, 2, 2 * INNER, HEADS_B, pe_s)
                    z_part(s, 0, 0, P, pe_val)
                    z_part(s, 1, INNER, P, pe_zg)
                for c in range(IC):
                    for u, s in enumerate(streams):
                        if c == 0:
                            pe.wait_ge(p_ready.sem, p_ready.at(t, 1, u))
                        pe.wait_ge(val_copied.sem, val_copied.at(t, c + 1, u))
                        head_rows(s, 2, c, s.p_t)
                        if c:
                            pe.wait_ge(yg_ready.sem, yg_ready.at(t, c, u))
                        head_rows(s, 0, c, s.inv_den).then_inc(pe_p_rows.sem, 1)
                    if c + 1 < IC:
                        for u, s in enumerate(streams):
                            pe.wait_ge(zg_copied.sem, zg_copied.at(t, c + 1, u))
                            z_part(s, 1, INNER + (c + 1) * P, P, pe_zg)
                        for u, s in enumerate(streams):
                            pe.wait_ge(product_ready.sem, product_ready.at(t, c + 1, u))
                            z_part(s, 2, (c + 1) * P, P, pe_val)
                    for u, s in enumerate(streams):
                        pe.wait_ge(mean_ready.sem, mean_ready.at(t, c + 1, u))
                        add_up(s.bank(0), [(w["w_re"][:, :], s.mean_re), (w["w_im"][:, :], s.mean_im)]) \
                            .then_inc(pe_y.sem, 1)
                    for u, s in enumerate(streams):
                        pe.wait_ge(sq_ready.sem, sq_ready.at(t, c + 1, u))
                        for k, part in enumerate((s.cos_t, s.sin_t)):
                            ins = mm(s.bank(3, p=HEADS_B), w["head_sum"][:, c, :], part, start=c == 0 and k == 0,
                                     stop=c == IC - 1 and k == 1, skip_group_check=True)
                        ins.then_inc(pe_sq.sem, 1)
                for u, s in enumerate(streams):
                    pe.wait_ge(rms_ready.sem, rms_ready.at(t, 1, u))
                    for c in range(IC):
                        ins = head_rows(s, c, c, s.rms_b)
                    ins.then_inc(pe_rms_rows.sem, 1)
                for u, s in enumerate(streams):
                    pe.wait_ge(ynorm_ready.sem, ynorm_ready.at(t, 1, u))
                    for e in range(DC):
                        ins = add_up(s.bank(e), [(w["w_proj"][:, c, e * P:(e + 1) * P], s.yg[:, c, :]) for c in range(IC)])
                    ins.then_inc(pe_proj.sem, 1)

            def pool_prompt(t):
                for u, s in enumerate(streams):
                    pe.wait_ge(x1_ready.sem, x1_ready.at(t, 1, u))
                    for k in range(NS):
                        for c in range(DC):
                            ins = nc.tensor.transpose(s.token_banks(2)[:, k, c * P:(c + 1) * P],
                                                      s.x[:, c, k * P:(k + 1) * P], w["ident"][:, :])
                    ins.then_inc(pe_x1_rows.sem, 1)
                    add_up(s.bank(0, p=HID), [(w["w_1"][:, c, :], s.x[:, c, :]) for c in range(DC)]) \
                        .then_inc(pe_score_hid.sem, 1)
                for u, s in enumerate(streams):
                    pe.wait_ge(score_hid.sem, score_hid.at(t, 1, u))
                    mm(s.bank(1), w["v_col"][:, 0:1].broadcast_to([HID, P]), s.score_h, start=True, stop=True) \
                        .then_inc(pe_score.sem, 1)
                for u, s in enumerate(streams):
                    pe.wait_ge(pool_p.sem, pool_p.at(t, 1, u))
                    for b in range(BT):
                        for l in range(2):
                            for j in range(2):
                                at = l * S + j * P
                                ins = nc.tensor.transpose(s.bank(2 + b)[:, at:at + P],
                                                          s.pool_w[:, 2 * b + j, l * P:(l + 1) * P], w["ident"][:, :])
                    ins.then_inc(pe_pool_t.sem, 1)
                for u, s in enumerate(streams):
                    pe.wait_ge(pool_t.sem, pool_t.at(t, 1, u))
                    for c in range(DC):
                        for b in range(BT):
                            ins = add_up(s.bank(c)[:, b * S:(b + 1) * S],
                                         [(s.x1_rows[:, 2 * b + l, c * P:(c + 1) * P], s.pool_wt[:, b, l * S:(l + 1) * S])
                                          for l in range(2)])
                    ins.then_inc(pe_pool.sem, 1)
                for u, s in enumerate(streams):
                    pe.wait_ge(pool_ready.sem, pool_ready.at(t, 1, u))
                    for k in range(NS):
                        ins = add_up(s.bank(0)[:, k * NE:(k + 1) * NE],
                                     [(s.pooled[:, c, k * P:(k + 1) * P], w["w_route"][:, c, :]) for c in range(DC)])
                    ins.then_inc(pe_route.sem, 1)
                for u, s in enumerate(streams):
                    for k in range(NS):
                        b, at = k // 2, (k % 2) * P
                        ins = add_up(s.token_banks(2)[:, k, :],
                                     [(s.pool_wt[:, b, l * S + at:l * S + at + P], s.x1_rows[:, 2 * b + l, :])
                                      for l in range(2)])
                    ins.then_inc(pe_pool_rows.sem, 1)

            def order():
                both = streams[0].sm(0, NE * BLOCKS)
                pe.wait_ge(order_in.sem, 32)
                pe.wait_ge(sort_dve.sem, 1)
                for bank, what in ((0, earlier), (1, w["ones"][:, 0:1].broadcast_to([P, P]))):
                    mm(psum[:, bank, 0:NE * BLOCKS], what, both, start=True, stop=True).then_inc(sort_pe.sem, 1)

            def shared_expert(t):
                for u in (0, 1):
                    x = pooled_in[u]
                    pe.wait_ge(ffn_in[u].sem, ffn_in[u].at(t, 32))
                    for m in range(FC):
                        n = u * FC + m
                        if n >= 2:
                            pe.wait_ge(h_read.sem, h_read.at(t, n - 1))
                        add_up(psum[:, 3 + n % 2, :], [(up_weight(0, c, m), x[:, c, :]) for c in range(DC)])
                        if n >= 2:
                            pe.wait_ge(g_ready.sem, g_ready.at(t, n - 1))
                        add_up(psum[:, 5 + n % 2, :], [(up_weight(1, c, m), x[:, c, :]) for c in range(DC)]) \
                            .then_inc(pe_up.sem, 1)
                    pe.wait_ge(x2_ready.sem, x2_ready.at(t, u))
                    for m in range(FC):
                        pe.wait_ge(g_ready.sem, g_ready.at(t, u * FC + m + 1))
                        for c, bank in ((0, 0), (1, 7)):
                            ins = mm(psum[:, bank, :], down_weight(m, c), g_buf[:, m, :], start=m == 0, stop=m == FC - 1,
                                     skip_group_check=True)
                    ins.then_inc(pe_down.sem, 1)

            def slot_turn(i, k):
                pe.wait_ge(slot_rows_in[k % 2].sem, slot_rows_in[k % 2].at(i, 16 * (k // 2 + 1)))
                for c in range(DC):
                    ins = nc.tensor.transpose(psum[:, 5, c * P:(c + 1) * P], slot_rows[:, k % 2, c * P:(c + 1) * P],
                                              w["ident"][:, :])
                ins.then_inc(pe_slot_t.sem, 1)

            def slot_up(i, k, which, done):
                expert = pe.value_load(slot_expert[0:1, bass.ds(i * 2 + k, 1)])
                if which == 0:
                    pe.wait_ge(slot_t_ready.sem, slot_t_ready.at(i, k + 1))
                add_up(psum[:, 2 * which + k % 2, :],
                       [(slot_t[:, k % 2, c, :], routed_weight(expert, (which * DC + c) * FF, FF)) for c in range(DC)]) \
                    .then_inc(done.sem, 1)

            def slot_turn_g(i, k):
                pe.wait_ge(slot_g_ready.sem, slot_g_ready.at(i, k + 1))
                for m in range(FC):
                    ins = nc.tensor.transpose(psum[:, 4, m * P:(m + 1) * P], slot_g[k % 2][:, m * P:(m + 1) * P],
                                              w["ident"][:, :])
                ins.then_inc(pe_slot_g_t.sem, 1)

            def slot_down(i, k):
                expert = pe.value_load(slot_expert[0:1, bass.ds(i * 2 + k, 1)])
                pe.wait_ge(slot_out_ready.sem, slot_out_ready.at(i, k))
                pe.wait_ge(slot_g_t_ready.sem, slot_g_t_ready.at(i, k + 1))
                add_up(psum[:, 6, 0:D],
                       [(slot_g_t[k % 2][:, m, :], routed_weight(expert, 2 * DC * FF + m * D, D)) for m in range(FC)]) \
                    .then_inc(pe_slot_out.sem, 1)

            def slot_step(i, k, last=False):
                slot_up(i, k, 0, pe_slot_h)
                slot_turn_g(i, k - 1)
                slot_up(i, k, 1, pe_slot_u)
                if not last:
                    slot_turn(i, k + 1)
                slot_down(i, k - 1)

            def picked(t):
                for u, s in enumerate(streams):
                    pe.wait_ge(out_ready.sem, out_ready.at(t, 0, u))
                    pe.wait_ge(picked_sum.sem, picked_sum.at(t, 1, u))
                    for c in range(DC):
                        for k in range(NS):
                            ins = nc.tensor.transpose(s.bank(c)[:, k * P:(k + 1) * P],
                                                      s.picked[0][:, k, c * P:(c + 1) * P], w["ident"][:, :])
                    ins.then_inc(pe_picked_t.sem, 1)

            def adapter(t):
                for u, s in enumerate(streams):
                    pe.wait_ge(x2_whole.sem, x2_whole.at(t, 1, u))
                    pe.wait_ge(own_in[u].sem, own_in[u].at(t, 8 * BT * 16))
                    for b in range(BT):
                        tokens = slice(b * S, (b + 1) * S)
                        ins = add_up(s.bank(0)[:, tokens], [(s.adapt_down[:, b, c, :], s.x[:, c, tokens]) for c in range(DC)])
                    ins.then_inc(pe_bottle.sem, 1)
                for u, s in enumerate(streams):
                    pe.wait_ge(bottle_ready.sem, bottle_ready.at(t, 1, u))
                    for k in range(NS):
                        tokens = slice(k * P, (k + 1) * P)
                        dst = s.token_banks(1)[:, k, :]
                        for c in range(DC):
                            mm(dst[:, c * P:(c + 1) * P], s.x[:, c, tokens], w["ident"][:, :], start=c == 0, stop=False,
                               skip_group_check=True)
                        mm(dst, w["ones"][0:1, 0:1].broadcast_to([1, P]), s.adapt_bu[:, k // 2, :], start=False, stop=False,
                           skip_group_check=True)
                        ins = mm(dst, s.bottle[:, tokens], s.adapt_up[:, k // 2, :], start=False, stop=True,
                                 skip_group_check=True)
                    ins.then_inc(pe_adapt.sem, 1)

            def integers_t(s, rows):
                for c in range(DC):
                    for k in range(NS):
                        ins = nc.tensor.transpose(s.bank_b(c, 1)[:, 0, k * P:(k + 1) * P], rows[:, k, c * P:(c + 1) * P],
                                                  ident_b[:, :])
                return ins

            def attention(t):
                for g in range(3):
                    for u, s in enumerate(streams):
                        pe.wait_ge(int_ready.sem, int_ready.at(t, g + 1, u))
                        if g == 1:
                            pe.wait_ge(q_ready.sem, q_ready.at(t, 1, u))
                        if g == 2:
                            pe.wait_ge(k_ready.sem, k_ready.at(t, 1, u))
                        integers_t(s, s.int_rows).then_inc(pe_int_t.sem, 1)
                        if g == 1:
                            pe.wait_ge(diag_ready.sem, diag_ready.at(t, 1, u))
                            mm(s.bank(2), w["ones"][:, 0:1].broadcast_to([P, P]), s.row_diag.rearrange("p s q -> p (s q)"),
                               start=True, stop=True).then_inc(pe_scale.sem, 1)
                    for u, s in enumerate(streams):
                        pe.wait_ge(int_t.sem, int_t.at(t, g + 1, u))
                        if g == 1:
                            pe.wait_ge(scale_ready.sem, scale_ready.at(t, 1, u))
                        if g < 2:
                            for k in range(4):
                                ins = add_up(s.bank(k), [(tern_qk[:, g, c, k * P:(k + 1) * P], s.int_tt[:, c, :])
                                                         for c in range(DC)])
                            ins.then_inc((pe_q, pe_k)[g].sem, 1)
                        else:
                            for k in range(NS):
                                ins = add_up(s.token_banks(2)[:, k, :],
                                             [(s.int_tt[:, c, k * P:(k + 1) * P], tern_vo[:, 0, c, :]) for c in range(DC)])
                            ins.then_inc(pe_v.sem, 1)

                def logits(n, u, s):
                    g = group(n)
                    if n == 0:
                        pe.wait_ge(v_ready.sem, v_ready.at(t, 1, u))
                    if n >= 2:
                        pe.wait_ge(probs_ready.sem, probs_ready.at(t, n - 1, u))
                    bank = s.bank(n % 2)
                    per = len(g.heads)
                    mm(bank.rearrange("p (j k) -> p j k", j=per)[:, :, g.width - P:], ident_b[:, :],
                       causal_a[:, 0:per * P].rearrange("p (j k) -> p j k", j=per), start=True, stop=False,
                       skip_group_check=True)
                    for j, head in enumerate(g.heads):
                        lanes = slice(32 * (head % 4), 32 * (head % 4) + 32)
                        ins = mm(bank[:, j * g.width:(j + 1) * g.width], s.q_t[lanes, head // 4, g.s * P:(g.s + 1) * P],
                                 s.k_t[lanes, head // 4, g.b * S:g.b * S + g.width], start=False, stop=j == per - 1,
                                 skip_group_check=True)
                    ins.then_inc(pe_logits.sem, 1)

                def transposed(n, u, s):
                    pe.wait_ge(probs_ready.sem, probs_ready.at(t, n + 1, u))
                    if n:
                        pe.wait_ge(probs_t.sem, probs_t.at(t, n, u))
                    if n >= 2 and group(n - 2).last:
                        pe.wait_ge(heads_ready.sem, heads_ready.at(t, group(n - 2).s + 1, u))
                    for k in range(4):
                        ins = nc.tensor.transpose(s.bank(2)[:, k * P:(k + 1) * P], s.probs[n % 2][:, k * P:(k + 1) * P],
                                                  w["ident"][:, :])
                    ins.then_inc(pe_probs_t.sem, 1)

                def weighted(n, u, s):
                    g = group(n)
                    pe.wait_ge(probs_t.sem, probs_t.at(t, n + 1, u))
                    if g.first and g.s:
                        pe.wait_ge(heads_t_ready.sem, heads_t_ready.at(t, g.s, u))
                    for j, head in enumerate(g.heads):
                        for kc in range(g.width // P):
                            at = j * g.width + kc * P
                            lanes = slice(32 * (head % 4), 32 * (head % 4) + 32)
                            ins = mm(s.bank(3)[lanes, (head // 4) * P:(head // 4 + 1) * P],
                                     s.v_rows[:, 2 * g.b + kc, (head // 2) * 2 * HD:(head // 2 + 1) * 2 * HD],
                                     s.probs_tt[n % 2][:, at:at + P], start=kc == 0, stop=kc == g.width // P - 1)
                    ins.then_inc(pe_heads.sem, 1)

                def heads_rows(n, u, s):
                    g = group(n)
                    if g.last:
                        pe.wait_ge(heads_t_ready.sem, heads_t_ready.at(t, g.s + 1, u))
                        pe.wait_ge(probs_t.sem, probs_t.at(t, min(n + 2, NG), u))
                        for k in range(4):
                            ins = nc.tensor.transpose(s.bank(2)[:, k * P:(k + 1) * P], s.heads_t[:, k * P:(k + 1) * P],
                                                      w["ident"][:, :])
                        ins.then_inc(pe_heads_rows.sem, 1)

                for u, s in enumerate(streams):
                    logits(0, u, s)
                for n in range(NG):
                    for u, s in enumerate(streams):
                        if n + 1 < NG:
                            logits(n + 1, u, s)
                        if n >= 2:
                            heads_rows(n - 2, u, s)
                        if n:
                            weighted(n - 1, u, s)
                    for u, s in enumerate(streams):
                        transposed(n, u, s)
                for u, s in enumerate(streams):
                    weighted(NG - 1, u, s)
                for u, s in enumerate(streams):
                    heads_rows(NG - 1, u, s)
                for u, s in enumerate(streams):
                    pe.wait_ge(int_ready.sem, int_ready.at(t, 4, u))
                    integers_t(s, s.y_rows).then_inc(pe_int_t.sem, 1)
                    pe.wait_ge(diag_ready.sem, diag_ready.at(t, 2, u))
                    mm(s.bank(2), w["ones"][:, 0:1].broadcast_to([P, P]), s.row_diag.rearrange("p s q -> p (s q)"),
                       start=True, stop=True).then_inc(pe_scale.sem, 1)
                for u, s in enumerate(streams):
                    pe.wait_ge(int_t.sem, int_t.at(t, 4, u))
                    for e, bank in ((0, 3), (1, 0)):
                        ins = add_up(s.bank(bank), [(tern_vo[:, 1, c, e * P:(e + 1) * P], s.y_tt[:, c, :]) for c in range(DC)])
                    ins.then_inc(pe_o.sem, 1)

            def last_ffn(t):
                for u, s in enumerate(streams):
                    pe.wait_ge(x3_ready.sem, x3_ready.at(t, 1, u))
                    for e in range(DC):
                        for b in range(BT):
                            tokens = slice(b * S, (b + 1) * S)
                            ins = add_up(s.bank(1 + e)[:, tokens],
                                         [(s.cat_w[:, b, c, e * P:(e + 1) * P], s.x[:, c, tokens]) for c in range(DC)])
                    ins.then_inc(pe_cat.sem, 1)
                for u, s in enumerate(streams):
                    pe.wait_ge(f8_ready.sem, f8_ready.at(t, 1, u))
                    for e in range(DC):
                        ins = add_up(s.bank(2 + e), [(f8_w[:, c, e * P:(e + 1) * P], s.f8_q[:, c, :]) for c in range(DC)])
                    ins.then_inc(pe_f8.sem, 1)

            with pe.Fori(0, PAIRS) as t:
                condition(t)
                scan_attention(t)
                pool_prompt(t)
            order()
            pe.wait_ge(expert_in.sem, 5 * 16)
            with pe.Fori(0, PAIRS) as t:
                shared_expert(t)
            pe.wait_ge(late_expert_in.sem, (EXPERTS - 5) * 16)
            pe.wait_ge(sort_dve.sem, ORDER_STEPS)
            pe.wait_ge(x2_ready.sem, x2_ready.at(PAIRS, 0))
            slot_turn(0, 0)
            slot_up(0, 0, 0, pe_slot_h)
            slot_up(0, 0, 1, pe_slot_u)
            slot_turn(0, 1)
            with pe.Fori(0, SLOT_PAIRS - 1) as i:
                for k in (1, 2):
                    slot_step(i, k)
            slot_step(SLOT_PAIRS - 1, 1, last=True)
            slot_turn_g(SLOT_PAIRS - 1, 1)
            slot_down(SLOT_PAIRS - 1, 1)
            with pe.Fori(0, PAIRS) as t:
                picked(t)
                adapter(t)
                attention(t)
                last_ffn(t)

        for name, s in signals:
            per = period(s)
            assert not s.given or not per or per == s.given, (name, per, s.given)


def setup_arrays(inputs):
    f = {n: np.asarray(a) for n, a in inputs.items()}

    def rows(a, k):
        return a.reshape(k, P, -1).transpose(1, 0, 2)

    def lhs(a, k):
        return rows(a.T, k)

    vecs = np.zeros((P, NVEC), np.float32)

    def put(name, a):
        at, n = VEC[name]
        a = np.asarray(a)
        vecs[:a.shape[0], at:at + n] = a.reshape(a.shape[0], n)

    def chunk_cols(a, k):
        return a.reshape(k, P).T

    put("tau", np.broadcast_to(np.concatenate([f["L0_cond_tau_ctx"].reshape(1), f["condB_tauraws"]]), (P, 1 + ND)))
    put("deriv", np.broadcast_to(f["L0_attn_deriv_logits"], (P, 3)))
    for name, key in (("bg", "bg"), ("btemp", "btemp"), ("bsoma", "bsoma"), ("gamma", "gamma"), ("beta", "beta")):
        put(name, chunk_cols(f["L0_cond_" + key], DC))
    put("bn1", f["L0_cond_bn1"].reshape(HID, 1))
    put("bn2", f["condB_bn2"].reshape(ND, 1))
    put("blend", f["cond_1024"].reshape(ND, DC, P).transpose(2, 1, 0))
    taps = np.zeros((TAPS, 9 * P), np.float32)
    taps[:, :C_IN] = f["L0_attn_conv_k"][:, 0, :]
    put("conv_k", taps.reshape(TAPS, 9, P).transpose(2, 1, 0))
    cb = np.zeros(9 * P, np.float32)
    cb[:C_IN] = f["L0_attn_conv_b"]
    put("conv_b", chunk_cols(cb, 9))
    put("theta", chunk_cols(f["L0_attn_theta"].reshape(-1), IC))
    put("slope", np.concatenate([f["L0_attn_decay_slopes"], f["L0_attn_anchor_slopes"]]).reshape(-1, 1))
    put("score_scale", f["L0_attn_score_scale"].reshape(-1, 1))
    put("norm_re", np.tile(f["L0_attn_norm_scale"][:HD_B], P // HD_B).reshape(-1, 1))
    put("norm_im", np.tile(f["L0_attn_norm_scale"][HD_B:], P // HD_B).reshape(-1, 1))
    put("b1", f["L0_cond2_b1"].reshape(-1, 1))
    put("fbias", chunk_cols(f["L1_ffn_bias"], DC))
    for name, value in (("eps5", 1e-5), ("eps6", 1e-6), ("half_pi", np.pi / 2), ("zero", 0.0)):
        put(name, np.full((P, 1), value, np.float32))

    def block_diagonal(a):
        out = np.zeros((P, P), np.float32)
        for k in range(P // HD_B):
            out[k * HD_B:(k + 1) * HD_B, k * HD_B:(k + 1) * HD_B] = a
        return out

    x = f["x"].reshape(TILES, T, DC, P).transpose(0, 3, 2, 1)
    a = {
        "x_t": x, "vecs": vecs,
        "w_g": lhs(f["L0_cond_Wg"], 2 * DC), "w_n1": lhs(f["L0_cond_Wn1"], DC), "w_n2": f["cond_256"].T,
        "w_soma": lhs(f["L0_cond_Wsoma"], DC), "w_temp": lhs(f["L0_cond_Wtemp"], DC),
        "w_out": lhs(f["L0_cond_Wout"], DC), "w_in": rows(f["L0_attn_in_proj_w"], DC),
        "w_re": block_diagonal(f["L0_attn_W_re"]), "w_im": block_diagonal(f["L0_attn_W_im"]),
        "w_proj": rows(f["L0_attn_out_proj_w"], IC), "w_1": rows(f["L0_cond2_W1"], DC),
        "v_col": f["L0_cond2_v"].reshape(HID, 1),
        "w_route": rows(f["L0_ffn_gate_w"], DC),
        "qkvo": np.stack([lhs(f["L1_attn_" + n], DC) for n in ("wq", "wk", "wv", "wo")], 1),
        "w_f8": lhs(f["L1_ffn_weight"], DC),
        "g_rows": np.broadcast_to(np.stack([f["L1_attn_" + n] for n in ("gq", "gk", "gv", "go")]), (P, 4, D)),
        "ids_row": np.concatenate([f["itok_B_0_6"], f["itok_B_0_63"]]).reshape(1, 2 * B),
        "kind_ids": np.broadcast_to(f["itok_B_0_2"], (P, B)),
        "down_w": f["L1_cond_down_w"].reshape(8, DC, P, P).transpose(0, 2, 1, 3),
        "down_b": f["L1_cond_down_b"].reshape(8, P, 1),
        "up_w": f["L1_cond_up_w"], "up_b": f["L1_cond_up_b"].reshape(8, 1, D),
        "ln_g": f["L1_cond_ln_g"].reshape(8, 1, D), "ln_b": f["L1_cond_ln_b"].reshape(8, 1, D),
        "cat_w": f["L1_cond2_W"].reshape(64, DC, P, D).transpose(0, 2, 1, 3),
        "cat_b": f["L1_cond2_b"].reshape(64, DC, P).transpose(0, 2, 1),
    }
    up = np.stack([np.concatenate([f["L0_ffn_sw1"][None], f["L0_ffn_ew1"]]),
                   np.concatenate([f["L0_ffn_sw2"][None], f["L0_ffn_ew2"]])], 1)
    up = up.reshape(EXPERTS, 2, DC, P, FF).transpose(0, 3, 1, 2, 4).reshape(EXPERTS, P, -1)
    down = np.concatenate([f["L0_ffn_sw3"][None], f["L0_ffn_ew3"]])
    down = down.reshape(EXPERTS, FC, P, D).transpose(0, 2, 1, 3).reshape(EXPERTS, P, -1)
    a["expert_w"] = np.concatenate([up, down], 2)

    a["ident"] = np.eye(P, dtype=np.float32)
    a["ones"] = np.ones((P, 1), np.float32)
    head = np.arange(INNER) // HD_B
    sel = (np.arange(HEADS_B)[:, None] == head[None, :]).astype(np.float32)
    a["head_sel"] = sel.reshape(HEADS_B, IC, P)
    a["head_sum"] = sel.T.reshape(IC, P, HEADS_B).transpose(1, 0, 2) / np.float32(2 * HD_B)
    j, l = np.arange(S)[:, None], np.arange(S)[None, :]
    mask = np.stack([np.where(m, 0.0, NEG) for m in (l <= j, l >= j, l != j)]).astype(np.float32)
    a["pool_mask"] = mask.reshape(3, 2, P, S).transpose(2, 0, 1, 3)
    count = np.stack([np.arange(S) + 1, S - np.arange(S), np.full(S, S - 1)]).astype(np.float32)
    a["pool_count"] = count.reshape(3, 2, P).transpose(2, 0, 1)
    pos = np.arange(S, dtype=np.float32)
    a["dist"] = np.where(np.arange(HEADS_B)[:, None] < HEADS_B - 4, S - 1 - pos, pos).astype(np.float32)
    q, k = np.arange(P)[:, None], np.arange(P)[None, :]
    a["causal"] = np.where(k <= q, 0.0, NEG).astype(np.float32)
    a["earlier"] = (q < k).astype(np.float32)
    a["slot_block"] = np.broadcast_to(np.arange(SLOTS, dtype=np.float32)[:, None], (SLOTS, NE - 1))[None]
    a["expert_no"] = np.broadcast_to(np.arange(NE, dtype=np.float32), (P, NS, NE))
    return {n: np.ascontiguousarray(v) for n, v in a.items()}


def kernel(**inputs):
    import concourse.bacc as bacc
    from concourse.bass_utils import run_bass_kernel_spmd

    nc = bacc.Bacc("TRN2", target_bir_lowering=False, num_devices=1)
    arrays = setup_arrays(inputs)
    dram = {n: nc.dram_tensor("in_" + n, a.shape, mybir.dt.from_np(a.dtype), kind="ExternalInput").ap()
            for n, a in arrays.items()}
    out = nc.dram_tensor("out_t", (TILES, P, DC, T), F32, kind="ExternalOutput").ap()
    adaln_attention_ffn(nc, dram, out)
    r = run_bass_kernel_spmd(nc, [{"in_" + n: a for n, a in arrays.items()}], core_ids=[0])
    y = np.asarray(r.results[0]["out_t"])
    return y.transpose(0, 3, 2, 1).reshape(B, S, D)
```
